# Optimizing a Trainium2 kernel written in Bass

```python
import numpy as np
import jax
import jax.numpy as jnp

def _softmax(x, axis=-1):
    return jax.nn.softmax(x, axis=axis)

def _gelu(x):
    return jax.nn.gelu(x, approximate=True)

def _silu(x):
    return jax.nn.silu(x)

def _sigmoid(x):
    return jax.nn.sigmoid(x)

def _layernorm(x, axis=-1, eps=1e-05):
    m = jnp.mean(x, axis=axis, keepdims=True)
    v = jnp.var(x, axis=axis, keepdims=True)
    return (x - m) / jnp.sqrt(v + eps)

def _scatter_add(tgt, idx, src, axis=0):
    return tgt.at[idx].add(src)

def _segment_sum(src, seg, n):
    return jax.ops.segment_sum(src, seg, n)
kernel_name = 'mk_recurrent_d1_jaxref_r4_a3bbb2'

def setup_inputs(seed: int=0):
    np.random.seed(seed)
    _w = jnp.asarray

    def _L0_attn_setup():
        import jax, jax.numpy as jnp
        import numpy as np
        from jax import lax
        B, L, D = (2, 512, 512)
        H, DK, DV, K = (16, 128, 128, 4)
        Q_DIM = H * DK
        V_DIM = H * DV

        def silu(x):
            return x * jax.nn.sigmoid(x)

        def causal_dwconv(x, w, b):
            Kk = w.shape[1]
            xp = jnp.pad(x, ((0, 0), (Kk - 1, 0), (0, 0)))
            kern = w.T[:, None, :]
            y = lax.conv_general_dilated(xp, kern, window_strides=(1,), padding='VALID', dimension_numbers=('NWC', 'WIO', 'NWC'), feature_group_count=w.shape[0])
            return y + b

        def layernorm(x, w, b, eps=1e-05):
            m = jnp.mean(x, axis=-1, keepdims=True)
            var = jnp.mean((x - m) ** 2, axis=-1, keepdims=True)
            return (x - m) * lax.rsqrt(var + eps) * w + b
        key = jax.random.key(seed)
        ks = jax.random.split(key, 16)
        s = 0.02
        f32 = jnp.float32
        return {'hidden_states': jax.random.normal(ks[0], (B, L, D), f32), 'Wq': jax.random.normal(ks[1], (D, Q_DIM), f32) * s, 'Wk': jax.random.normal(ks[2], (D, Q_DIM), f32) * s, 'Wv': jax.random.normal(ks[3], (D, V_DIM), f32) * s, 'Wb': jax.random.normal(ks[4], (D, H), f32) * s, 'bb': jnp.full((H,), -2.0, f32), 'Wg': jax.random.normal(ks[5], (D, V_DIM), f32) * s, 'Wo': jax.random.normal(ks[6], (V_DIM, D), f32) * s, 'qconv_w': jax.random.normal(ks[7], (Q_DIM, K), f32) * 0.5, 'qconv_b': jnp.zeros((Q_DIM,), f32), 'kconv_w': jax.random.normal(ks[8], (Q_DIM, K), f32) * 0.5, 'kconv_b': jnp.zeros((Q_DIM,), f32), 'qn_w': jnp.ones((DK,), f32), 'qn_b': jnp.zeros((DK,), f32), 'kn_w': jnp.ones((DK,), f32), 'kn_b': jnp.zeros((DK,), f32)}
    _L0_attn_in = _L0_attn_setup()

    def _L0_ffn_setup():
        import jax, jax.numpy as jnp
        import numpy as np
        B, L, D = (4, 1024, 512)
        DF = 4 * D
        CAPACITY_RATIO = 0.5
        key = jax.random.key(seed)
        ks = jax.random.split(key, 4)
        s = 0.02
        return {'x': jax.random.normal(ks[0], (B, L, D), dtype=jnp.float32), 'w_r': jax.random.normal(ks[1], (D,), dtype=jnp.float32) * s, 'b_r': jnp.zeros((), dtype=jnp.float32), 'w1': jax.random.normal(ks[2], (D, DF), dtype=jnp.float32) * s, 'b1': jnp.zeros((DF,), dtype=jnp.float32), 'w2': jax.random.normal(ks[3], (DF, D), dtype=jnp.float32) * s, 'b2': jnp.zeros((D,), dtype=jnp.float32)}
    _L0_ffn_in = _L0_ffn_setup()
    _d = {'L0_attn_hidden_states': _L0_attn_in['hidden_states'], 'L0_attn_Wq': _L0_attn_in['Wq'], 'L0_attn_Wk': _L0_attn_in['Wk'], 'L0_attn_Wv': _L0_attn_in['Wv'], 'L0_attn_Wb': _L0_attn_in['Wb'], 'L0_attn_bb': _L0_attn_in['bb'], 'L0_attn_Wg': _L0_attn_in['Wg'], 'L0_attn_Wo': _L0_attn_in['Wo'], 'L0_attn_qconv_w': _L0_attn_in['qconv_w'], 'L0_attn_qconv_b': _L0_attn_in['qconv_b'], 'L0_attn_kconv_w': _L0_attn_in['kconv_w'], 'L0_attn_kconv_b': _L0_attn_in['kconv_b'], 'L0_attn_qn_w': _L0_attn_in['qn_w'], 'L0_attn_qn_b': _L0_attn_in['qn_b'], 'L0_attn_kn_w': _L0_attn_in['kn_w'], 'L0_attn_kn_b': _L0_attn_in['kn_b'], 'L0_ffn_w_r': _L0_ffn_in['w_r'], 'L0_ffn_b_r': _L0_ffn_in['b_r'], 'L0_ffn_w1': _L0_ffn_in['w1'], 'L0_ffn_b1': _L0_ffn_in['b1'], 'L0_ffn_w2': _L0_ffn_in['w2'], 'L0_ffn_b2': _L0_ffn_in['b2']}
    _x0 = _d['L0_attn_hidden_states']
    _d['L0_attn_hidden_states'] = jax.random.normal(jax.random.fold_in(jax.random.key(seed), 1), (4, 1024, 512), dtype=_x0.dtype)
    del _x0
    return _d

def reference(L0_attn_hidden_states, L0_attn_Wq, L0_attn_Wk, L0_attn_Wv, L0_attn_Wb, L0_attn_bb, L0_attn_Wg, L0_attn_Wo, L0_attn_qconv_w, L0_attn_qconv_b, L0_attn_kconv_w, L0_attn_kconv_b, L0_attn_qn_w, L0_attn_qn_b, L0_attn_kn_w, L0_attn_kn_b, L0_ffn_w_r, L0_ffn_b_r, L0_ffn_w1, L0_ffn_b1, L0_ffn_w2, L0_ffn_b2):

    def _L0_attn_ref(hidden_states, Wq, Wk, Wv, Wb, bb, Wg, Wo, qconv_w, qconv_b, kconv_w, kconv_b, qn_w, qn_b, kn_w, kn_b):
        import jax, jax.numpy as jnp
        import numpy as np
        from jax import lax
        B, L, D = (2, 512, 512)
        H, DK, DV, K = (16, 128, 128, 4)
        Q_DIM = H * DK
        V_DIM = H * DV

        def silu(x):
            return x * jax.nn.sigmoid(x)

        def causal_dwconv(x, w, b):
            Kk = w.shape[1]
            xp = jnp.pad(x, ((0, 0), (Kk - 1, 0), (0, 0)))
            kern = w.T[:, None, :]
            y = lax.conv_general_dilated(xp, kern, window_strides=(1,), padding='VALID', dimension_numbers=('NWC', 'WIO', 'NWC'), feature_group_count=w.shape[0])
            return y + b

        def layernorm(x, w, b, eps=1e-05):
            m = jnp.mean(x, axis=-1, keepdims=True)
            var = jnp.mean((x - m) ** 2, axis=-1, keepdims=True)
            return (x - m) * lax.rsqrt(var + eps) * w + b
        Bs, Ls, Ds = hidden_states.shape
        q = hidden_states @ Wq
        k = hidden_states @ Wk
        v = hidden_states @ Wv
        beta = jax.nn.sigmoid(hidden_states @ Wb + bb)
        gate = silu(hidden_states @ Wg)
        q = silu(causal_dwconv(q, qconv_w, qconv_b))
        k = silu(causal_dwconv(k, kconv_w, kconv_b))
        q = layernorm(q.reshape(Bs, Ls, H, DK), qn_w, qn_b)
        k = layernorm(k.reshape(Bs, Ls, H, DK), kn_w, kn_b)
        v = v.reshape(Bs, Ls, H, DV)
        qs = q.transpose(1, 0, 2, 3)
        ks_ = k.transpose(1, 0, 2, 3)
        vs = v.transpose(1, 0, 2, 3)
        bs = beta.transpose(1, 0, 2)
        S0 = jnp.zeros((Bs, H, DV, DK), hidden_states.dtype)

        def step(S, inp):
            q_t, k_t, v_t, b_t = inp
            b = b_t[..., None, None]
            S = (1.0 - b) * S + b * (v_t[..., :, None] * k_t[..., None, :])
            o_t = jnp.einsum('bhvk,bhk->bhv', S, q_t)
            return (S, o_t)
        _, os = lax.scan(step, S0, (qs, ks_, vs, bs))
        o = os.transpose(1, 0, 2, 3).reshape(Bs, Ls, H * DV)
        o = o * gate
        return o @ Wo

    def _L0_ffn_ref(x, w_r, b_r, w1, b1, w2, b2):
        import jax, jax.numpy as jnp
        import numpy as np
        B, L, D = (4, 1024, 512)
        DF = 4 * D
        CAPACITY_RATIO = 0.5
        b, l, d = x.shape
        k = int(l * CAPACITY_RATIO)
        scores = jnp.einsum('bld,d->bl', x, w_r) + b_r
        _, idx = jax.lax.top_k(scores, k)
        x_sel = jnp.take_along_axis(x, idx[:, :, None], axis=1)
        h = jax.nn.gelu(jnp.einsum('bkd,df->bkf', x_sel, w1) + b1)
        out_sel = jnp.einsum('bkf,fd->bkd', h, w2) + b2
        batch_ix = jnp.arange(b)[:, None]
        out = jnp.zeros_like(x).at[batch_ix, idx].set(out_sel)
        return out
    x = L0_attn_hidden_states
    xn = _layernorm(x, axis=-1)
    s = _L0_attn_ref(xn, L0_attn_Wq, L0_attn_Wk, L0_attn_Wv, L0_attn_Wb, L0_attn_bb, L0_attn_Wg, L0_attn_Wo, L0_attn_qconv_w, L0_attn_qconv_b, L0_attn_kconv_w, L0_attn_kconv_b, L0_attn_qn_w, L0_attn_qn_b, L0_attn_kn_w, L0_attn_kn_b)
    g = _silu(_L0_ffn_ref(xn, L0_ffn_w_r, L0_ffn_b_r, L0_ffn_w1, L0_ffn_b1, L0_ffn_w2, L0_ffn_b2))
    x = x + s * g
    return x

_drawn_inputs = setup_inputs


def setup_inputs(seed=0):
    import zlib

    import numpy as np

    out = dict(_drawn_inputs(seed))
    spreads = {'L0_attn_bb': (-2.0, 0.6),
     'L0_attn_qconv_b': (0.0, 0.8),
     'L0_attn_kconv_b': (0.0, 0.8),
     'L0_attn_qn_w': (1.0, 0.6),
     'L0_attn_qn_b': (0.0, 0.8),
     'L0_attn_kn_w': (1.0, 0.6),
     'L0_attn_kn_b': (0.0, 0.8),
     'L0_ffn_b1': (0.0, 0.8),
     'L0_ffn_b2': (0.0, 0.642)}
    factors = {'L0_attn_Wb': 4.604}
    for name, (base, spread) in spreads.items():
        noise = np.random.default_rng([zlib.crc32(name.encode()), seed]).standard_normal(out[name].shape)
        drawn = base * np.exp(spread * noise) if base else spread * noise
        out[name] = jnp.asarray(drawn.astype(out[name].dtype))
    for name, factor in factors.items():
        out[name] = (out[name] * factor).astype(out[name].dtype)
    return out
```

```python
from contextlib import ExitStack

import numpy as np

import concourse.bass as bass
from concourse import mybir

ALU = mybir.AluOpType
ACT = mybir.ActivationFunctionType
F32 = mybir.dt.float32
F32R = mybir.dt.float32r
I32 = mybir.dt.int32
P = 128
EPS = 1e-5
BANK = 512


class Shapes:

    def __init__(self, x, wq, wb, qn_w, w1):
        self.B, self.L, self.D = x.shape
        self.H = wb.shape[1]
        self.DK = qn_w.shape[0]
        self.HD = wq.shape[1]
        self.F = w1.shape[1]
        self.KC = self.D // P
        self.NC = self.L // P
        self.HALVES = self.L // BANK
        self.SEL = self.L // 2
        self.ST = self.SEL // P
        self.N = self.B * self.H
        self.BLK = self.F // P
        self.PAIRS_PER_SEQ = self.H // 2
        assert self.DK == P and self.HD == self.H * P and self.F == self.HD
        assert self.KC == self.ST and self.D == BANK and self.SEL == BANK and self.HALVES == 2


def after(eng, sem, n):
    if isinstance(n, int) and n <= 0:
        return
    eng.wait_ge(sem, n)


def stand(eng, carrier):
    eng.sem_inc(carrier, 1)


def peeled(eng, first, count, body):
    for n in range(first):
        body(n)
    with eng.Fori(first, count) as n:
        body(n)


def row(ap, n):
    return ap[n] if isinstance(n, int) else ap[bass.ds(n, 1)].squeeze(0)


def stage_tokens(nc, s, a, scratch, keep):
    B, L, D, H, KC, NC = s.B, s.L, s.D, s.H, s.KC, s.NC
    with ExitStack() as ctx:
        def sb(name, shape, dt=F32):
            return ctx.enter_context(nc.sbuf_tensor("tk_" + name, shape, dt))

        def sem(name):
            return ctx.enter_context(nc.semaphore("tk_" + name))

        x_in = sb("x_in", [P, NC, D])
        xn = sb("xn", [P, NC, D])
        xt_hi = sb("xt_hi", [P, KC, L], F32R)
        xt_lo = sb("xt_lo", [P, KC, L], F32R)
        stats = sb("stats", [P, NC, 6])
        mean_var = sb("mean_var", [P, NC, 2])
        var_eps = sb("var_eps", [P, NC])
        minus_half = sb("minus_half", [P, NC])
        rstd = sb("rstd", [P, NC])
        shift = sb("shift", [P, NC])
        product = sb("product", [P, D])
        wr_all = sb("wr_all", [P, D])
        br_all = sb("br_all", [P, 1])
        raw_score = sb("raw_score", [P, NC])
        score = sb("score", [P, NC])
        wb_raw = sb("wb_raw", [P, KC, H])
        wb_hi = sb("wb_hi", [P, KC, P], F32R)
        wb_lo = sb("wb_lo", [P, KC, P], F32R)
        bb = sb("bb", [H, 1])
        beta = sb("beta", [H, L])
        one_minus = sb("one_minus", [H, L])
        inside = sb("inside", [H, L])
        decay = sb("decay", [H, L])
        restart = sb("restart", [H, L])
        cum = sb("cum", [H, L])
        ps_t = ctx.enter_context(nc.psum_tensor("tk_ps_t", [P, 2, L], F32))
        ps_beta = ctx.enter_context(nc.psum_tensor("tk_ps_beta", [P, L], F32))
        ps_tok = ctx.enter_context(nc.psum_tensor("tk_ps_tok", [P, NC, H], F32))

        consts_loaded = sem("consts_loaded")
        x_loaded = sem("x_loaded")
        xn_stored = sem("xn_stored")
        hi_stored = sem("hi_stored")
        lo_stored = sem("lo_stored")
        score_stored = sem("score_stored")
        decay_stored = sem("decay_stored")
        cum_stored = sem("cum_stored")
        consts_set = sem("consts_set")
        wb_split = sem("wb_split")
        stats_done = sem("stats_done")
        mean_done = sem("mean_done")
        var_done = sem("var_done")
        rstd_done = sem("rstd_done")
        shift_done = sem("shift_done")
        xn_done = sem("xn_done")
        raw_score_done = sem("raw_score_done")
        score_done = sem("score_done")
        t_done = sem("t_done")
        hi_done = sem("hi_done")
        lo_done = sem("lo_done")
        beta_mm = sem("beta_mm")
        beta_done = sem("beta_done")
        tok_mm = sem("tok_mm")
        tok_done = sem("tok_done")
        one_minus_done = sem("one_minus_done")
        decay_done = sem("decay_done")
        restart_done = sem("restart_done")
        cum_done = sem("cum_done")

        x_rows = a["x"].rearrange("b (c p) d -> b p c d", p=P)
        xn_rows = scratch["xn"].rearrange("(b c p) d -> b p c d", p=P, c=NC)
        score_rows = scratch["score"].rearrange("b (c p) -> b p c", p=P)
        decay_rows = scratch["decay"].rearrange("(b h) t -> b h t", h=H)
        cum_rows = scratch["cum"].rearrange("(b h) t -> b h t", h=H)

        block = ctx.enter_context(nc.Block())

        @block.sync
        def _(sp):
            sp.dma_start(x_in[:], x_rows[0]).then_inc(x_loaded, 16)
            with nc.allow_non_contiguous_dma("small constants and scores"):
                sp.dma_start(wr_all[:], a["w_r"].partition_broadcast(P)).then_inc(consts_loaded, 16)
                sp.dma_start(br_all[:], a["b_r"].partition_broadcast(P)).then_inc(consts_loaded, 16)
                sp.dma_start(wb_raw[:], a["wb"].rearrange("(k p) h -> p k h", p=P)).then_inc(consts_loaded, 16)
                sp.dma_start(bb[:], a["bb"].rearrange("(h o) -> h o", o=1)).then_inc(consts_loaded, 16)

                def sequence(b):
                    sp.wait_ge(xn_done, b + 1)
                    if not isinstance(b, int) or b < B - 1:
                        sp.dma_start(x_in[:], row(x_rows, b + 1)).then_inc(x_loaded, 16)
                    store(b)

                def store(b):
                    sp.wait_ge(xn_done, b + 1)
                    sp.dma_start(row(xn_rows, b), xn[:]).then_inc(xn_stored, 16)
                    sp.wait_ge(score_done, b + 1)
                    sp.dma_start(row(score_rows, b), score[:]).then_inc(score_stored, 16)
                    sp.wait_ge(hi_done, KC * b + KC)
                    sp.dma_start(row(scratch["xt_hi"], b), xt_hi[:].bitcast(F32)).then_inc(hi_stored, 16)
                    sp.wait_ge(lo_done, KC * b + KC)
                    sp.dma_start(row(scratch["xt_lo"], b), xt_lo[:].bitcast(F32)).then_inc(lo_stored, 16)
                    sp.wait_ge(decay_done, b + 1)
                    sp.dma_start(row(decay_rows, b), decay[:]).then_inc(decay_stored, 16)
                    sp.wait_ge(cum_done, b + 1)
                    sp.dma_start(row(cum_rows, b), cum[:]).then_inc(cum_stored, 16)

                with sp.Fori(0, B - 1) as b:
                    sequence(b)
                store(B - 1)
            for stored in (xn_stored, score_stored, hi_stored, lo_stored, decay_stored, cum_stored):
                sp.wait_ge(stored, 16 * B)
            sp.dma_start(a["out"].rearrange("b l d -> (b l) d"),
                         a["x"].rearrange("b l d -> (b l) d")).then_inc(keep["out_copied"], 16)

        @block.gpsimd
        def _(pool):
            nc.gpsimd.memset(minus_half[:], -0.5).then_inc(consts_set, 1)
            nc.gpsimd.memset(wb_hi[:].bitcast(F32), 0.0).then_inc(consts_set, 1)
            nc.gpsimd.memset(wb_lo[:].bitcast(F32), 0.0).then_inc(consts_set, 1)
            nc.gpsimd.memset(keep["ident"][:], 0.0).then_inc(consts_set, 1)
            nc.gpsimd.memset(inside[:], 1.0).then_inc(consts_set, 1)
            pool.wait_ge(consts_set, 5)
            nc.gpsimd.affine_select(out=keep["ident"][:], in_=keep["ident"][:], compare_op=ALU.not_equal,
                                    fill=1.0, base=0, pattern=[[-1, P]], channel_multiplier=1
                                    ).then_inc(consts_set, 1)
            nc.gpsimd.memset(inside[:].rearrange("h (c t) -> h c t", t=P)[:, :, 0:1], 0.0).then_inc(consts_set, 1)
            groups = s.BLK // 4
            nc.gpsimd.iota(keep["seq_shift"][:], pattern=[[-(L * B - 1) * groups, B]], base=0, channel_multiplier=0,
                           allow_small_or_imprecise_dtypes=True).then_inc(consts_set, 1)
            with pool.Fori(0, B) as b:
                pool.wait_ge(var_done, b + 1)
                nc.gpsimd.tensor_tensor(rstd[:], var_eps[:], minus_half[:], ALU.pow).then_inc(rstd_done, 1)

        @block.scalar
        def _(act):
            act.wait_ge(consts_loaded, 64)
            act.wait_ge(consts_set, 3)
            nc.scalar.activation(wb_hi[:, :, 0:H], wb_raw[:], ACT.Copy).then_inc(wb_split, 1)

            def sequence(b):
                after(act, xn_stored, 16 * b)
                after(act, raw_score_done, NC * b)
                after(act, t_done, KC * b)
                act.wait_ge(shift_done, b + 1)
                for c in range(NC):
                    last = nc.scalar.activation(xn[:, c], x_in[:, c], ACT.Identity,
                                                bias=shift[:, c:c + 1], scale=rstd[:, c:c + 1])
                last.then_inc(xn_done, 1)
                after(act, hi_stored, 16 * b)
                for k in range(KC):
                    act.wait_ge(t_done, KC * b + k + 1)
                    nc.scalar.activation(xt_hi[:, k], ps_t[:, k % 2], ACT.Copy).then_inc(hi_done, 1)
                act.wait_ge(beta_mm, b + 1)
                after(act, tok_mm, b)
                after(act, one_minus_done, b)
                nc.scalar.activation(beta[:], ps_beta[0:H], ACT.Sigmoid, bias=bb[:]).then_inc(beta_done, 1)

            peeled(act, 1, B, sequence)

        @block.vector
        def _(dve):
            dve.wait_ge(wb_split, 1)
            nc.vector.tensor_tensor(wb_lo[:, :, 0:H], wb_raw[:], wb_hi[:, :, 0:H].bitcast(F32), ALU.subtract
                                    ).then_inc(wb_split, 1)

            def sequence(b):
                dve.wait_ge(x_loaded, 16 * b + 16)
                for c in range(NC):
                    last = nc.vector.bn_stats(stats[:, c], x_in[:, c])
                last.then_inc(stats_done, 1)
                dve.wait_ge(stats_done, b + 1)
                after(dve, xn_done, b)
                stand(dve, keep["carrier_dve"])
                for c in range(NC):
                    last = nc.vector.bn_aggr(mean_var[:, c], stats[:, c])
                last.then_inc(mean_done, 1)
                dve.wait_ge(mean_done, b + 1)
                nc.vector.tensor_scalar(var_eps[:], mean_var[:, :, 1], EPS, None, ALU.add).then_inc(var_done, 1)
                dve.wait_ge(rstd_done, b + 1)
                nc.vector.scalar_tensor_tensor(out=shift[:], in0=mean_var[:, :, 0], scalar=-1.0, in1=rstd[:],
                                               op0=ALU.mult, op1=ALU.mult).then_inc(shift_done, 1)
                dve.wait_ge(xn_done, b + 1)
                after(dve, score_done, b)
                for c in range(NC):
                    after(dve, raw_score_done, NC * b + c)
                    nc.vector.scalar_tensor_tensor(out=product[:], in0=xn[:, c], scalar=1.0, in1=wr_all[:],
                                                   op0=ALU.mult, op1=ALU.mult, accum_out=raw_score[:, c:c + 1]
                                                   ).then_inc(raw_score_done, 1)
                dve.wait_ge(raw_score_done, NC * b + NC)
                after(dve, score_stored, 16 * b)
                nc.vector.tensor_scalar(score[:], raw_score[:], br_all[:], None, ALU.add).then_inc(score_done, 1)
                after(dve, lo_stored, 16 * b)
                for k in range(KC):
                    dve.wait_ge(hi_done, KC * b + k + 1)
                    nc.vector.tensor_tensor(xt_lo[:, k], ps_t[:, k % 2], xt_hi[:, k].bitcast(F32), ALU.subtract
                                            ).then_inc(lo_done, 1)
                dve.wait_ge(beta_done, b + 1)
                nc.vector.tensor_scalar(one_minus[:], beta[:], -1.0, 1.0, ALU.mult, ALU.add).then_inc(one_minus_done, 1)
                dve.wait_ge(one_minus_done, b + 1)
                after(dve, decay_stored, 16 * b)
                nc.vector.tensor_tensor(decay[:], one_minus[:], inside[:], ALU.mult).then_inc(decay_done, 1)
                dve.wait_ge(decay_done, b + 1)
                nc.vector.tensor_tensor(restart[:], one_minus[:], decay[:], ALU.subtract).then_inc(restart_done, 1)
                dve.wait_ge(restart_done, b + 1)
                after(dve, cum_stored, 16 * b)
                nc.vector.tensor_tensor_scan(cum[:], decay[:], restart[:], 0.0, ALU.mult, ALU.add).then_inc(cum_done, 1)
                dve.wait_ge(tok_mm, b + 1)
                nc.vector.tensor_copy(keep["beta_steps"][:, :, bass.ds(b * H, H)], ps_tok[:]).then_inc(tok_done, 1)

            dve.wait_ge(consts_loaded, 64)
            dve.wait_ge(consts_set, 8)
            peeled(dve, 1, B, sequence)

        @block.tensor
        def _(pe):
            pe.wait_ge(consts_set, 6)
            pe.wait_ge(wb_split, 2)

            def sequence(b):
                pe.wait_ge(xn_done, b + 1)
                for k in range(KC):
                    after(pe, lo_done, KC * b + k - 1)
                    for c in range(NC):
                        last = nc.tensor.transpose(ps_t[:, k % 2, c * P:(c + 1) * P],
                                                   xn[:, c, k * P:(k + 1) * P], keep["ident"][:])
                    last.then_inc(t_done, 1)
                pe.wait_ge(hi_done, KC * b + KC)
                pe.wait_ge(lo_done, KC * b + KC)
                after(pe, beta_done, b)
                for half in range(s.HALVES):
                    cols = slice(half * BANK, (half + 1) * BANK)
                    for k in range(KC):
                        nc.tensor.matmul(ps_beta[:, cols], wb_hi[:, k], xt_hi[:, k, cols], start=k == 0, stop=False)
                        nc.tensor.matmul(ps_beta[:, cols], wb_hi[:, k], xt_lo[:, k, cols], start=False, stop=False)
                        last = nc.tensor.matmul(ps_beta[:, cols], wb_lo[:, k], xt_hi[:, k, cols],
                                                start=False, stop=k == KC - 1)
                last.then_inc(beta_mm, 1)
                pe.wait_ge(beta_done, b + 1)
                after(pe, tok_done, b)
                stand(pe, keep["carrier_pe"])
                for c in range(NC):
                    last = nc.tensor.transpose(ps_tok[:, c], beta[:, c * P:(c + 1) * P], keep["ident"][0:H, 0:H])
                last.then_inc(tok_mm, 1)

            peeled(pe, 1, B, sequence)


def stage_recurrence(nc, s, a, scratch, keep):
    B, L, H, KC, NC, N = s.B, s.L, s.H, s.KC, s.NC, s.N
    TAPS = a["qconv_w"].shape[1]
    PAD = TAPS - 1
    LAG_B, LAG_C, LAG_D = 1, 2, 3
    PEELED_PAIRS = 2
    PAIRS = N // 2
    PPS = s.PAIRS_PER_SEQ
    with ExitStack() as ctx:
        def sb(name, shape, dt=F32):
            return ctx.enter_context(nc.sbuf_tensor("rc_" + name, shape, dt))

        def two(name, shape, dt=F32):
            return [sb(f"{name}{i}", shape, dt) for i in range(2)]

        def sem(name):
            return ctx.enter_context(nc.semaphore("rc_" + name))

        ident = keep["ident"]
        xt_hi = sb("xt_hi", [P, KC, L], F32R)
        xt_lo = sb("xt_lo", [P, KC, L], F32R)
        w_raw = two("w_raw", [P, 3, KC, P])
        w_hi = two("w_hi", [P, 3, KC, P], F32R)
        w_lo = two("w_lo", [P, 3, KC, P], F32R)
        conv = two("conv", [P, 2, TAPS + 1])
        norm = sb("norm", [P, 2, 2])
        raw = [sb("raw_q", [P, PAD + L]), sb("raw_k", [P, PAD + L])]
        act_cm = [sb("act_q", [P, L]), sb("act_k", [P, L])]
        tok = [sb("tok_q", [P, NC, P]), sb("tok_k", [P, NC, P])]
        v_cm = two("v_cm", [P, L])
        q_cm = two("q_cm", [P, L])
        k_cm = two("k_cm", [P, L])
        k_state = two("k_state", [P, NC, P])
        v_beta = two("v_beta", [P, NC, P])
        decay_all = two("decay_all", [P, L])
        cum_all = two("cum_all", [P, L])
        dmat = two("dmat", [P, NC, P])
        q_cum = sb("q_cum", [P, L])
        scores = sb("scores", [P, NC, P])
        states = sb("states", [P, NC - 1, P])
        o_sb = two("o_sb", [P, NC, P])
        chunk_ident = sb("chunk_ident", [P, NC, P])
        stats = sb("stats", [P, 2, NC, 6])
        small = sb("small", [P, 8, 2, NC])
        minus_half = sb("minus_half", [P, 2, NC])
        score_all = sb("score_all", [P, L])
        score_tok = sb("score_tok", [P, B * NC])
        equal = sb("equal", [P, L])
        token_row = sb("token_row", [P, L])
        token_col = sb("token_col", [P, B * NC])
        first_slot = sb("first_slot", [P, B * NC])
        greater = sb("greater", [P, 1])
        ties = sb("ties", [P, 1])
        slot = sb("slot", [P, 1], I32)
        token_id = sb("token_id", [P, 1], I32)

        ps_proj = ctx.enter_context(nc.psum_tensor("rc_ps_proj", [P, 2, L], F32))
        ps_work = ctx.enter_context(nc.psum_tensor("rc_ps_work", [P, 2, L], F32))

        names = """consts_loaded consts_set xt_loaded w_split
            q_projected k_projected v_projected q_raw k_raw q_tap k_tap q_conv k_conv q_silu k_silu v_copied
            q_turned k_turned q_tok k_tok stats_q stats_k small_done rstd_done shift_done q_normed k_normed
            q_back k_back k_again v_turned q_ready k_ready k_state_done v_beta_done
            dmat_done scores_mm scores_done updates_mm states_done outputs_mm outputs_done q_cum_done
            score_loaded greater_done equal_done ties_done slot_done id_done scattered"""
        S = {n: sem(n) for n in names.split()}
        w_loaded = [sem(f"w_loaded{i}") for i in range(2)]
        conv_loaded = [sem(f"conv_loaded{i}") for i in range(2)]
        decay_loaded = [sem(f"decay_loaded{i}") for i in range(2)]
        cum_loaded = [sem(f"cum_loaded{i}") for i in range(2)]
        o_stored = [sem(f"o_stored{i}") for i in range(2)]

        w_views = [a[n].rearrange("(k p) n -> p k n", p=P) for n in ("wq", "wk", "wv")]
        conv_w = [a["qconv_w"], a["kconv_w"]]
        conv_b = [a["qconv_b"].rearrange("(n o) -> n o", o=1), a["kconv_b"].rearrange("(n o) -> n o", o=1)]
        o_rows = scratch["o"].rearrange("(c p) n -> p c n", p=P)
        W_PARTS, CONV_PARTS = 3, 4

        class At:

            def __init__(self, u, par, lag=0):
                self.i = 2 * u + par - lag
                self.par = (par - lag) % 2
                self.pair = u + (par - lag) // 2
                self.live = not isinstance(self.i, int) or 0 <= self.i < N

        def after_step(eng, name, i, per=1, part=None):
            if isinstance(i, int):
                if i < 0:
                    return
                i = min(i, N - 1)
            eng.wait_ge(S[name], per * i + (per if part is None else part))

        def after_pair(eng, semaphore, pair, per=16):
            if isinstance(pair, int) and pair < 0:
                return
            eng.wait_ge(semaphore, per * pair + per)

        def steps(eng, step):
            for u in range(PEELED_PAIRS):
                for par in range(2):
                    step(u, par)
            with eng.Fori(PEELED_PAIRS, PAIRS) as u:
                for par in range(2):
                    step(u, par)
            for i in range(N, N + LAG_D):
                step(i // 2, i % 2)

        block = ctx.enter_context(nc.Block())

        @block.sync
        def _(sp):
            def load_xt(b):
                sp.dma_start(xt_hi[:].bitcast(F32), row(scratch["xt_hi"], b)).then_inc(S["xt_loaded"], 16)
                sp.dma_start(xt_lo[:].bitcast(F32), row(scratch["xt_lo"], b)).then_inc(S["xt_loaded"], 16)

            def load_pair(pair, head, seq):
                for par in range(2):
                    after(sp, S["w_split"], 2 * (2 * pair + par - 1))
                    for j in range(W_PARTS):
                        sp.dma_start(w_raw[par][:, j], w_views[j][:, :, bass.ds((head + par) * P, P)]
                                     ).then_inc(w_loaded[par], 16)
                for par in range(2):
                    after(sp, S["k_conv"], PAD * (2 * pair + par - 1))
                    stand(sp, keep["carrier_sp"])
                    for j in range(2):
                        sp.dma_start(conv[par][:, j, 0:TAPS], conv_w[j][bass.ds((head + par) * P, P), :]
                                     ).then_inc(conv_loaded[par], 16)
                        sp.dma_start(conv[par][:, j, TAPS:TAPS + 1], conv_b[j][bass.ds((head + par) * P, P), :]
                                     ).then_inc(conv_loaded[par], 16)
                after(sp, S["greater_done"], pair)
                after(sp, S["equal_done"], pair)
                sp.dma_start(score_all[:], row(scratch["score"], seq).partition_broadcast(P)
                             ).then_inc(S["score_loaded"], 16)

            with nc.allow_non_contiguous_dma("per-channel constants"):
                load_xt(0)
                for j in range(2):
                    for n, name in enumerate((("qn_w", "qn_b"), ("kn_w", "kn_b"))[j]):
                        sp.dma_start(norm[:, j, n:n + 1], a[name].rearrange("(n o) -> n o", o=1)
                                     ).then_inc(S["consts_loaded"], 16)
                sp.dma_start(score_tok[:], scratch["score"].rearrange("b (c p) -> p (b c)", p=P)
                             ).then_inc(S["consts_loaded"], 16)
                load_pair(0, 0, 0)
                with sp.Fori(0, B - 1) as b:
                    with sp.Fori(0, PPS) as hp:
                        load_pair(b * PPS + hp + 1, (hp * 2 + 2) % H, (b * PPS + hp + 1) // PPS)
                    sp.wait_ge(S["v_projected"], b * H + H)
                    load_xt(b + 1)
                with sp.Fori(0, PPS - 1) as hp:
                    load_pair((B - 1) * PPS + hp + 1, hp * 2 + 2, B - 1)

        @block.gpsimd
        def _(pool):
            nc.gpsimd.memset(minus_half[:], -0.5).then_inc(S["consts_set"], 1)
            nc.gpsimd.memset(raw[0][:, 0:PAD], 0.0).then_inc(S["consts_set"], 1)
            nc.gpsimd.memset(raw[1][:, 0:PAD], 0.0).then_inc(S["consts_set"], 1)
            for c in range(NC):
                last = nc.gpsimd.tensor_copy(chunk_ident[:, c], ident[:])
            last.then_inc(S["consts_set"], 1)
            nc.gpsimd.iota(token_row[:], pattern=[[1, L]], base=0, channel_multiplier=0,
                           allow_small_or_imprecise_dtypes=True).then_inc(S["consts_set"], 1)
            nc.gpsimd.iota(token_col[:], pattern=[[0, B], [P, NC]], base=0, channel_multiplier=1,
                           allow_small_or_imprecise_dtypes=True).then_inc(S["consts_set"], 1)
            nc.gpsimd.iota(first_slot[:], pattern=[[L, B], [0, NC]], base=0, channel_multiplier=0,
                           allow_small_or_imprecise_dtypes=True).then_inc(S["consts_set"], 1)

            def split(i, par, pair):
                after_pair(pool, w_loaded[par], pair, 16 * W_PARTS)
                after_step(pool, "v_projected", i - 2)
                stand(pool, keep["carrier_pool"])
                nc.gpsimd.tensor_copy(w_hi[par][:], w_raw[par][:]).then_inc(S["w_split"], 1)
                pool.wait_ge(S["w_split"], 2 * i + 1)
                nc.gpsimd.tensor_tensor(w_lo[par][:], w_raw[par][:], w_hi[par][:].bitcast(F32), ALU.subtract
                                        ).then_inc(S["w_split"], 1)

            def step(u, par):
                B_, D_, nxt = At(u, par, LAG_B), At(u, par, LAG_D), At(u, par, -1)
                if D_.live:
                    after_step(pool, "q_ready", D_.i)
                    after_pair(pool, cum_loaded[D_.par], D_.pair)
                    after_step(pool, "outputs_mm", D_.i - 1)
                    nc.gpsimd.tensor_tensor(q_cum[:], q_cm[D_.par][:], cum_all[D_.par][:], ALU.mult
                                            ).then_inc(S["q_cum_done"], 1)
                if B_.live:
                    after_step(pool, "small_done", B_.i, 6)
                    nc.gpsimd.tensor_tensor(small[:, 6], small[:, 5], minus_half[:], ALU.pow
                                            ).then_inc(S["rstd_done"], 1)
                if isinstance(nxt.i, int) and nxt.i >= N:
                    return
                split(nxt.i, nxt.par, nxt.pair)

            split(0, 0, 0)

            def pair_steps(u):
                step(u, 0)
                step(u, 1)
                scatter(u)

            def scatter(u):
                pool.wait_ge(S["slot_done"], u + 1)
                pool.wait_ge(S["id_done"], u + 1)
                stand(pool, keep["carrier_pool"])
                nc.gpsimd.indirect_dma_start(
                    out=scratch["ids"], out_offset=bass.IndirectOffsetOnAxis(ap=slot[:, 0:1], axis=0),
                    in_=token_id[:, 0:1], in_offset=None).then_inc(S["scattered"], 16)

            for u in range(PEELED_PAIRS):
                pair_steps(u)
            with pool.Fori(PEELED_PAIRS, PAIRS - 1) as u:
                pair_steps(u)
            pair_steps(PAIRS - 1)
            for i in range(N, N + LAG_D):
                step(i // 2, i % 2)
            pool.wait_ge(S["scattered"], 16 * PAIRS)

        @block.scalar
        def _(act):
            act.wait_ge(S["consts_loaded"], 16 * 5)
            act.wait_ge(S["consts_set"], 7)

            def load_decay(par, i, pair):
                after_step(act, "dmat_done", i - 2)
                act.dma_start(decay_all[par][:], row(scratch["decay"], i).partition_broadcast(P)
                              ).then_inc(decay_loaded[par], 16)

            def load_cum(par, i, pair):
                after_step(act, "states_done", i - 2, NC - 1)
                after_step(act, "q_cum_done", i - 2)
                act.dma_start(cum_all[par][:], row(scratch["cum"], i).partition_broadcast(P)
                              ).then_inc(cum_loaded[par], 16)

            def step(u, par):
                A_, B_, C_, D_ = (At(u, par, lag) for lag in (0, LAG_B, LAG_C, LAG_D))
                proj_of = lambda pos: ps_proj[:, (par + pos) % 2]

                def ready(j, name_in, name_out, out):
                    after_step(act, name_in, C_.i)
                    after_step(act, "scores_mm", C_.i - 2)
                    if j == 0:
                        after_step(act, "q_cum_done", C_.i - 2)
                    else:
                        after_step(act, "k_again", C_.i - 2)
                    nc.scalar.activation(out[:], work(par, j), ACT.Identity,
                                         bias=norm[:, j, 1:2], scale=norm[:, j, 0:1]).then_inc(S[name_out], 1)

                def own_raw(j):
                    n = "qk"[j]
                    after_step(act, n + "_projected", A_.i)
                    after_step(act, n + "_conv", A_.i - 1, PAD)
                    nc.scalar.activation(raw[j][:, PAD:], proj_of(j), ACT.Copy).then_inc(S[n + "_raw"], 1)

                def tap(j):
                    n = "qk"[j]
                    if j == 0:
                        after_pair(act, conv_loaded[par], A_.pair, 16 * CONV_PARTS)
                    after_step(act, n + "_turned", A_.i - 1)
                    nc.scalar.activation(act_cm[j][:], proj_of(j), ACT.Identity,
                                         bias=conv[par][:, j, TAPS:TAPS + 1],
                                         scale=conv[par][:, j, PAD:TAPS]).then_inc(S[n + "_tap"], 1)

                def tokens(j):
                    n = "qk"[j]
                    after_step(act, n + "_turned", B_.i)
                    after_step(act, n + "_back", B_.i - 1)
                    nc.scalar.activation(tok[j][:], work(par, 2 + j), ACT.Copy).then_inc(S[n + "_tok"], 1)

                def silu(j):
                    n = "qk"[j]
                    after_step(act, n + "_conv", B_.i, PAD)
                    nc.scalar.activation(act_cm[j][:], act_cm[j][:], ACT.Silu).then_inc(S[n + "_silu"], 1)

                if C_.live:
                    ready(0, "q_back", "q_ready", q_cm[C_.par])
                if B_.live:
                    silu(0)
                if A_.live:
                    own_raw(0)
                if C_.live:
                    ready(1, "k_back", "k_ready", k_cm[C_.par])
                if B_.live:
                    silu(1)
                    tokens(0)
                if A_.live:
                    tap(0)
                if B_.live:
                    tokens(1)
                if A_.live:
                    own_raw(1)
                    tap(1)
                if B_.live:
                    load_decay(B_.par, B_.i, B_.pair)
                if C_.live:
                    load_cum(C_.par, C_.i, C_.pair)
                if A_.live:
                    after_step(act, "v_projected", A_.i)
                    after_step(act, "v_turned", A_.i - 2)
                    nc.scalar.activation(v_cm[par][:], proj_of(2), ACT.Copy).then_inc(S["v_copied"], 1)
                if D_.live:
                    after_step(act, "outputs_mm", D_.i)
                    after_pair(act, o_stored[D_.par], D_.pair - 1)
                    nc.scalar.activation(o_sb[D_.par][:], work(par, 8), ACT.Copy).then_inc(S["outputs_done"], 1)
                    after_step(act, "outputs_done", D_.i)
                    act.dma_start(o_rows[:, :, bass.ds(D_.i * P, P)], o_sb[D_.par][:]).then_inc(o_stored[D_.par], 16)

            def work(par, pos):
                return ps_work[:, (par + pos) % 2]

            steps(act, step)
            for par in range(2):
                act.wait_ge(o_stored[par], 16 * PAIRS)

        @block.vector
        def _(dve):
            dve.wait_ge(S["consts_loaded"], 16 * 5)
            dve.wait_ge(S["consts_set"], 7)

            def work(par, pos):
                return ps_work[:, (par + pos) % 2]

            def chunks(ap):
                return ap.rearrange("p (c t) -> p c t", t=P)

            def step(u, par):
                A_, B_, C_, D_ = (At(u, par, lag) for lag in (0, LAG_B, LAG_C, LAG_D))

                def convolve(j):
                    n = "qk"[j]
                    after_step(dve, n + "_raw", B_.i)
                    after_step(dve, n + "_tap", B_.i)
                    for t in range(PAD):
                        if t:
                            after_step(dve, n + "_conv", B_.i, PAD, t)
                        nc.vector.scalar_tensor_tensor(out=act_cm[j][:], in0=raw[j][:, t:t + L],
                                                       scalar=conv[B_.par][:, j, t:t + 1], in1=act_cm[j][:],
                                                       op0=ALU.mult, op1=ALU.add).then_inc(S[n + "_conv"], 1)

                def statistics(j):
                    n = "qk"[j]
                    after_step(dve, n + "_tok", B_.i)
                    for c in range(NC):
                        last = nc.vector.bn_stats(stats[:, j, c], tok[j][:, c])
                    last.then_inc(S["stats_" + n], 1)

                def variance():
                    m_even, q_even, m_odd, q_odd = (stats[:, :, :, n] for n in (1, 2, 4, 5))
                    after_step(dve, "stats_q", B_.i)
                    after_step(dve, "stats_k", B_.i)
                    after_step(dve, "shift_done", B_.i - 1)
                    after_step(dve, "k_normed", B_.i - 1)
                    done = lambda part: after_step(dve, "small_done", B_.i, 6, part)
                    inc = lambda ins: ins.then_inc(S["small_done"], 1)
                    inc(nc.vector.tensor_tensor(small[:, 0], m_even, m_odd, ALU.add))
                    inc(nc.vector.tensor_tensor(small[:, 1], m_even, m_odd, ALU.subtract))
                    inc(nc.vector.tensor_tensor(small[:, 2], q_even, q_odd, ALU.add))
                    done(2)
                    inc(nc.vector.tensor_tensor(small[:, 3], small[:, 1], small[:, 1], ALU.mult))
                    done(3)
                    inc(nc.vector.tensor_scalar(small[:, 4], small[:, 2], 1.0 / P, EPS, ALU.mult, ALU.add))
                    done(5)
                    inc(nc.vector.scalar_tensor_tensor(out=small[:, 5], in0=small[:, 3], scalar=0.25,
                                                       in1=small[:, 4], op0=ALU.mult, op1=ALU.add))

                def normalise():
                    after_step(dve, "rstd_done", B_.i)
                    nc.vector.scalar_tensor_tensor(out=small[:, 7], in0=small[:, 0], scalar=-0.5, in1=small[:, 6],
                                                   op0=ALU.mult, op1=ALU.mult).then_inc(S["shift_done"], 1)
                    after_step(dve, "shift_done", B_.i)
                    for j in range(2):
                        for c in range(NC):
                            last = nc.vector.tensor_scalar(tok[j][:, c], tok[j][:, c], small[:, 6, j, c:c + 1],
                                                           small[:, 7, j, c:c + 1], ALU.mult, ALU.add)
                        last.then_inc(S["qk"[j] + "_normed"], 1)

                if B_.live:
                    convolve(0)
                    convolve(1)
                if C_.live:
                    after_pair(dve, decay_loaded[C_.par], C_.pair)
                    after_step(dve, "scores_done", C_.i - 2)
                    nc.vector.tensor_tensor_scan(dmat[C_.par][:].rearrange("p c t -> p (c t)"), decay_all[C_.par][:],
                                                 chunk_ident[:].rearrange("p c t -> p (c t)"), 0.0,
                                                 ALU.mult, ALU.add).then_inc(S["dmat_done"], 1)
                if B_.live:
                    statistics(0)
                    statistics(1)
                if D_.live:
                    after_step(dve, "scores_mm", D_.i)
                    after_step(dve, "outputs_mm", D_.i - 1)
                    nc.vector.tensor_tensor(scores[:], chunks(work(par, 4)), dmat[D_.par][:], ALU.mult
                                            ).then_inc(S["scores_done"], 1)
                if B_.live:
                    variance()
                if C_.live:
                    after_step(dve, "k_again", C_.i)
                    after_step(dve, "dmat_done", C_.i)
                    after_step(dve, "updates_mm", C_.i - 2)
                    nc.vector.tensor_tensor(k_state[C_.par][:], chunks(work(par, 5)),
                                            dmat[C_.par][:, :, P - 1:P].to_broadcast([P, NC, P]), ALU.mult
                                            ).then_inc(S["k_state_done"], 1)
                if D_.live:
                    after_step(dve, "updates_mm", D_.i)
                    after_step(dve, "outputs_mm", D_.i - 1)
                    after_pair(dve, cum_loaded[D_.par], D_.pair)
                    updates = chunks(work(par, 6))
                    nc.vector.tensor_copy(states[:, 0], updates[:, 0]).then_inc(S["states_done"], 1)
                    for c in range(1, NC - 1):
                        after_step(dve, "states_done", D_.i, NC - 1, c)
                        last_token = c * P + P - 1
                        nc.vector.scalar_tensor_tensor(out=states[:, c], in0=states[:, c - 1],
                                                       scalar=cum_all[D_.par][:, last_token:last_token + 1],
                                                       in1=updates[:, c], op0=ALU.mult, op1=ALU.add
                                                       ).then_inc(S["states_done"], 1)
                if B_.live:
                    normalise()
                if C_.live:
                    after_step(dve, "v_turned", C_.i)
                    after_step(dve, "outputs_mm", C_.i - 2)
                    after_step(dve, "updates_mm", C_.i - 2)
                    gate = keep["beta_steps"][:, :, bass.ds(C_.i, 1)].to_broadcast([P, NC, P])
                    nc.vector.tensor_tensor(v_beta[C_.par][:], chunks(work(par, 7)), gate, ALU.mult
                                            ).then_inc(S["v_beta_done"], 1)
                if A_.live and par == 1:
                    ranks(u)

            def ranks(u):
                dve.wait_ge(S["score_loaded"], 16 * u + 16)
                own = score_tok[:, bass.ds(u, 1)]
                after(dve, S["slot_done"], u)
                nc.vector.tensor_scalar(equal[:], score_all[:], own, None, ALU.is_gt, ALU.add, accum_out=greater[:]
                                        ).then_inc(S["greater_done"], 1)
                dve.wait_ge(S["greater_done"], u + 1)
                after(dve, S["ties_done"], u)
                nc.vector.tensor_scalar(equal[:], score_all[:], own, None, ALU.is_equal).then_inc(S["equal_done"], 1)
                dve.wait_ge(S["equal_done"], u + 1)
                nc.vector.scalar_tensor_tensor(out=equal[:], in0=token_row[:], scalar=token_col[:, bass.ds(u, 1)],
                                               in1=equal[:], op0=ALU.is_lt, op1=ALU.mult, accum_out=ties[:]
                                               ).then_inc(S["ties_done"], 1)
                dve.wait_ge(S["ties_done"], u + 1)
                after(dve, S["scattered"], 16 * u)
                nc.vector.scalar_tensor_tensor(out=slot[:], in0=greater[:], scalar=ties[:], in1=first_slot[:, bass.ds(u, 1)],
                                               op0=ALU.add, op1=ALU.add).then_inc(S["slot_done"], 1)
                nc.vector.tensor_scalar(token_id[:], token_col[:, bass.ds(u, 1)], 1.0, first_slot[:, bass.ds(u, 1)],
                                        ALU.mult, ALU.add).then_inc(S["id_done"], 1)

            steps(dve, step)

        @block.tensor
        def _(pe):
            def work(par, pos):
                return ps_work[:, (par + pos) % 2]

            def turn(out, source):
                for c in range(NC):
                    last = nc.tensor.transpose(out[:, c * P:(c + 1) * P], source(c), ident[:])
                return last

            def step(u, par):
                A_, B_, C_, D_ = (At(u, par, lag) for lag in (0, LAG_B, LAG_C, LAG_D))

                def project(pos, half):
                    if half == 0:
                        if pos == 0:
                            pe.wait_ge(S["xt_loaded"], ((A_.i // H) + 1) * 32)
                            after_step(pe, "w_split", A_.i, 2)
                            after_step(pe, "k_tap", A_.i - 1)
                        elif pos == 1:
                            after_step(pe, "v_copied", A_.i - 1)
                        else:
                            after_step(pe, "q_tap", A_.i)
                    out = ps_proj[:, (par + pos) % 2, half * BANK:(half + 1) * BANK]
                    cols = slice(half * BANK, (half + 1) * BANK)
                    for k in range(KC):
                        hi, lo = w_hi[par][:, pos, k], w_lo[par][:, pos, k]
                        nc.tensor.matmul(out, hi, xt_hi[:, k, cols], start=k == 0, stop=False)
                        nc.tensor.matmul(out, hi, xt_lo[:, k, cols], start=False, stop=False)
                        last = nc.tensor.matmul(out, lo, xt_hi[:, k, cols], start=False, stop=k == KC - 1)
                    if half == s.HALVES - 1:
                        last.then_inc(S["qkv"[pos] + "_projected"], 1)

                if A_.live:
                    project(0, 0)
                if C_.live:
                    after_step(pe, "q_normed", C_.i)
                    after_step(pe, "v_beta_done", C_.i - 1)
                    turn(work(par, 0), lambda c: tok[0][:, c]).then_inc(S["q_back"], 1)
                if A_.live:
                    project(0, 1)
                if C_.live:
                    after_step(pe, "k_normed", C_.i)
                    after_step(pe, "outputs_done", D_.i - 1)
                    turn(work(par, 1), lambda c: tok[1][:, c]).then_inc(S["k_back"], 1)
                if B_.live:
                    after_step(pe, "q_silu", B_.i)
                    after_step(pe, "q_ready", C_.i)
                    turn(work(par, 2), lambda c: act_cm[0][:, c * P:(c + 1) * P]).then_inc(S["q_turned"], 1)
                if A_.live:
                    project(1, 0)
                if B_.live:
                    after_step(pe, "k_silu", B_.i)
                    after_step(pe, "k_ready", C_.i)
                    turn(work(par, 3), lambda c: act_cm[1][:, c * P:(c + 1) * P]).then_inc(S["k_turned"], 1)
                if D_.live:
                    after_step(pe, "k_ready", D_.i)
                    after_step(pe, "q_ready", D_.i)
                    after_step(pe, "q_tok", B_.i)
                    if not B_.live:
                        after_step(pe, "q_ready", C_.i)
                    if not C_.live:
                        after_step(pe, "v_beta_done", C_.i)
                    for c in range(NC):
                        t = slice(c * P, (c + 1) * P)
                        last = nc.tensor.matmul(work(par, 4)[:, t], k_cm[D_.par][:, t], q_cm[D_.par][:, t],
                                                start=True, stop=True)
                    last.then_inc(S["scores_mm"], 1)
                if A_.live:
                    project(1, 1)
                if C_.live:
                    after_step(pe, "k_ready", C_.i)
                    after_step(pe, "k_tok", B_.i)
                    turn(work(par, 5), lambda c: k_cm[C_.par][:, c * P:(c + 1) * P]).then_inc(S["k_again"], 1)
                if D_.live:
                    after_step(pe, "k_state_done", D_.i)
                    after_step(pe, "v_beta_done", D_.i)
                    after_step(pe, "scores_done", D_.i)
                    for c in range(NC - 1):
                        last = nc.tensor.matmul(work(par, 6)[:, c * P:(c + 1) * P], k_state[D_.par][:, c],
                                                v_beta[D_.par][:, c], start=True, stop=True)
                    last.then_inc(S["updates_mm"], 1)
                if A_.live:
                    project(2, 0)
                if C_.live:
                    after_step(pe, "v_copied", C_.i)
                    after_step(pe, "k_state_done", C_.i)
                    turn(work(par, 7), lambda c: v_cm[C_.par][:, c * P:(c + 1) * P]).then_inc(S["v_turned"], 1)
                if A_.live:
                    project(2, 1)
                if D_.live:
                    after_step(pe, "states_done", D_.i, NC - 1)
                    after_step(pe, "q_cum_done", D_.i)
                    after_step(pe, "scores_done", D_.i)
                    for c in range(NC):
                        out = work(par, 8)[:, c * P:(c + 1) * P]
                        last = nc.tensor.matmul(out, scores[:, c], v_beta[D_.par][:, c], start=True, stop=c == 0)
                        if c:
                            last = nc.tensor.matmul(out, q_cum[:, c * P:(c + 1) * P], states[:, c - 1],
                                                    start=False, stop=True)
                    last.then_inc(S["outputs_mm"], 1)

            pe.wait_ge(S["consts_set"], 4)
            steps(pe, step)


def stage_kept_tokens(nc, s, a, scratch, keep, gated):
    B, L, H, KC, ST, SEL, BLK, D = s.B, s.L, s.H, s.KC, s.ST, s.SEL, s.BLK, s.D
    tag = "gt_" if gated else "ff_"
    GROUP = 4
    GROUPS = BLK // GROUP
    WIDE = GROUP * P
    with ExitStack() as ctx:
        def sb(name, shape, dt=F32):
            return ctx.enter_context(nc.sbuf_tensor(tag + name, shape, dt))

        def two(name, shape, dt=F32):
            return [sb(f"{name}{i}", shape, dt) for i in range(2)]

        def sem(name):
            return ctx.enter_context(nc.semaphore(tag + name))

        ident = keep["ident"]
        up_hi = sb("up_hi", [P, GROUPS, KC, WIDE], F32R)
        up_lo = sb("up_lo", [P, GROUPS, KC, WIDE], F32R)
        down_hi = sb("down_hi", [P, GROUPS, GROUP, D], F32R)
        down_lo = sb("down_lo", [P, GROUPS, GROUP, D], F32R)
        x_rows = sb("x_rows", [P, ST, D])
        xt_hi = sb("xt_hi", [P, KC, SEL], F32R)
        xt_lo = sb("xt_lo", [P, KC, SEL], F32R)
        ids = sb("ids", [P, ST], I32)
        ids_f = sb("ids_f", [P, ST])
        wide = two("wide", [P, SEL])
        wide_hi = two("wide_hi", [P, SEL], F32R)
        wide_lo = two("wide_lo", [P, SEL], F32R)
        if gated:
            w_raw = two("w_raw", [P, KC, WIDE // 2])
            o_ids_f = sb("o_ids_f", [P, 2, ST])
            o_ids = sb("o_ids", [P, GROUPS, ST], I32)
            o_rows = two("o_rows", [P, ST, WIDE])
            gate = two("gate", [P, SEL])
            ffn = sb("ffn", [P, D])
        else:
            w_raw = two("w_raw", [P, KC, WIDE // 2])
            b1 = sb("b1", [P, BLK])
            b2 = sb("b2", [P, D])
            result = sb("result", [P, ST, D])
        ps_up = ctx.enter_context(nc.psum_tensor(tag + "ps_up", [P, 2, SEL], F32))
        ps_turn = ctx.enter_context(nc.psum_tensor(tag + "ps_turn", [P, 2, SEL], F32))
        ps_out = ctx.enter_context(nc.psum_tensor(tag + "ps_out", [P, ST, D], F32))

        names = """consts_loaded w_hi_done w_lo_done ids_loaded ids_f_done x_gathered x_turned x_hi_done x_lo_done
            up_mm wide_done wide_hi_done wide_lo_done down_mm o_ids_f_done o_ids_done o_turned gate_done
            result_done stored ffn_loaded silu_done times_done kept_loaded plus_done"""
        S = {n: sem(n) for n in names.split()}
        w_loaded = [sem(f"w_loaded{i}") for i in range(2)]
        o_gathered = [sem(f"o_gathered{i}") for i in range(2)]

        up_w, down_w = (a["wg"], a["wo"]) if gated else (a["w1"], a["w2"])
        up_view = up_w.rearrange("(k p) n -> p k n", p=P)
        down_view = down_w.rearrange("(m p) n -> p m n", p=P)
        PIECES = 4 * GROUPS
        HALF_W, HALF_G = WIDE // 2, GROUP // 2
        ffn_rows = scratch["ffn"].rearrange("(b t p) d -> b p t d", p=P, t=ST)
        id_rows = scratch["ids"].rearrange("(b h t p) o -> b h p (t o)", p=P, t=ST, h=L // SEL)

        def piece(n):
            g, part = divmod(n, 4)
            half = part % 2
            if part < 2:
                cols = slice(half * HALF_W, (half + 1) * HALF_W)
                return (up_view[:, :, g * WIDE + half * HALF_W:g * WIDE + (half + 1) * HALF_W],
                        w_raw[n % 2][:], up_hi[:, g, :, cols], up_lo[:, g, :, cols])
            blocks = slice(half * HALF_G, (half + 1) * HALF_G)
            staged = w_raw[n % 2][:].rearrange("p k w -> p (k w)").rearrange("p (m d) -> p m d", d=D)
            return (down_view[:, g * GROUP + half * HALF_G:g * GROUP + (half + 1) * HALF_G, :],
                    staged, down_hi[:, g, blocks], down_lo[:, g, blocks])

        block = ctx.enter_context(nc.Block())

        @block.sync
        def _(sp):
            with nc.allow_non_contiguous_dma("token ids and per-channel constants"):
                sp.dma_start(ids[:], id_rows[0, 0]).then_inc(S["ids_loaded"], 16)
                if not gated:
                    sp.dma_start(b1[:], a["b1"].rearrange("(m p) -> p m", p=P)).then_inc(S["consts_loaded"], 16)
                    sp.dma_start(b2[:], a["b2"].partition_broadcast(P)).then_inc(S["consts_loaded"], 16)
                for n in range(PIECES):
                    after(sp, S["w_lo_done"], n - 1)
                    sp.dma_start(piece(n)[1], piece(n)[0]).then_inc(w_loaded[n % 2], 16)

                def sequence(b):
                    if gated:
                        for t in range(ST):
                            after(sp, S["times_done"], ST * b + t)
                            sp.dma_start(ffn[:], row(ffn_rows, b)[:, t]).then_inc(S["ffn_loaded"], 16)
                    else:
                        sp.wait_ge(S["result_done"], ST * b + ST)
                        sp.dma_start(row(ffn_rows, b), result[:]).then_inc(S["stored"], 16)
                    if not (isinstance(b, int) and b == B - 1):
                        if gated:
                            sp.wait_ge(S["stored"], 16 * (ST * b + ST))
                        sp.wait_ge(S["x_gathered"], 16 * (ST * b + ST))
                        sp.dma_start(ids[:], id_rows[bass.ds(b + 1, 1), 0].squeeze(0)).then_inc(S["ids_loaded"], 16)

                with sp.Fori(0, B - 1) as b:
                    sequence(b)
                sequence(B - 1)
            if not gated:
                sp.wait_ge(S["stored"], 16 * B)

        @block.gpsimd
        def _(pool):
            if gated:
                pool.wait_ge(keep["out_copied"], 16)

            def gather(out, source, index):
                return nc.gpsimd.indirect_dma_start(out=out, out_offset=None, in_=source,
                                                    in_offset=bass.IndirectOffsetOnAxis(ap=index, axis=0))

            def sequence(b):
                pool.wait_ge(S["ids_loaded"], 16 * b + 16)
                after(pool, S["x_turned"], KC * b)
                stand(pool, keep["carrier_pool"])
                for t in range(ST):
                    gather(x_rows[:, t], scratch["xn"], ids[:, t:t + 1]).then_inc(S["x_gathered"], 16)
                if not gated:
                    return
                for g in range(GROUPS):
                    after(pool, S["o_turned"], BLK * b + GROUP * (g - 1))
                    if g == 0:
                        pool.wait_ge(S["o_ids_done"], b + 1)
                    stand(pool, keep["carrier_pool"])
                    for t in range(ST):
                        gather(o_rows[g % 2][:, t], scratch["o"].rearrange("l (g w) -> (l g) w", w=WIDE),
                               o_ids[:, g, t:t + 1]).then_inc(o_gathered[g % 2], 16)
                pool.wait_ge(S["x_turned"], KC * b + KC)
                stand(pool, keep["carrier_pool"])
                for t in range(ST):
                    gather(x_rows[:, t], a["x"].rearrange("b l d -> (b l) d"), ids[:, t:t + 1]
                           ).then_inc(S["kept_loaded"], 16)
                for t in range(ST):
                    pool.wait_ge(S["plus_done"], ST * b + t + 1)
                    stand(pool, keep["carrier_pool"])
                    nc.gpsimd.indirect_dma_start(
                        out=a["out"].rearrange("b l d -> (b l) d"),
                        out_offset=bass.IndirectOffsetOnAxis(ap=ids[:, t:t + 1], axis=0),
                        in_=x_rows[:, t], in_offset=None).then_inc(S["stored"], 16)
                pool.wait_ge(S["stored"], 16 * (ST * b + ST))

            peeled(pool, 1, B, sequence)

        @block.scalar
        def _(act):
            def split_piece(n):
                _, staged, hi, _ = piece(n)
                act.wait_ge(w_loaded[n % 2], 16 * (n // 2 + 1))
                nc.scalar.activation(hi, staged, ACT.Copy).then_inc(S["w_hi_done"], 1)

            def split_x(b):
                for k in range(KC):
                    act.wait_ge(S["x_turned"], KC * b + k + 1)
                    after(act, S["up_mm"], BLK * b)
                    nc.scalar.activation(xt_hi[:, k], ps_turn[:, k % 2], ACT.Copy).then_inc(S["x_hi_done"], 1)

            def sequence(b, pieces=False):
                if pieces:
                    for n in range(4):
                        split_piece(n)
                split_x(b)
                for m in range(BLK):
                    if pieces and m % GROUP == 0 and m // GROUP + 1 < GROUPS:
                        for n in range(4):
                            split_piece(4 * (m // GROUP + 1) + n)
                    act.wait_ge(S["up_mm"], BLK * b + m + 1)
                    if gated:
                        after(act, S["wide_done"], BLK * b + m - 1)
                        nc.scalar.activation(gate[m % 2][:], ps_up[:, m % 2], ACT.Silu).then_inc(S["gate_done"], 1)
                    else:
                        after(act, S["wide_lo_done"], BLK * b + m - 1)
                        nc.scalar.activation(wide[m % 2][:], ps_up[:, m % 2], ACT.Gelu_apprx_tanh,
                                             bias=b1[:, m:m + 1]).then_inc(S["wide_done"], 1)
                    act.wait_ge(S["wide_done"], BLK * b + m + 1)
                    after(act, S["down_mm"], BLK * b + m - 1)
                    nc.scalar.activation(wide_hi[m % 2][:], wide[m % 2][:], ACT.Copy).then_inc(S["wide_hi_done"], 1)
                if gated:
                    for t in range(ST):
                        act.wait_ge(S["ffn_loaded"], 16 * (ST * b + t + 1))
                        nc.scalar.activation(ffn[:], ffn[:], ACT.Silu).then_inc(S["silu_done"], 1)

            if not gated:
                act.wait_ge(S["consts_loaded"], 32)
            sequence(0, True)
            with act.Fori(1, B) as b:
                sequence(b)

        @block.vector
        def _(dve):
            def split_piece(n):
                _, staged, hi, lo = piece(n)
                dve.wait_ge(S["w_hi_done"], n + 1)
                nc.vector.tensor_tensor(lo, staged, hi.bitcast(F32), ALU.subtract).then_inc(S["w_lo_done"], 1)

            def o_indices(b):
                dve.wait_ge(S["ids_loaded"], 16 * b + 16)
                dve.wait_ge(S["ids_f_done"], b + 1)
                nc.vector.tensor_scalar(o_ids_f[:, 0], ids_f[:], float(B * GROUPS),
                                        keep["seq_shift"][:, bass.ds(b, 1)], ALU.mult, ALU.add
                                        ).then_inc(S["o_ids_f_done"], 1)
                dve.wait_ge(S["o_ids_f_done"], b + 1)
                after(dve, o_gathered[(GROUPS - 1) % 2], 16 * ST * (GROUPS // 2) * b)
                for g in range(GROUPS):
                    last = nc.vector.tensor_scalar(o_ids[:, g], o_ids_f[:, 0], float(g), None, ALU.add)
                last.then_inc(S["o_ids_done"], 1)

            def sequence(b, pieces=False):
                if gated:
                    dve.wait_ge(S["ids_loaded"], 16 * b + 16)
                    nc.vector.tensor_copy(ids_f[:], ids[:]).then_inc(S["ids_f_done"], 1)
                    o_indices(b)
                if pieces:
                    for n in range(4):
                        split_piece(n)
                for k in range(KC):
                    dve.wait_ge(S["x_hi_done"], KC * b + k + 1)
                    nc.vector.tensor_tensor(xt_lo[:, k], ps_turn[:, k % 2], xt_hi[:, k].bitcast(F32), ALU.subtract
                                            ).then_inc(S["x_lo_done"], 1)
                for m in range(BLK):
                    if pieces and m % GROUP == 0 and m // GROUP + 1 < GROUPS:
                        for n in range(4):
                            split_piece(4 * (m // GROUP + 1) + n)
                    if gated:
                        dve.wait_ge(S["gate_done"], BLK * b + m + 1)
                        dve.wait_ge(S["o_turned"], BLK * b + m + 1)
                        after(dve, S["wide_hi_done"], BLK * b + m - 1)
                        after(dve, S["wide_lo_done"], BLK * b + m - 1)
                        nc.vector.tensor_tensor(wide[m % 2][:], ps_turn[:, m % 2], gate[m % 2][:], ALU.mult
                                                ).then_inc(S["wide_done"], 1)
                    dve.wait_ge(S["wide_hi_done"], BLK * b + m + 1)
                    after(dve, S["down_mm"], BLK * b + m - 1)
                    nc.vector.tensor_tensor(wide_lo[m % 2][:], wide[m % 2][:], wide_hi[m % 2][:].bitcast(F32),
                                            ALU.subtract).then_inc(S["wide_lo_done"], 1)
                dve.wait_ge(S["down_mm"], BLK * b + BLK)
                for t in range(ST):
                    if gated:
                        dve.wait_ge(S["silu_done"], ST * b + t + 1)
                        nc.vector.tensor_tensor(product[:], ps_out[:, t], ffn[:], ALU.mult).then_inc(S["times_done"], 1)
                        dve.wait_ge(S["times_done"], ST * b + t + 1)
                        dve.wait_ge(S["kept_loaded"], 16 * (ST * b + ST))
                        nc.vector.tensor_tensor(x_rows[:, t], x_rows[:, t], product[:], ALU.add
                                                ).then_inc(S["plus_done"], 1)
                        dve.wait_ge(S["plus_done"], ST * b + t + 1)
                    else:
                        after(dve, S["stored"], 16 * b)
                        nc.vector.tensor_tensor(result[:, t], ps_out[:, t], b2[:], ALU.add
                                                ).then_inc(S["result_done"], 1)

            if gated:
                product = keep["product"]
            else:
                dve.wait_ge(S["consts_loaded"], 32)
            sequence(0, True)
            with dve.Fori(1, B) as b:
                sequence(b)

        @block.tensor
        def _(pe):
            def up(b, m):
                g, j = divmod(m, GROUP)
                if isinstance(b, int) and b == 0 and j % HALF_G == 0:
                    pe.wait_ge(S["w_lo_done"], 4 * g + j // HALF_G + 1)
                after(pe, S["gate_done" if gated else "wide_done"], BLK * b + m - 1)
                for k in range(KC):
                    hi, lo = (w[:, g, k, j * P:(j + 1) * P] for w in (up_hi, up_lo))
                    out = ps_up[:, m % 2]
                    nc.tensor.matmul(out, hi, xt_hi[:, k], start=k == 0, stop=False)
                    nc.tensor.matmul(out, hi, xt_lo[:, k], start=False, stop=False)
                    last = nc.tensor.matmul(out, lo, xt_hi[:, k], start=False, stop=k == KC - 1)
                last.then_inc(S["up_mm"], 1)
                if gated:
                    if j == 0:
                        pe.wait_ge(o_gathered[g % 2], 16 * ST * ((GROUPS // 2) * b + g // 2 + 1))
                    pe.wait_ge(S["x_lo_done"], KC * b + KC)
                    after(pe, S["wide_done"], BLK * b + m - 1)
                    for t in range(ST):
                        last = nc.tensor.transpose(ps_turn[:, m % 2, t * P:(t + 1) * P],
                                                   o_rows[g % 2][:, t, j * P:(j + 1) * P], ident[:])
                    last.then_inc(S["o_turned"], 1)

            def down(b, m):
                g, j = divmod(m, GROUP)
                if isinstance(b, int) and b == 0 and j % HALF_G == 0:
                    pe.wait_ge(S["w_lo_done"], 4 * g + 2 + j // HALF_G + 1)
                pe.wait_ge(S["wide_hi_done"], BLK * b + m + 1)
                pe.wait_ge(S["wide_lo_done"], BLK * b + m + 1)
                if m == 0:
                    after(pe, S["times_done" if gated else "result_done"], ST * b)
                for t in range(ST):
                    cols = slice(t * P, (t + 1) * P)
                    hi, lo = wide_hi[m % 2][:, cols], wide_lo[m % 2][:, cols]
                    nc.tensor.matmul(ps_out[:, t], hi, down_hi[:, g, j], start=m == 0, stop=False)
                    nc.tensor.matmul(ps_out[:, t], hi, down_lo[:, g, j], start=False, stop=False)
                    last = nc.tensor.matmul(ps_out[:, t], lo, down_hi[:, g, j], start=False, stop=m == BLK - 1)
                last.then_inc(S["down_mm"], 1)

            def sequence(b):
                pe.wait_ge(S["x_gathered"], 16 * (ST * b + ST))
                if gated:
                    after(pe, S["wide_done"], BLK * b)
                for k in range(KC):
                    after(pe, S["x_lo_done"], KC * b + k - 1)
                    for t in range(ST):
                        last = nc.tensor.transpose(ps_turn[:, k % 2, t * P:(t + 1) * P],
                                                   x_rows[:, t, k * P:(k + 1) * P], ident[:])
                    last.then_inc(S["x_turned"], 1)
                pe.wait_ge(S["x_hi_done"], KC * b + KC)
                pe.wait_ge(S["x_lo_done"], KC * b + KC)
                for m in range(BLK):
                    up(b, m)
                    if m:
                        down(b, m - 1)
                down(b, BLK - 1)

            peeled(pe, 1, B, sequence)


ARGUMENTS = {
    "x": "L0_attn_hidden_states", "wq": "L0_attn_Wq", "wk": "L0_attn_Wk", "wv": "L0_attn_Wv",
    "wb": "L0_attn_Wb", "bb": "L0_attn_bb", "wg": "L0_attn_Wg", "wo": "L0_attn_Wo",
    "qconv_w": "L0_attn_qconv_w", "qconv_b": "L0_attn_qconv_b",
    "kconv_w": "L0_attn_kconv_w", "kconv_b": "L0_attn_kconv_b",
    "qn_w": "L0_attn_qn_w", "qn_b": "L0_attn_qn_b", "kn_w": "L0_attn_kn_w", "kn_b": "L0_attn_kn_b",
    "w_r": "L0_ffn_w_r", "b_r": "L0_ffn_b_r", "w1": "L0_ffn_w1", "b1": "L0_ffn_b1",
    "w2": "L0_ffn_w2", "b2": "L0_ffn_b2",
}


def build(nc, a):
    s = Shapes(a["x"], a["wq"], a["wb"], a["qn_w"], a["w1"])

    def dram(name, shape, dt=F32):
        return nc.dram_tensor("scratch_" + name, shape, dt).ap()

    scratch = {
        "xn": dram("xn", [s.B * s.L, s.D]),
        "xt_hi": dram("xt_hi", [s.B, P, s.KC, s.L]),
        "xt_lo": dram("xt_lo", [s.B, P, s.KC, s.L]),
        "score": dram("score", [s.B, s.L]),
        "decay": dram("decay", [s.N, s.L]),
        "cum": dram("cum", [s.N, s.L]),
        "o": dram("o", [s.L, s.B * s.HD]),
        "ids": dram("ids", [s.B * s.L, 1], I32),
        "ffn": dram("ffn", [s.B * s.SEL, s.D]),
    }
    with ExitStack() as ctx:
        keep = {
            "ident": ctx.enter_context(nc.sbuf_tensor("ident", [P, P], F32)),
            "beta_steps": ctx.enter_context(nc.sbuf_tensor("beta_steps", [P, s.NC, s.N], F32)),
            "seq_shift": ctx.enter_context(nc.sbuf_tensor("seq_shift", [P, s.B], F32)),
            "product": ctx.enter_context(nc.sbuf_tensor("product", [P, s.D], F32)),
            "carrier_dve": ctx.enter_context(nc.semaphore("carrier_dve")),
            "carrier_pe": ctx.enter_context(nc.semaphore("carrier_pe")),
            "carrier_sp": ctx.enter_context(nc.semaphore("carrier_sp")),
            "carrier_pool": ctx.enter_context(nc.semaphore("carrier_pool")),
            "out_copied": ctx.enter_context(nc.semaphore("out_copied")),
        }
        stage_tokens(nc, s, a, scratch, keep)
        stage_recurrence(nc, s, a, scratch, keep)
        stage_kept_tokens(nc, s, a, scratch, keep, gated=False)
        stage_kept_tokens(nc, s, a, scratch, keep, gated=True)


def kernel(**inputs):
    import concourse.bacc as bacc
    from concourse.bass_utils import run_bass_kernel_spmd

    nc = bacc.Bacc("TRN2", target_bir_lowering=False, num_devices=1)
    arrays, a = {}, {}
    for name, given in ARGUMENTS.items():
        array = np.ascontiguousarray(inputs[given])
        if array.ndim == 0:
            array = array.reshape(1)
        arrays["in_" + name] = array
        a[name] = nc.dram_tensor("in_" + name, array.shape, mybir.dt.from_np(array.dtype), kind="ExternalInput").ap()
    x = inputs["L0_attn_hidden_states"]
    a["out"] = nc.dram_tensor("out", x.shape, F32, kind="ExternalOutput").ap()
    build(nc, a)
    result = run_bass_kernel_spmd(nc, [arrays], core_ids=[0])
    return result.results[0]["out"]
```

```python
from contextlib import ExitStack

import numpy as np

import concourse.bass as bass
from concourse import mybir

ALU = mybir.AluOpType
ACT = mybir.ActivationFunctionType
F32 = mybir.dt.float32
F32R = mybir.dt.float32r
I32 = mybir.dt.int32
P = 128
EPS = 1e-5
BANK = 512


class Shapes:

    def __init__(self, x, wq, wb, qn_w, w1):
        self.B, self.L, self.D = x.shape
        self.H = wb.shape[1]
        self.DK = qn_w.shape[0]
        self.HD = wq.shape[1]
        self.F = w1.shape[1]
        self.KC = self.D // P
        self.NC = self.L // P
        self.HALVES = self.L // BANK
        self.SEL = self.L // 2
        self.ST = self.SEL // P
        self.N = self.B * self.H
        self.BLK = self.F // P
        self.PAIRS_PER_SEQ = self.H // 2
        assert self.DK == P and self.HD == self.H * P and self.F == self.HD
        assert self.KC == self.ST and self.D == BANK and self.SEL == BANK and self.HALVES == 2


def after(eng, sem, n):
    if isinstance(n, int) and n <= 0:
        return
    eng.wait_ge(sem, n)


def stand(eng, carrier):
    eng.sem_inc(carrier, 1)


def peeled(eng, first, count, body):
    for n in range(first):
        body(n)
    with eng.Fori(first, count) as n:
        body(n)


def row(ap, n):
    return ap[n] if isinstance(n, int) else ap[bass.ds(n, 1)].squeeze(0)


def stage_tokens(nc, s, a, scratch, keep):
    B, L, D, H, KC, NC = s.B, s.L, s.D, s.H, s.KC, s.NC
    ROUTER = 32
    with ExitStack() as ctx:
        def sb(name, shape, dt=F32):
            return ctx.enter_context(nc.sbuf_tensor("tk_" + name, shape, dt))

        def two(name, shape, dt=F32):
            return [sb(f"{name}{i}", shape, dt) for i in range(2)]

        def sem(name):
            return ctx.enter_context(nc.semaphore("tk_" + name))

        xt_hi, xt_lo = keep["xt_hi"], keep["xt_lo"]
        x_in = two("x_in", [P, NC, D])
        xn = sb("xn", [P, NC, D])
        stats = sb("stats", [P, NC, 6])
        mean_var = two("mean_var", [P, NC, 2])
        var_eps = two("var_eps", [P, NC])
        rstd = two("rstd", [P, NC])
        shift = two("shift", [P, NC])
        minus_half = sb("minus_half", [P, NC])
        w_raw = sb("w_raw", [P, KC, ROUTER + 1])
        w_hi = sb("w_hi", [P, KC, P], F32R)
        w_lo = sb("w_lo", [P, KC, P], F32R)
        bias = sb("bias", [ROUTER + 1, 1])
        beta = sb("beta", [H, L])
        score = sb("score", [ROUTER + 1, L])
        one_minus = sb("one_minus", [H, L])
        inside = sb("inside", [H, L])
        decay = sb("decay", [H, L])
        restart = sb("restart", [H, L])
        cum = sb("cum", [H, L])
        ps_t = ctx.enter_context(nc.psum_tensor("tk_ps_t", [P, 2, L], F32))
        ps_gate = ctx.enter_context(nc.psum_tensor("tk_ps_gate", [P, L], F32))
        ps_tok = ctx.enter_context(nc.psum_tensor("tk_ps_tok", [P, NC, H], F32))

        names = """consts_loaded consts_set w_split hi_stored lo_stored score_stored decay_stored cum_stored
            stats_done mean_done var_done rstd_done shift_done xn_done score_done t_done hi_done lo_done gate_mm
            beta_done tok_mm tok_done one_minus_done decay_done restart_done cum_done"""
        S = {n: sem(n) for n in names.split()}
        x_loaded = [sem(f"x_loaded{i}") for i in range(2)]

        x_rows = a["x"].rearrange("b (c p) d -> b p c d", p=P)
        decay_rows = scratch["decay"].rearrange("(b h) t -> b h t", h=H)
        cum_rows = scratch["cum"].rearrange("(b h) t -> b h t", h=H)
        sequences = [(n, B - 1 - n, n % 2) for n in range(B)]

        block = ctx.enter_context(nc.Block())

        @block.sync
        def _(sp):
            with nc.allow_non_contiguous_dma("small constants"):
                sp.dma_start(x_in[0][:], x_rows[B - 1]).then_inc(x_loaded[0], 16)
                sp.dma_start(w_raw[:, :, 0:H], a["wb"].rearrange("(k p) h -> p k h", p=P)).then_inc(S["consts_loaded"], 16)
                sp.dma_start(w_raw[:, :, ROUTER:ROUTER + 1], a["w_r"].rearrange("(k p o) -> p k o", p=P, o=1)
                             ).then_inc(S["consts_loaded"], 16)
                sp.dma_start(bias[0:H], a["bb"].rearrange("(h o) -> h o", o=1)).then_inc(S["consts_loaded"], 16)
                sp.dma_start(bias[ROUTER:ROUTER + 1], a["b_r"].rearrange("(h o) -> h o", o=1)
                             ).then_inc(S["consts_loaded"], 16)
                sp.dma_start(x_in[1][:], x_rows[B - 2]).then_inc(x_loaded[1], 16)
            for n, b, par in sequences:
                if b > 0:
                    sp.wait_ge(S["hi_done"], KC * n + KC)
                    sp.dma_start(scratch["xt_hi"][b], xt_hi[:].bitcast(F32)).then_inc(S["hi_stored"], 16)
                    sp.wait_ge(S["lo_done"], KC * n + KC)
                    sp.dma_start(scratch["xt_lo"][b], xt_lo[:].bitcast(F32)).then_inc(S["lo_stored"], 16)
                if b > 1:
                    sp.wait_ge(S["xn_done"], n + 1)
                    sp.dma_start(x_in[par][:], x_rows[b - 2]).then_inc(x_loaded[par], 16)
                sp.wait_ge(S["score_done"], n + 1)
                sp.dma_start(scratch["score"][b:b + 1, :], score[ROUTER:ROUTER + 1]).then_inc(S["score_stored"], 16)
                sp.wait_ge(S["decay_done"], n + 1)
                sp.dma_start(decay_rows[b], decay[:]).then_inc(S["decay_stored"], 16)
                sp.wait_ge(S["cum_done"], n + 1)
                sp.dma_start(cum_rows[b], cum[:]).then_inc(S["cum_stored"], 16)
            for stored in ("score_stored", "decay_stored", "cum_stored"):
                sp.wait_ge(S[stored], 16 * B)
            for stored in ("hi_stored", "lo_stored"):
                sp.wait_ge(S[stored], 16 * (B - 1))

        @block.gpsimd
        def _(pool):
            nc.gpsimd.memset(minus_half[:], -0.5).then_inc(S["consts_set"], 1)
            nc.gpsimd.memset(w_hi[:].bitcast(F32), 0.0).then_inc(S["consts_set"], 1)
            nc.gpsimd.memset(w_lo[:].bitcast(F32), 0.0).then_inc(S["consts_set"], 1)
            nc.gpsimd.memset(keep["ident"][:], 0.0).then_inc(S["consts_set"], 1)
            nc.gpsimd.memset(inside[:], 1.0).then_inc(S["consts_set"], 1)
            pool.wait_ge(S["consts_set"], 5)
            nc.gpsimd.affine_select(out=keep["ident"][:], in_=keep["ident"][:], compare_op=ALU.not_equal,
                                    fill=1.0, base=0, pattern=[[-1, P]], channel_multiplier=1
                                    ).then_inc(S["consts_set"], 1)
            nc.gpsimd.memset(inside[:].rearrange("h (c t) -> h c t", t=P)[:, :, 0:1], 0.0).then_inc(S["consts_set"], 1)
            for n, b, par in sequences:
                pool.wait_ge(S["var_done"], n + 1)
                nc.gpsimd.tensor_tensor(rstd[par][:], var_eps[par][:], minus_half[:], ALU.pow).then_inc(S["rstd_done"], 1)

        @block.scalar
        def _(act):
            act.wait_ge(S["consts_loaded"], 64)
            act.wait_ge(S["consts_set"], 3)
            nc.scalar.activation(w_hi[:, :, 0:H], w_raw[:, :, 0:H], ACT.Copy).then_inc(S["w_split"], 1)
            nc.scalar.activation(w_hi[:, :, ROUTER:ROUTER + 1], w_raw[:, :, ROUTER:ROUTER + 1], ACT.Copy
                                 ).then_inc(S["w_split"], 1)

            def normalise(n, par):
                act.wait_ge(S["shift_done"], n + 1)
                act.wait_ge(S["rstd_done"], n + 1)
                after(act, S["t_done"], KC * n)
                for c in range(NC):
                    last = nc.scalar.activation(xn[:, c], x_in[par][:, c], ACT.Identity,
                                                bias=shift[par][:, c:c + 1], scale=rstd[par][:, c:c + 1])
                last.then_inc(S["xn_done"], 1)

            normalise(0, 0)
            for n, b, par in sequences:
                after(act, S["hi_stored"], 16 * n)
                for k in range(KC):
                    act.wait_ge(S["t_done"], KC * n + k + 1)
                    nc.scalar.activation(xt_hi[:, k], ps_t[:, k % 2], ACT.Copy).then_inc(S["hi_done"], 1)
                if n + 1 < B:
                    normalise(n + 1, 1 - par)
                act.wait_ge(S["gate_mm"], n + 1)
                after(act, S["tok_mm"], n)
                after(act, S["one_minus_done"], n)
                nc.scalar.activation(beta[:], ps_gate[0:H], ACT.Sigmoid, bias=bias[0:H]).then_inc(S["beta_done"], 1)
                after(act, S["score_stored"], 16 * n)
                nc.scalar.activation(score[ROUTER:ROUTER + 1], ps_gate[ROUTER:ROUTER + 1], ACT.Identity,
                                     bias=bias[ROUTER:ROUTER + 1]).then_inc(S["score_done"], 1)

        @block.vector
        def _(dve):
            def statistics(n, par):
                dve.wait_ge(x_loaded[par], 16 * (n // 2) + 16)
                after(dve, S["mean_done"], n)
                for c in range(NC):
                    last = nc.vector.bn_stats(stats[:, c], x_in[par][:, c])
                last.then_inc(S["stats_done"], 1)
                dve.wait_ge(S["stats_done"], n + 1)
                for c in range(NC):
                    last = nc.vector.bn_aggr(mean_var[par][:, c], stats[:, c])
                last.then_inc(S["mean_done"], 1)
                dve.wait_ge(S["mean_done"], n + 1)
                nc.vector.tensor_scalar(var_eps[par][:], mean_var[par][:, :, 1], EPS, None, ALU.add
                                        ).then_inc(S["var_done"], 1)

            def shifts(n, par):
                dve.wait_ge(S["rstd_done"], n + 1)
                after(dve, S["xn_done"], n - 1)
                nc.vector.scalar_tensor_tensor(out=shift[par][:], in0=mean_var[par][:, :, 0], scalar=-1.0,
                                               in1=rstd[par][:], op0=ALU.mult, op1=ALU.mult
                                               ).then_inc(S["shift_done"], 1)

            statistics(0, 0)
            shifts(0, 0)
            dve.wait_ge(S["w_split"], 2)
            nc.vector.tensor_tensor(w_lo[:, :, 0:H], w_raw[:, :, 0:H], w_hi[:, :, 0:H].bitcast(F32), ALU.subtract
                                    ).then_inc(S["w_split"], 1)
            nc.vector.tensor_tensor(w_lo[:, :, ROUTER:ROUTER + 1], w_raw[:, :, ROUTER:ROUTER + 1],
                                    w_hi[:, :, ROUTER:ROUTER + 1].bitcast(F32), ALU.subtract
                                    ).then_inc(S["w_split"], 1)
            dve.wait_ge(S["consts_set"], 7)
            for n, b, par in sequences:
                if n + 1 < B:
                    statistics(n + 1, 1 - par)
                    shifts(n + 1, 1 - par)
                after(dve, S["lo_stored"], 16 * n)
                for k in range(KC):
                    dve.wait_ge(S["hi_done"], KC * n + k + 1)
                    nc.vector.tensor_tensor(xt_lo[:, k], ps_t[:, k % 2], xt_hi[:, k].bitcast(F32), ALU.subtract
                                            ).then_inc(S["lo_done"], 1)
                dve.wait_ge(S["beta_done"], n + 1)
                nc.vector.tensor_scalar(one_minus[:], beta[:], -1.0, 1.0, ALU.mult, ALU.add
                                        ).then_inc(S["one_minus_done"], 1)
                dve.wait_ge(S["one_minus_done"], n + 1)
                after(dve, S["decay_stored"], 16 * n)
                nc.vector.tensor_tensor(decay[:], one_minus[:], inside[:], ALU.mult).then_inc(S["decay_done"], 1)
                dve.wait_ge(S["decay_done"], n + 1)
                nc.vector.tensor_tensor(restart[:], one_minus[:], decay[:], ALU.subtract).then_inc(S["restart_done"], 1)
                dve.wait_ge(S["restart_done"], n + 1)
                after(dve, S["cum_stored"], 16 * n)
                nc.vector.tensor_tensor_scan(cum[:], decay[:], restart[:], 0.0, ALU.mult, ALU.add
                                             ).then_inc(S["cum_done"], 1)
                dve.wait_ge(S["tok_mm"], n + 1)
                nc.vector.tensor_copy(keep["beta_steps"][:, :, b * H:(b + 1) * H], ps_tok[:]).then_inc(S["tok_done"], 1)

        @block.tensor
        def _(pe):
            pe.wait_ge(S["consts_set"], 6)
            for n, b, par in sequences:
                pe.wait_ge(S["xn_done"], n + 1)
                for k in range(KC):
                    after(pe, S["lo_done"], KC * n + k - 1)
                    for c in range(NC):
                        last = nc.tensor.transpose(ps_t[:, k % 2, c * P:(c + 1) * P],
                                                   xn[:, c, k * P:(k + 1) * P], keep["ident"][:])
                    last.then_inc(S["t_done"], 1)
                pe.wait_ge(S["w_split"], 4)
                pe.wait_ge(S["hi_done"], KC * n + KC)
                pe.wait_ge(S["lo_done"], KC * n + KC)
                after(pe, S["beta_done"], n)
                after(pe, S["score_done"], n)
                for half in range(s.HALVES):
                    cols = slice(half * BANK, (half + 1) * BANK)
                    for k in range(KC):
                        nc.tensor.matmul(ps_gate[:, cols], w_hi[:, k], xt_hi[:, k, cols], start=k == 0, stop=False)
                        nc.tensor.matmul(ps_gate[:, cols], w_hi[:, k], xt_lo[:, k, cols], start=False, stop=False)
                        last = nc.tensor.matmul(ps_gate[:, cols], w_lo[:, k], xt_hi[:, k, cols],
                                                start=False, stop=k == KC - 1)
                last.then_inc(S["gate_mm"], 1)
                pe.wait_ge(S["beta_done"], n + 1)
                after(pe, S["tok_done"], n)
                for c in range(NC):
                    last = nc.tensor.transpose(ps_tok[:, c], beta[:, c * P:(c + 1) * P], keep["ident"][0:H, 0:H])
                last.then_inc(S["tok_mm"], 1)


def stage_recurrence(nc, s, a, scratch, keep):
    B, L, H, KC, NC, N = s.B, s.L, s.H, s.KC, s.NC, s.N
    TAPS = a["qconv_w"].shape[1]
    PAD = TAPS - 1
    LAG_B, LAG_C, LAG_D = 1, 2, 3
    PEELED_PAIRS = 2
    PAIRS = N // 2
    PPS = s.PAIRS_PER_SEQ
    with ExitStack() as ctx:
        def sb(name, shape, dt=F32):
            return ctx.enter_context(nc.sbuf_tensor("rc_" + name, shape, dt))

        def two(name, shape, dt=F32):
            return [sb(f"{name}{i}", shape, dt) for i in range(2)]

        def sem(name):
            return ctx.enter_context(nc.semaphore("rc_" + name))

        ident = keep["ident"]
        xt_hi, xt_lo = keep["xt_hi"], keep["xt_lo"]
        w_raw = two("w_raw", [P, 3, KC, P])
        w_hi = two("w_hi", [P, 3, KC, P], F32R)
        w_lo = two("w_lo", [P, 3, KC, P], F32R)
        conv = two("conv", [P, 2, TAPS + 1])
        norm = sb("norm", [P, 2, 2])
        raw = [sb("raw_q", [P, PAD + L]), sb("raw_k", [P, PAD + L])]
        act_cm = [sb("act_q", [P, L]), sb("act_k", [P, L])]
        tok = [sb("tok_q", [P, NC, P]), sb("tok_k", [P, NC, P])]
        v_cm = two("v_cm", [P, L])
        q_cm = two("q_cm", [P, L])
        k_cm = two("k_cm", [P, L])
        k_state = two("k_state", [P, NC, P])
        v_beta = two("v_beta", [P, NC, P])
        decay_all = two("decay_all", [P, L])
        cum_all = two("cum_all", [P, L])
        dmat = two("dmat", [P, NC, P])
        q_cum = sb("q_cum", [P, L])
        scores = sb("scores", [P, NC, P])
        states = sb("states", [P, NC - 1, P])
        o_sb = two("o_sb", [P, NC, P])
        chunk_ident = sb("chunk_ident", [P, NC, P])
        stats = sb("stats", [P, 2, NC, 6])
        small = sb("small", [P, 8, 2, NC])
        minus_half = sb("minus_half", [P, 2, NC])
        score_all = sb("score_all", [P, L])
        score_tok = sb("score_tok", [P, B * NC])
        equal = sb("equal", [P, L])
        token_row = sb("token_row", [P, L])
        token_col = sb("token_col", [P, B * NC])
        first_slot = sb("first_slot", [P, B * NC])
        greater = sb("greater", [P, 1])
        ties = sb("ties", [P, 1])
        slot = sb("slot", [P, 1], I32)
        token_id = sb("token_id", [P, 1], I32)

        ps_proj = ctx.enter_context(nc.psum_tensor("rc_ps_proj", [P, 2, L], F32))
        ps_work = ctx.enter_context(nc.psum_tensor("rc_ps_work", [P, 2, L], F32))

        names = """consts_loaded consts_set v_half w_split
            q_projected k_projected v_projected q_raw k_raw q_tap k_tap q_conv k_conv q_silu k_silu v_copied
            q_turned k_turned q_tok k_tok stats_q stats_k small_done rstd_done shift_done q_normed k_normed
            q_back k_back k_again v_turned q_ready k_ready k_state_done v_beta_done
            dmat_done scores_mm scores_done updates_mm states_done outputs_mm outputs_done q_cum_done
            score_loaded greater_done equal_done ties_done slot_done id_done scattered"""
        S = {n: sem(n) for n in names.split()}
        w_loaded = [sem(f"w_loaded{i}") for i in range(2)]
        xt_loaded = [sem(f"xt_loaded{i}") for i in range(2)]
        conv_loaded = [sem(f"conv_loaded{i}") for i in range(2)]
        decay_loaded = [sem(f"decay_loaded{i}") for i in range(2)]
        cum_loaded = [sem(f"cum_loaded{i}") for i in range(2)]
        o_stored = [sem(f"o_stored{i}") for i in range(2)]

        w_views = [a[n].rearrange("(k p) n -> p k n", p=P) for n in ("wq", "wk", "wv")]
        conv_w = [a["qconv_w"], a["kconv_w"]]
        conv_b = [a["qconv_b"].rearrange("(n o) -> n o", o=1), a["kconv_b"].rearrange("(n o) -> n o", o=1)]
        o_rows = scratch["o"].rearrange("(c p) n -> p c n", p=P)
        W_PARTS, CONV_PARTS = 3, 4

        class At:

            def __init__(self, u, par, lag=0):
                self.i = 2 * u + par - lag
                self.par = (par - lag) % 2
                self.pair = u + (par - lag) // 2
                self.live = not isinstance(self.i, int) or 0 <= self.i < N

        def after_step(eng, name, i, per=1, part=None):
            if isinstance(i, int):
                if i < 0:
                    return
                i = min(i, N - 1)
            eng.wait_ge(S[name], per * i + (per if part is None else part))

        def after_pair(eng, semaphore, pair, per=16):
            if isinstance(pair, int) and pair < 0:
                return
            eng.wait_ge(semaphore, per * pair + per)

        def steps(eng, step):
            for u in range(PEELED_PAIRS):
                for par in range(2):
                    step(u, par)
            with eng.Fori(PEELED_PAIRS, PAIRS) as u:
                for par in range(2):
                    step(u, par)
            for i in range(N, N + LAG_D):
                step(i // 2, i % 2)

        block = ctx.enter_context(nc.Block())

        @block.sync
        def _(sp):
            def load_weights(pair, head):
                for par in range(2):
                    after(sp, S["w_split"], 2 * (2 * pair + par - 1))
                    for j in range(W_PARTS):
                        sp.dma_start(w_raw[par][:, j], w_views[j][:, :, bass.ds((head + par) * P, P)]
                                     ).then_inc(w_loaded[par], 16)

            def load_constants(pair, head, seq):
                for par in range(2):
                    after(sp, S["k_conv"], PAD * (2 * pair + par - 1))
                    stand(sp, keep["carrier_sp"])
                    for j in range(2):
                        sp.dma_start(conv[par][:, j, 0:TAPS], conv_w[j][bass.ds((head + par) * P, P), :]
                                     ).then_inc(conv_loaded[par], 16)
                        sp.dma_start(conv[par][:, j, TAPS:TAPS + 1], conv_b[j][bass.ds((head + par) * P, P), :]
                                     ).then_inc(conv_loaded[par], 16)
                after(sp, S["greater_done"], pair)
                after(sp, S["equal_done"], pair)
                sp.dma_start(score_all[:], row(scratch["score"], seq).partition_broadcast(P)
                             ).then_inc(S["score_loaded"], 16)

            with nc.allow_non_contiguous_dma("per-channel constants"):
                load_weights(0, 0)
                for half in range(s.HALVES):
                    sp.sem_inc(xt_loaded[half], 32)
                for j in range(2):
                    for n, name in enumerate((("qn_w", "qn_b"), ("kn_w", "kn_b"))[j]):
                        sp.dma_start(norm[:, j, n:n + 1], a[name].rearrange("(n o) -> n o", o=1)
                                     ).then_inc(S["consts_loaded"], 16)
                sp.dma_start(score_tok[:], scratch["score"].rearrange("b (c p) -> p (b c)", p=P)
                             ).then_inc(S["consts_loaded"], 16)
                load_constants(0, 0, 0)
                with sp.Fori(0, B - 1) as b:
                    with sp.Fori(0, PPS - 1) as hp:
                        load_weights(b * PPS + hp + 1, hp * 2 + 2)
                        load_constants(b * PPS + hp + 1, hp * 2 + 2, b)
                    load_weights((b + 1) * PPS, 0)
                    for half in range(s.HALVES):
                        cols = slice(half * BANK, (half + 1) * BANK)
                        sp.wait_ge(S[("v_half", "v_projected")[half]], b * H + H)
                        for part, name in ((xt_hi, "xt_hi"), (xt_lo, "xt_lo")):
                            sp.dma_start(part[:, :, cols].bitcast(F32), row(scratch[name], b + 1)[:, :, cols]
                                         ).then_inc(xt_loaded[half], 16)
                    load_constants((b + 1) * PPS, 0, b + 1)
                with sp.Fori(0, PPS - 1) as hp:
                    load_weights((B - 1) * PPS + hp + 1, hp * 2 + 2)
                    load_constants((B - 1) * PPS + hp + 1, hp * 2 + 2, B - 1)
                sp.dma_start(a["out"].rearrange("b l d -> (b l) d"),
                             a["x"].rearrange("b l d -> (b l) d")).then_inc(keep["out_copied"], 16)

        @block.gpsimd
        def _(pool):
            nc.gpsimd.memset(minus_half[:], -0.5).then_inc(S["consts_set"], 1)
            nc.gpsimd.memset(raw[0][:, 0:PAD], 0.0).then_inc(S["consts_set"], 1)
            nc.gpsimd.memset(raw[1][:, 0:PAD], 0.0).then_inc(S["consts_set"], 1)
            for c in range(NC):
                last = nc.gpsimd.tensor_copy(chunk_ident[:, c], ident[:])
            last.then_inc(S["consts_set"], 1)
            nc.gpsimd.iota(token_row[:], pattern=[[1, L]], base=0, channel_multiplier=0,
                           allow_small_or_imprecise_dtypes=True).then_inc(S["consts_set"], 1)
            nc.gpsimd.iota(token_col[:], pattern=[[0, B], [P, NC]], base=0, channel_multiplier=1,
                           allow_small_or_imprecise_dtypes=True).then_inc(S["consts_set"], 1)
            nc.gpsimd.iota(first_slot[:], pattern=[[L, B], [0, NC]], base=0, channel_multiplier=0,
                           allow_small_or_imprecise_dtypes=True).then_inc(S["consts_set"], 1)

            def split(i, par, pair):
                after_pair(pool, w_loaded[par], pair, 16 * W_PARTS)
                after_step(pool, "v_projected", i - 2)
                stand(pool, keep["carrier_pool"])
                nc.gpsimd.tensor_copy(w_hi[par][:], w_raw[par][:]).then_inc(S["w_split"], 1)
                pool.wait_ge(S["w_split"], 2 * i + 1)
                nc.gpsimd.tensor_tensor(w_lo[par][:], w_raw[par][:], w_hi[par][:].bitcast(F32), ALU.subtract
                                        ).then_inc(S["w_split"], 1)

            def step(u, par):
                B_, D_, nxt = At(u, par, LAG_B), At(u, par, LAG_D), At(u, par, -1)
                if D_.live:
                    after_step(pool, "q_ready", D_.i)
                    after_pair(pool, cum_loaded[D_.par], D_.pair)
                    after_step(pool, "outputs_mm", D_.i - 1)
                    nc.gpsimd.tensor_tensor(q_cum[:], q_cm[D_.par][:], cum_all[D_.par][:], ALU.mult
                                            ).then_inc(S["q_cum_done"], 1)
                if B_.live:
                    after_step(pool, "small_done", B_.i, 6)
                    nc.gpsimd.tensor_tensor(small[:, 6], small[:, 5], minus_half[:], ALU.pow
                                            ).then_inc(S["rstd_done"], 1)
                if isinstance(nxt.i, int) and nxt.i >= N:
                    return
                split(nxt.i, nxt.par, nxt.pair)

            split(0, 0, 0)

            def pair_steps(u):
                step(u, 0)
                step(u, 1)
                scatter(u)

            def scatter(u):
                pool.wait_ge(S["slot_done"], u + 1)
                pool.wait_ge(S["id_done"], u + 1)
                stand(pool, keep["carrier_pool"])
                nc.gpsimd.indirect_dma_start(
                    out=scratch["ids"], out_offset=bass.IndirectOffsetOnAxis(ap=slot[:, 0:1], axis=0),
                    in_=token_id[:, 0:1], in_offset=None).then_inc(S["scattered"], 16)

            for u in range(PEELED_PAIRS):
                pair_steps(u)
            with pool.Fori(PEELED_PAIRS, PAIRS - 1) as u:
                pair_steps(u)
            pair_steps(PAIRS - 1)
            for i in range(N, N + LAG_D):
                step(i // 2, i % 2)
            pool.wait_ge(S["scattered"], 16 * PAIRS)

        @block.scalar
        def _(act):
            act.wait_ge(S["consts_loaded"], 16 * 5)
            act.wait_ge(S["consts_set"], 7)

            def load_decay(par, i, pair):
                after_step(act, "dmat_done", i - 2)
                act.dma_start(decay_all[par][:], row(scratch["decay"], i).partition_broadcast(P)
                              ).then_inc(decay_loaded[par], 16)

            def load_cum(par, i, pair):
                after_step(act, "states_done", i - 2, NC - 1)
                after_step(act, "q_cum_done", i - 2)
                act.dma_start(cum_all[par][:], row(scratch["cum"], i).partition_broadcast(P)
                              ).then_inc(cum_loaded[par], 16)

            def step(u, par):
                A_, B_, C_, D_ = (At(u, par, lag) for lag in (0, LAG_B, LAG_C, LAG_D))
                proj_of = lambda pos: ps_proj[:, (par + pos) % 2]

                def ready(j, name_in, name_out, out):
                    after_step(act, name_in, C_.i)
                    after_step(act, "scores_mm", C_.i - 2)
                    if j == 0:
                        after_step(act, "q_cum_done", C_.i - 2)
                    else:
                        after_step(act, "k_again", C_.i - 2)
                    nc.scalar.activation(out[:], work(par, j), ACT.Identity,
                                         bias=norm[:, j, 1:2], scale=norm[:, j, 0:1]).then_inc(S[name_out], 1)

                def own_raw(j):
                    n = "qk"[j]
                    after_step(act, n + "_projected", A_.i)
                    after_step(act, n + "_conv", A_.i - 1, PAD)
                    nc.scalar.activation(raw[j][:, PAD:], proj_of(j), ACT.Copy).then_inc(S[n + "_raw"], 1)

                def tap(j):
                    n = "qk"[j]
                    if j == 0:
                        after_pair(act, conv_loaded[par], A_.pair, 16 * CONV_PARTS)
                    after_step(act, n + "_turned", A_.i - 1)
                    nc.scalar.activation(act_cm[j][:], proj_of(j), ACT.Identity,
                                         bias=conv[par][:, j, TAPS:TAPS + 1],
                                         scale=conv[par][:, j, PAD:TAPS]).then_inc(S[n + "_tap"], 1)

                def tokens(j):
                    n = "qk"[j]
                    after_step(act, n + "_turned", B_.i)
                    after_step(act, n + "_back", B_.i - 1)
                    nc.scalar.activation(tok[j][:], work(par, 2 + j), ACT.Copy).then_inc(S[n + "_tok"], 1)

                def silu(j):
                    n = "qk"[j]
                    after_step(act, n + "_conv", B_.i, PAD)
                    nc.scalar.activation(act_cm[j][:], act_cm[j][:], ACT.Silu).then_inc(S[n + "_silu"], 1)

                if C_.live:
                    ready(0, "q_back", "q_ready", q_cm[C_.par])
                if B_.live:
                    silu(0)
                if A_.live:
                    own_raw(0)
                if C_.live:
                    ready(1, "k_back", "k_ready", k_cm[C_.par])
                if B_.live:
                    silu(1)
                    tokens(0)
                if A_.live:
                    tap(0)
                if B_.live:
                    tokens(1)
                if A_.live:
                    own_raw(1)
                    tap(1)
                if B_.live:
                    load_decay(B_.par, B_.i, B_.pair)
                if C_.live:
                    load_cum(C_.par, C_.i, C_.pair)
                if A_.live:
                    after_step(act, "v_projected", A_.i)
                    after_step(act, "v_turned", A_.i - 2)
                    nc.scalar.activation(v_cm[par][:], proj_of(2), ACT.Copy).then_inc(S["v_copied"], 1)
                if D_.live:
                    after_step(act, "outputs_mm", D_.i)
                    after_pair(act, o_stored[D_.par], D_.pair - 1)
                    nc.scalar.activation(o_sb[D_.par][:], work(par, 8), ACT.Copy).then_inc(S["outputs_done"], 1)
                    after_step(act, "outputs_done", D_.i)
                    act.dma_start(o_rows[:, :, bass.ds(D_.i * P, P)], o_sb[D_.par][:]).then_inc(o_stored[D_.par], 16)

            def work(par, pos):
                return ps_work[:, (par + pos) % 2]

            steps(act, step)
            for par in range(2):
                act.wait_ge(o_stored[par], 16 * PAIRS)

        @block.vector
        def _(dve):
            dve.wait_ge(S["consts_loaded"], 16 * 5)
            dve.wait_ge(S["consts_set"], 7)

            def work(par, pos):
                return ps_work[:, (par + pos) % 2]

            def chunks(ap):
                return ap.rearrange("p (c t) -> p c t", t=P)

            def step(u, par):
                A_, B_, C_, D_ = (At(u, par, lag) for lag in (0, LAG_B, LAG_C, LAG_D))

                def convolve(j):
                    n = "qk"[j]
                    after_step(dve, n + "_raw", B_.i)
                    after_step(dve, n + "_tap", B_.i)
                    for t in range(PAD):
                        if t:
                            after_step(dve, n + "_conv", B_.i, PAD, t)
                        nc.vector.scalar_tensor_tensor(out=act_cm[j][:], in0=raw[j][:, t:t + L],
                                                       scalar=conv[B_.par][:, j, t:t + 1], in1=act_cm[j][:],
                                                       op0=ALU.mult, op1=ALU.add).then_inc(S[n + "_conv"], 1)

                def statistics(j):
                    n = "qk"[j]
                    after_step(dve, n + "_tok", B_.i)
                    for c in range(NC):
                        last = nc.vector.bn_stats(stats[:, j, c], tok[j][:, c])
                    last.then_inc(S["stats_" + n], 1)

                def variance():
                    m_even, q_even, m_odd, q_odd = (stats[:, :, :, n] for n in (1, 2, 4, 5))
                    after_step(dve, "stats_q", B_.i)
                    after_step(dve, "stats_k", B_.i)
                    after_step(dve, "shift_done", B_.i - 1)
                    after_step(dve, "k_normed", B_.i - 1)
                    done = lambda part: after_step(dve, "small_done", B_.i, 6, part)
                    inc = lambda ins: ins.then_inc(S["small_done"], 1)
                    inc(nc.vector.tensor_tensor(small[:, 0], m_even, m_odd, ALU.add))
                    inc(nc.vector.tensor_tensor(small[:, 1], m_even, m_odd, ALU.subtract))
                    inc(nc.vector.tensor_tensor(small[:, 2], q_even, q_odd, ALU.add))
                    done(2)
                    inc(nc.vector.tensor_tensor(small[:, 3], small[:, 1], small[:, 1], ALU.mult))
                    done(3)
                    inc(nc.vector.tensor_scalar(small[:, 4], small[:, 2], 1.0 / P, EPS, ALU.mult, ALU.add))
                    done(5)
                    inc(nc.vector.scalar_tensor_tensor(out=small[:, 5], in0=small[:, 3], scalar=0.25,
                                                       in1=small[:, 4], op0=ALU.mult, op1=ALU.add))

                def normalise():
                    after_step(dve, "rstd_done", B_.i)
                    nc.vector.scalar_tensor_tensor(out=small[:, 7], in0=small[:, 0], scalar=-0.5, in1=small[:, 6],
                                                   op0=ALU.mult, op1=ALU.mult).then_inc(S["shift_done"], 1)
                    after_step(dve, "shift_done", B_.i)
                    for j in range(2):
                        for c in range(NC):
                            last = nc.vector.tensor_scalar(tok[j][:, c], tok[j][:, c], small[:, 6, j, c:c + 1],
                                                           small[:, 7, j, c:c + 1], ALU.mult, ALU.add)
                        last.then_inc(S["qk"[j] + "_normed"], 1)

                if B_.live:
                    convolve(0)
                    convolve(1)
                if C_.live:
                    after_pair(dve, decay_loaded[C_.par], C_.pair)
                    after_step(dve, "scores_done", C_.i - 2)
                    nc.vector.tensor_tensor_scan(dmat[C_.par][:].rearrange("p c t -> p (c t)"), decay_all[C_.par][:],
                                                 chunk_ident[:].rearrange("p c t -> p (c t)"), 0.0,
                                                 ALU.mult, ALU.add).then_inc(S["dmat_done"], 1)
                if B_.live:
                    statistics(0)
                    statistics(1)
                if D_.live:
                    after_step(dve, "scores_mm", D_.i)
                    after_step(dve, "outputs_mm", D_.i - 1)
                    nc.vector.tensor_tensor(scores[:], chunks(work(par, 4)), dmat[D_.par][:], ALU.mult
                                            ).then_inc(S["scores_done"], 1)
                if B_.live:
                    variance()
                if C_.live:
                    after_step(dve, "k_again", C_.i)
                    after_step(dve, "dmat_done", C_.i)
                    after_step(dve, "updates_mm", C_.i - 2)
                    nc.vector.tensor_tensor(k_state[C_.par][:], chunks(work(par, 5)),
                                            dmat[C_.par][:, :, P - 1:P].to_broadcast([P, NC, P]), ALU.mult
                                            ).then_inc(S["k_state_done"], 1)
                if D_.live:
                    after_step(dve, "updates_mm", D_.i)
                    after_step(dve, "outputs_mm", D_.i - 1)
                    after_pair(dve, cum_loaded[D_.par], D_.pair)
                    updates = chunks(work(par, 6))
                    nc.vector.tensor_copy(states[:, 0], updates[:, 0]).then_inc(S["states_done"], 1)
                    for c in range(1, NC - 1):
                        after_step(dve, "states_done", D_.i, NC - 1, c)
                        last_token = c * P + P - 1
                        nc.vector.scalar_tensor_tensor(out=states[:, c], in0=states[:, c - 1],
                                                       scalar=cum_all[D_.par][:, last_token:last_token + 1],
                                                       in1=updates[:, c], op0=ALU.mult, op1=ALU.add
                                                       ).then_inc(S["states_done"], 1)
                if B_.live:
                    normalise()
                if C_.live:
                    after_step(dve, "v_turned", C_.i)
                    after_step(dve, "outputs_mm", C_.i - 2)
                    after_step(dve, "updates_mm", C_.i - 2)
                    gate = keep["beta_steps"][:, :, bass.ds(C_.i, 1)].to_broadcast([P, NC, P])
                    nc.vector.tensor_tensor(v_beta[C_.par][:], chunks(work(par, 7)), gate, ALU.mult
                                            ).then_inc(S["v_beta_done"], 1)
                if A_.live and par == 1:
                    ranks(u)

            def ranks(u):
                dve.wait_ge(S["score_loaded"], 16 * u + 16)
                own = score_tok[:, bass.ds(u, 1)]
                after(dve, S["slot_done"], u)
                nc.vector.tensor_scalar(equal[:], score_all[:], own, None, ALU.is_gt, ALU.add, accum_out=greater[:]
                                        ).then_inc(S["greater_done"], 1)
                dve.wait_ge(S["greater_done"], u + 1)
                after(dve, S["ties_done"], u)
                nc.vector.tensor_scalar(equal[:], score_all[:], own, None, ALU.is_equal).then_inc(S["equal_done"], 1)
                dve.wait_ge(S["equal_done"], u + 1)
                nc.vector.scalar_tensor_tensor(out=equal[:], in0=token_row[:], scalar=token_col[:, bass.ds(u, 1)],
                                               in1=equal[:], op0=ALU.is_lt, op1=ALU.mult, accum_out=ties[:]
                                               ).then_inc(S["ties_done"], 1)
                dve.wait_ge(S["ties_done"], u + 1)
                after(dve, S["scattered"], 16 * u)
                nc.vector.scalar_tensor_tensor(out=slot[:], in0=greater[:], scalar=ties[:], in1=first_slot[:, bass.ds(u, 1)],
                                               op0=ALU.add, op1=ALU.add).then_inc(S["slot_done"], 1)
                nc.vector.tensor_scalar(token_id[:], token_col[:, bass.ds(u, 1)], 1.0, first_slot[:, bass.ds(u, 1)],
                                        ALU.mult, ALU.add).then_inc(S["id_done"], 1)

            steps(dve, step)

        @block.tensor
        def _(pe):
            def work(par, pos):
                return ps_work[:, (par + pos) % 2]

            def turn(out, source):
                for c in range(NC):
                    last = nc.tensor.transpose(out[:, c * P:(c + 1) * P], source(c), ident[:])
                return last

            def step(u, par):
                A_, B_, C_, D_ = (At(u, par, lag) for lag in (0, LAG_B, LAG_C, LAG_D))

                def project(pos, half):
                    if half == 0:
                        if pos == 0:
                            after_step(pe, "w_split", A_.i, 2)
                            after_step(pe, "k_tap", A_.i - 1)
                        elif pos == 1:
                            after_step(pe, "v_copied", A_.i - 1)
                        else:
                            after_step(pe, "q_tap", A_.i)
                    if pos == 0:
                        pe.wait_ge(xt_loaded[half], (A_.i // H) * 32 + 32)
                    out = ps_proj[:, (par + pos) % 2, half * BANK:(half + 1) * BANK]
                    cols = slice(half * BANK, (half + 1) * BANK)
                    for k in range(KC):
                        hi, lo = w_hi[par][:, pos, k], w_lo[par][:, pos, k]
                        nc.tensor.matmul(out, hi, xt_hi[:, k, cols], start=k == 0, stop=False)
                        nc.tensor.matmul(out, hi, xt_lo[:, k, cols], start=False, stop=False)
                        last = nc.tensor.matmul(out, lo, xt_hi[:, k, cols], start=False, stop=k == KC - 1)
                    if half == s.HALVES - 1:
                        last.then_inc(S["qkv"[pos] + "_projected"], 1)
                    elif pos == 2:
                        last.then_inc(S["v_half"], 1)

                if A_.live:
                    project(0, 0)
                if C_.live:
                    after_step(pe, "q_normed", C_.i)
                    after_step(pe, "v_beta_done", C_.i - 1)
                    turn(work(par, 0), lambda c: tok[0][:, c]).then_inc(S["q_back"], 1)
                if A_.live:
                    project(0, 1)
                if C_.live:
                    after_step(pe, "k_normed", C_.i)
                    after_step(pe, "outputs_done", D_.i - 1)
                    turn(work(par, 1), lambda c: tok[1][:, c]).then_inc(S["k_back"], 1)
                if B_.live:
                    after_step(pe, "q_silu", B_.i)
                    after_step(pe, "q_ready", C_.i)
                    turn(work(par, 2), lambda c: act_cm[0][:, c * P:(c + 1) * P]).then_inc(S["q_turned"], 1)
                if A_.live:
                    project(1, 0)
                if B_.live:
                    after_step(pe, "k_silu", B_.i)
                    after_step(pe, "k_ready", C_.i)
                    turn(work(par, 3), lambda c: act_cm[1][:, c * P:(c + 1) * P]).then_inc(S["k_turned"], 1)
                if D_.live:
                    after_step(pe, "k_ready", D_.i)
                    after_step(pe, "q_ready", D_.i)
                    after_step(pe, "q_tok", B_.i)
                    if not B_.live:
                        after_step(pe, "q_ready", C_.i)
                    if not C_.live:
                        after_step(pe, "v_beta_done", C_.i)
                    for c in range(NC):
                        t = slice(c * P, (c + 1) * P)
                        last = nc.tensor.matmul(work(par, 4)[:, t], k_cm[D_.par][:, t], q_cm[D_.par][:, t],
                                                start=True, stop=True)
                    last.then_inc(S["scores_mm"], 1)
                if A_.live:
                    project(1, 1)
                if C_.live:
                    after_step(pe, "k_ready", C_.i)
                    after_step(pe, "k_tok", B_.i)
                    turn(work(par, 5), lambda c: k_cm[C_.par][:, c * P:(c + 1) * P]).then_inc(S["k_again"], 1)
                if D_.live:
                    after_step(pe, "k_state_done", D_.i)
                    after_step(pe, "v_beta_done", D_.i)
                    after_step(pe, "scores_done", D_.i)
                    for c in range(NC - 1):
                        last = nc.tensor.matmul(work(par, 6)[:, c * P:(c + 1) * P], k_state[D_.par][:, c],
                                                v_beta[D_.par][:, c], start=True, stop=True)
                    last.then_inc(S["updates_mm"], 1)
                if A_.live:
                    project(2, 0)
                if C_.live:
                    after_step(pe, "v_copied", C_.i)
                    after_step(pe, "k_state_done", C_.i)
                    turn(work(par, 7), lambda c: v_cm[C_.par][:, c * P:(c + 1) * P]).then_inc(S["v_turned"], 1)
                if A_.live:
                    project(2, 1)
                if D_.live:
                    after_step(pe, "states_done", D_.i, NC - 1)
                    after_step(pe, "q_cum_done", D_.i)
                    after_step(pe, "scores_done", D_.i)
                    for c in range(NC):
                        out = work(par, 8)[:, c * P:(c + 1) * P]
                        last = nc.tensor.matmul(out, scores[:, c], v_beta[D_.par][:, c], start=True, stop=c == 0)
                        if c:
                            last = nc.tensor.matmul(out, q_cum[:, c * P:(c + 1) * P], states[:, c - 1],
                                                    start=False, stop=True)
                    last.then_inc(S["outputs_mm"], 1)

            pe.wait_ge(S["consts_set"], 4)
            steps(pe, step)


def stage_kept_tokens(nc, s, a, scratch, keep, gated):
    B, L, H, KC, ST, SEL, BLK, D = s.B, s.L, s.H, s.KC, s.ST, s.SEL, s.BLK, s.D
    tag = "gt_" if gated else "ff_"
    GROUP = 4
    GROUPS = BLK // GROUP
    WIDE = GROUP * P
    with ExitStack() as ctx:
        def sb(name, shape, dt=F32):
            return ctx.enter_context(nc.sbuf_tensor(tag + name, shape, dt))

        def two(name, shape, dt=F32):
            return [sb(f"{name}{i}", shape, dt) for i in range(2)]

        def sem(name):
            return ctx.enter_context(nc.semaphore(tag + name))

        ident = keep["ident"]
        up_hi = sb("up_hi", [P, GROUPS, KC, WIDE], F32R)
        up_lo = sb("up_lo", [P, GROUPS, KC, WIDE], F32R)
        down_hi = sb("down_hi", [P, GROUPS, GROUP, D], F32R)
        down_lo = sb("down_lo", [P, GROUPS, GROUP, D], F32R)
        staging = sb("staging", [P, 2, KC, WIDE // 2])
        xn_rows = sb("xn_rows", [P, ST, D])
        xt_hi = sb("xt_hi", [P, KC, SEL], F32R)
        xt_lo = sb("xt_lo", [P, KC, SEL], F32R)
        ids = sb("ids", [P, B, ST], I32)
        wide = two("wide", [P, SEL])
        wide_hi = two("wide_hi", [P, SEL], F32R)
        wide_lo = two("wide_lo", [P, SEL], F32R)
        x_rows = sb("x_rows", [P, ST, D])
        if gated:
            ids_f = sb("ids_f", [P, B, ST])
            seq_shift = sb("seq_shift", [P, B, ST])
            o_ids_f = sb("o_ids_f", [P, B, ST])
            o_ids = sb("o_ids", [P, GROUPS, B, ST], I32)
            o_rows = two("o_rows", [P, ST, WIDE])
            gate = two("gate", [P, SEL])
            ffn = staging[:].rearrange("p i k w -> p (i k w)").rearrange("p (t d) -> p t d", d=D)
        else:
            b1 = sb("b1", [P, BLK])
            b2 = sb("b2", [P, D])
            result = sb("result", [P, ST, D])
            stats = sb("stats", [P, ST, 6])
            mean_var = sb("mean_var", [P, ST, 2])
            var_eps = sb("var_eps", [P, ST])
            rstd = sb("rstd", [P, ST])
            shift = sb("shift", [P, ST])
            minus_half = sb("minus_half", [P, ST])
        ps_up = ctx.enter_context(nc.psum_tensor(tag + "ps_up", [P, 2, SEL], F32))
        ps_turn = ctx.enter_context(nc.psum_tensor(tag + "ps_turn", [P, 2, SEL], F32))
        ps_out = ctx.enter_context(nc.psum_tensor(tag + "ps_out", [P, ST, D], F32))

        names = """consts_loaded w_hi_done w_lo_done ids_loaded x_loaded xn_done x_turned x_hi_done x_lo_done
            up_mm wide_done wide_hi_done wide_lo_done down_mm stored"""
        names += """ xn_loaded seq_shift_set ids_f_done o_ids_f_done o_ids_done o_turned gate_done
            ffn_loaded silu_done times_done plus_done""" if gated else """
            consts_set x_kept xn_kept stats_done mean_done var_done rstd_done shift_done result_done"""
        S = {n: sem(n) for n in names.split()}
        w_loaded = [sem(f"w_loaded{i}") for i in range(2)]
        if gated:
            o_gathered = [sem(f"o_gathered{i}") for i in range(2)]

        up_w, down_w = (a["wg"], a["wo"]) if gated else (a["w1"], a["w2"])
        up_view = up_w.rearrange("(k p) n -> p k n", p=P)
        down_view = down_w.rearrange("(m p) n -> p m n", p=P)
        PIECES = 4 * GROUPS
        HALF_W, HALF_G = WIDE // 2, GROUP // 2
        by_rank = lambda name: scratch[name].rearrange("(b p t) d -> b p t d", p=P, t=ST)
        ffn_rows, kept_x, kept_xn = by_rank("ffn"), by_rank("kept_x"), by_rank("kept_xn")
        id_rows = scratch["ids"].rearrange("(b h p t) o -> h p b (t o)", p=P, t=ST, h=L // SEL)[0]
        STAT_M, SHIFT_M, NORM_M = 4, 6, 9
        PLUS_M, SILU_M = 2, 13

        def is_last(b):
            return isinstance(b, int) and b == B - 1

        def piece(n):
            g, part = divmod(n, 4)
            half = part % 2
            if part < 2:
                cols = slice(half * HALF_W, (half + 1) * HALF_W)
                return (up_view[:, :, g * WIDE + half * HALF_W:g * WIDE + (half + 1) * HALF_W],
                        staging[:, n % 2], up_hi[:, g, :, cols], up_lo[:, g, :, cols])
            blocks = slice(half * HALF_G, (half + 1) * HALF_G)
            staged = staging[:, n % 2].rearrange("p k w -> p (k w)").rearrange("p (m d) -> p m d", d=D)
            return (down_view[:, g * GROUP + half * HALF_G:g * GROUP + (half + 1) * HALF_G, :],
                    staged, down_hi[:, g, blocks], down_lo[:, g, blocks])

        block = ctx.enter_context(nc.Block())

        @block.sync
        def _(sp):
            with nc.allow_non_contiguous_dma("token ids and per-channel constants"):
                sp.dma_start(ids[:], id_rows).then_inc(S["ids_loaded"], 16)
                if gated:
                    sp.dma_start(xn_rows[:], kept_xn[0]).then_inc(S["xn_loaded"], 16)
                for n in range(PIECES):
                    after(sp, S["w_lo_done"], n - 1)
                    sp.dma_start(piece(n)[1], piece(n)[0]).then_inc(w_loaded[n % 2], 16)
                    if n == 1 and not gated:
                        sp.dma_start(b1[:], a["b1"].rearrange("(m p) -> p m", p=P)).then_inc(S["consts_loaded"], 16)
                        sp.dma_start(b2[:], a["b2"].partition_broadcast(P)).then_inc(S["consts_loaded"], 16)

                def sequence(b):
                    if not gated:
                        sp.wait_ge(S["result_done"], ST * b + ST)
                        sp.dma_start(row(ffn_rows, b), result[:]).then_inc(S["stored"], 16)
                        return
                    if not (isinstance(b, int) and b == 0):
                        sp.wait_ge(S["x_turned"], KC * b)
                        sp.dma_start(xn_rows[:], row(kept_xn, b)).then_inc(S["xn_loaded"], 16)
                    sp.wait_ge(S["w_lo_done"], PIECES)
                    after(sp, S["plus_done"], b)
                    sp.dma_start(ffn, row(ffn_rows, b)).then_inc(S["ffn_loaded"], 16)
                    after(sp, S["stored"], 16 * ST * b)
                    sp.dma_start(x_rows[:], row(kept_x, b)).then_inc(S["x_loaded"], 16)

                peeled(sp, 1, B, sequence)
            if not gated:
                sp.wait_ge(S["stored"], 16 * B)
                sp.wait_ge(S["x_kept"], 16 * B)
                sp.wait_ge(S["xn_kept"], 16 * B)

        @block.gpsimd
        def _(pool):
            def gather(out, source, index):
                return nc.gpsimd.indirect_dma_start(out=out, out_offset=None, in_=source,
                                                    in_offset=bass.IndirectOffsetOnAxis(ap=index, axis=0))

            if gated:
                nc.gpsimd.iota(seq_shift[:], pattern=[[-(L * B - 1) * GROUPS, B], [0, ST]], base=0,
                               channel_multiplier=0, allow_small_or_imprecise_dtypes=True
                               ).then_inc(S["seq_shift_set"], 1)
                pool.wait_ge(S["o_ids_done"], 1)
            else:
                nc.gpsimd.memset(minus_half[:], -0.5).then_inc(S["consts_set"], 1)
                pool.wait_ge(S["ids_loaded"], 16)

            def gather_x(b):
                after(pool, S["xn_done"], b)
                after(pool, S["x_kept"], 16 * b)
                for t in range(ST):
                    gather(x_rows[:, t], a["x"].rearrange("b l d -> (b l) d"), ids[:, b, t:t + 1]
                           ).then_inc(S["x_loaded"], 16)

            def rstd_of(b):
                pool.wait_ge(S["var_done"], b + 1)
                after(pool, S["xn_done"], b)
                nc.gpsimd.tensor_tensor(rstd[:], var_eps[:], minus_half[:], ALU.pow).then_inc(S["rstd_done"], 1)

            def gather_o(b, g):
                after(pool, S["o_turned"], BLK * b + GROUP * (g - 1))
                for t in range(ST):
                    gather(o_rows[g % 2][:, t], scratch["o"].rearrange("l (g w) -> (l g) w", w=WIDE),
                           o_ids[:, g, b, t:t + 1]).then_inc(o_gathered[g % 2], 16)

            def scatter(b):
                pool.wait_ge(S["plus_done"], b + 1)
                if b == 0:
                    pool.wait_ge(keep["out_copied"], 16)
                for t in range(ST):
                    nc.gpsimd.indirect_dma_start(
                        out=a["out"].rearrange("b l d -> (b l) d"),
                        out_offset=bass.IndirectOffsetOnAxis(ap=ids[:, b, t:t + 1], axis=0),
                        in_=x_rows[:, t], in_offset=None).then_inc(S["stored"], 16)

            if gated:
                for b in range(B):
                    gather_o(b, 0)
                    gather_o(b, 1)
                    if b:
                        scatter(b - 1)
                    gather_o(b, 2)
                    gather_o(b, 3)
                scatter(B - 1)
                pool.wait_ge(S["stored"], 16 * ST * B)
            else:
                pool.wait_ge(S["consts_set"], 1)
                for b in range(B):
                    gather_x(b)
                    rstd_of(b)

        @block.scalar
        def _(act):
            def split_piece(n):
                _, staged, hi, _ = piece(n)
                act.wait_ge(w_loaded[n % 2], 16 * (n // 2 + 1))
                nc.scalar.activation(hi, staged, ACT.Copy).then_inc(S["w_hi_done"], 1)

            def split_x(b):
                after(act, S["up_mm"], BLK * b)
                for k in range(KC):
                    act.wait_ge(S["x_turned"], KC * b + k + 1)
                    nc.scalar.activation(xt_hi[:, k], ps_turn[:, k % 2], ACT.Copy).then_inc(S["x_hi_done"], 1)

            def normalise(b):
                act.wait_ge(S["x_loaded"], 16 * (ST * b + ST))
                act.dma_start(row(kept_x, b), x_rows[:]).then_inc(S["x_kept"], 16)
                act.wait_ge(S["shift_done"], b + 1)
                act.wait_ge(S["rstd_done"], b + 1)
                after(act, S["x_turned"], KC * b)
                after(act, S["xn_kept"], 16 * b)
                for t in range(ST):
                    last = nc.scalar.activation(xn_rows[:, t], x_rows[:, t], ACT.Identity,
                                                bias=shift[:, t:t + 1], scale=rstd[:, t:t + 1])
                last.then_inc(S["xn_done"], 1)
                act.wait_ge(S["xn_done"], b + 1)
                act.dma_start(row(kept_xn, b), xn_rows[:]).then_inc(S["xn_kept"], 16)

            def sequence(b, pieces=False):
                split_x(b)
                for m in range(BLK):
                    if pieces and m % GROUP == 0 and m // GROUP + 1 < GROUPS:
                        for n in range(4):
                            split_piece(4 * (m // GROUP + 1) + n)
                    act.wait_ge(S["up_mm"], BLK * b + m + 1)
                    if gated:
                        after(act, S["wide_done"], BLK * b + m - 1)
                        nc.scalar.activation(gate[m % 2][:], ps_up[:, m % 2], ACT.Silu).then_inc(S["gate_done"], 1)
                    else:
                        after(act, S["wide_lo_done"], BLK * b + m - 1)
                        nc.scalar.activation(wide[m % 2][:], ps_up[:, m % 2], ACT.Gelu_apprx_tanh,
                                             bias=b1[:, m:m + 1]).then_inc(S["wide_done"], 1)
                    act.wait_ge(S["wide_done"], BLK * b + m + 1)
                    after(act, S["down_mm"], BLK * b + m - 1)
                    nc.scalar.activation(wide_hi[m % 2][:], wide[m % 2][:], ACT.Copy).then_inc(S["wide_hi_done"], 1)
                    if not gated and m == NORM_M and not is_last(b):
                        normalise(b + 1)
                    if gated and m == SILU_M:
                        act.wait_ge(S["ffn_loaded"], 16 * b + 16)
                        nc.scalar.activation(ffn, ffn, ACT.Silu).then_inc(S["silu_done"], 1)

            if not gated:
                normalise(0)
                act.wait_ge(S["consts_loaded"], 32)
            for n in range(4):
                split_piece(n)
            sequence(0, True)
            with act.Fori(1, B - 1) as b:
                sequence(b)
            sequence(B - 1)

        @block.vector
        def _(dve):
            def split_piece(n):
                _, staged, hi, lo = piece(n)
                dve.wait_ge(S["w_hi_done"], n + 1)
                nc.vector.tensor_tensor(lo, staged, hi.bitcast(F32), ALU.subtract).then_inc(S["w_lo_done"], 1)

            def o_indices():
                dve.wait_ge(S["ids_loaded"], 16)
                nc.vector.tensor_copy(ids_f[:], ids[:]).then_inc(S["ids_f_done"], 1)
                dve.wait_ge(S["ids_f_done"], 1)
                dve.wait_ge(S["seq_shift_set"], 1)
                nc.vector.scalar_tensor_tensor(out=o_ids_f[:], in0=ids_f[:], scalar=float(B * GROUPS),
                                               in1=seq_shift[:], op0=ALU.mult, op1=ALU.add
                                               ).then_inc(S["o_ids_f_done"], 1)
                dve.wait_ge(S["o_ids_f_done"], 1)
                for g in range(GROUPS):
                    last = nc.vector.tensor_scalar(o_ids[:, g], o_ids_f[:], float(g), None, ALU.add)
                last.then_inc(S["o_ids_done"], 1)

            def statistics(b):
                dve.wait_ge(S["x_loaded"], 16 * (ST * b + ST))
                stand(dve, keep["carrier_dve"])
                after(dve, S["xn_done"], b)
                stand(dve, keep["carrier_dve"])
                for t in range(ST):
                    last = nc.vector.bn_stats(stats[:, t], x_rows[:, t])
                last.then_inc(S["stats_done"], 1)
                dve.wait_ge(S["stats_done"], b + 1)
                stand(dve, keep["carrier_dve"])
                for t in range(ST):
                    last = nc.vector.bn_aggr(mean_var[:, t], stats[:, t])
                last.then_inc(S["mean_done"], 1)
                dve.wait_ge(S["mean_done"], b + 1)
                after(dve, S["rstd_done"], b)
                nc.vector.tensor_scalar(var_eps[:], mean_var[:, :, 1], EPS, None, ALU.add).then_inc(S["var_done"], 1)

            def shifts(b):
                dve.wait_ge(S["rstd_done"], b + 1)
                nc.vector.scalar_tensor_tensor(out=shift[:], in0=mean_var[:, :, 0], scalar=-1.0, in1=rstd[:],
                                               op0=ALU.mult, op1=ALU.mult).then_inc(S["shift_done"], 1)

            def finish(b):
                dve.wait_ge(S["down_mm"], BLK * b + BLK)
                if gated:
                    dve.wait_ge(S["silu_done"], b + 1)
                    for t in range(ST):
                        nc.vector.tensor_tensor(ffn[:, t], ps_out[:, t], ffn[:, t], ALU.mult
                                                ).then_inc(S["times_done"], 1)
                else:
                    after(dve, S["stored"], 16 * b)
                    for t in range(ST):
                        nc.vector.tensor_tensor(result[:, t], ps_out[:, t], b2[:], ALU.add
                                                ).then_inc(S["result_done"], 1)

            def plus(b):
                dve.wait_ge(S["times_done"], ST * b + ST)
                dve.wait_ge(S["x_loaded"], 16 * b + 16)
                nc.vector.tensor_tensor(x_rows[:], x_rows[:], ffn, ALU.add).then_inc(S["plus_done"], 1)

            def sequence(b, pieces=False):
                for k in range(KC):
                    dve.wait_ge(S["x_hi_done"], KC * b + k + 1)
                    nc.vector.tensor_tensor(xt_lo[:, k], ps_turn[:, k % 2], xt_hi[:, k].bitcast(F32), ALU.subtract
                                            ).then_inc(S["x_lo_done"], 1)
                if not pieces:
                    finish(b - 1)
                for m in range(BLK):
                    if pieces and m % GROUP == 0 and m // GROUP + 1 < GROUPS:
                        for n in range(4):
                            split_piece(4 * (m // GROUP + 1) + n)
                    if gated:
                        dve.wait_ge(S["gate_done"], BLK * b + m + 1)
                        dve.wait_ge(S["o_turned"], BLK * b + m + 1)
                        after(dve, S["wide_hi_done"], BLK * b + m - 1)
                        after(dve, S["wide_lo_done"], BLK * b + m - 1)
                        nc.vector.tensor_tensor(wide[m % 2][:], ps_turn[:, m % 2], gate[m % 2][:], ALU.mult
                                                ).then_inc(S["wide_done"], 1)
                    dve.wait_ge(S["wide_hi_done"], BLK * b + m + 1)
                    after(dve, S["down_mm"], BLK * b + m - 1)
                    nc.vector.tensor_tensor(wide_lo[m % 2][:], wide[m % 2][:], wide_hi[m % 2][:].bitcast(F32),
                                            ALU.subtract).then_inc(S["wide_lo_done"], 1)
                    if gated and m == PLUS_M and not pieces:
                        plus(b - 1)
                    if not gated and not is_last(b):
                        if m == STAT_M:
                            statistics(b + 1)
                        if m == SHIFT_M:
                            shifts(b + 1)

            if gated:
                o_indices()
            else:
                statistics(0)
                shifts(0)
                dve.wait_ge(S["consts_loaded"], 32)
            for n in range(4):
                split_piece(n)
            sequence(0, True)
            with dve.Fori(1, B - 1) as b:
                sequence(b)
            sequence(B - 1)
            finish(B - 1)
            if gated:
                plus(B - 1)

        @block.tensor
        def _(pe):
            def turn_x(b, k):
                if gated and k < 2:
                    after(pe, S["wide_done"], BLK * b + k - 1)
                else:
                    after(pe, S["x_lo_done"], KC * b + k - 1)
                for t in range(ST):
                    last = nc.tensor.transpose(ps_turn[:, k % 2, t * P:(t + 1) * P],
                                               xn_rows[:, t, k * P:(k + 1) * P], ident[:])
                last.then_inc(S["x_turned"], 1)

            def up(b, m):
                g, j = divmod(m, GROUP)
                if isinstance(b, int) and b == 0 and j % HALF_G == 0:
                    pe.wait_ge(S["w_lo_done"], 4 * g + j // HALF_G + 1)
                after(pe, S["gate_done" if gated else "wide_done"], BLK * b + m - 1)
                for k in range(KC):
                    if m == 0:
                        pe.wait_ge(S["x_hi_done"], KC * b + k + 1)
                        pe.wait_ge(S["x_lo_done"], KC * b + k + 1)
                    hi, lo = (w[:, g, k, j * P:(j + 1) * P] for w in (up_hi, up_lo))
                    out = ps_up[:, m % 2]
                    nc.tensor.matmul(out, hi, xt_hi[:, k], start=k == 0, stop=False)
                    nc.tensor.matmul(out, hi, xt_lo[:, k], start=False, stop=False)
                    last = nc.tensor.matmul(out, lo, xt_hi[:, k], start=False, stop=k == KC - 1)
                last.then_inc(S["up_mm"], 1)
                if gated:
                    if j == 0:
                        pe.wait_ge(o_gathered[g % 2], 16 * ST * ((GROUPS // 2) * b + g // 2 + 1))
                    if m < 2:
                        pe.wait_ge(S["x_lo_done"], KC * b + KC)
                    else:
                        pe.wait_ge(S["wide_done"], BLK * b + m - 1)
                    for t in range(ST):
                        last = nc.tensor.transpose(ps_turn[:, m % 2, t * P:(t + 1) * P],
                                                   o_rows[g % 2][:, t, j * P:(j + 1) * P], ident[:])
                    last.then_inc(S["o_turned"], 1)

            def down(b, m):
                g, j = divmod(m, GROUP)
                if isinstance(b, int) and b == 0 and j % HALF_G == 0:
                    pe.wait_ge(S["w_lo_done"], 4 * g + 2 + j // HALF_G + 1)
                pe.wait_ge(S["wide_hi_done"], BLK * b + m + 1)
                pe.wait_ge(S["wide_lo_done"], BLK * b + m + 1)
                for t in range(ST):
                    if m == 0:
                        after(pe, S["times_done" if gated else "result_done"], ST * (b - 1) + t + 1)
                    cols = slice(t * P, (t + 1) * P)
                    hi, lo = wide_hi[m % 2][:, cols], wide_lo[m % 2][:, cols]
                    nc.tensor.matmul(ps_out[:, t], hi, down_hi[:, g, j], start=m == 0, stop=False)
                    nc.tensor.matmul(ps_out[:, t], hi, down_lo[:, g, j], start=False, stop=False)
                    last = nc.tensor.matmul(ps_out[:, t], lo, down_hi[:, g, j], start=False, stop=m == BLK - 1)
                last.then_inc(S["down_mm"], 1)

            def sequence(b):
                if gated:
                    pe.wait_ge(S["xn_loaded"], 16 * b + 16)
                else:
                    pe.wait_ge(S["xn_done"], b + 1)
                stand(pe, keep["carrier_pe"])
                turn_x(b, 0)
                turn_x(b, 1)
                if not (isinstance(b, int) and b == 0):
                    down(b - 1, BLK - 1)
                for k in range(2, KC):
                    turn_x(b, k)
                for m in range(BLK):
                    up(b, m)
                    if m:
                        down(b, m - 1)

            peeled(pe, 1, B, sequence)
            down(B - 1, BLK - 1)


ARGUMENTS = {
    "x": "L0_attn_hidden_states", "wq": "L0_attn_Wq", "wk": "L0_attn_Wk", "wv": "L0_attn_Wv",
    "wb": "L0_attn_Wb", "bb": "L0_attn_bb", "wg": "L0_attn_Wg", "wo": "L0_attn_Wo",
    "qconv_w": "L0_attn_qconv_w", "qconv_b": "L0_attn_qconv_b",
    "kconv_w": "L0_attn_kconv_w", "kconv_b": "L0_attn_kconv_b",
    "qn_w": "L0_attn_qn_w", "qn_b": "L0_attn_qn_b", "kn_w": "L0_attn_kn_w", "kn_b": "L0_attn_kn_b",
    "w_r": "L0_ffn_w_r", "b_r": "L0_ffn_b_r", "w1": "L0_ffn_w1", "b1": "L0_ffn_b1",
    "w2": "L0_ffn_w2", "b2": "L0_ffn_b2",
}


def build(nc, a):
    s = Shapes(a["x"], a["wq"], a["wb"], a["qn_w"], a["w1"])

    def dram(name, shape, dt=F32):
        return nc.dram_tensor("scratch_" + name, shape, dt).ap()

    scratch = {
        "xt_hi": dram("xt_hi", [s.B, P, s.KC, s.L]),
        "xt_lo": dram("xt_lo", [s.B, P, s.KC, s.L]),
        "score": dram("score", [s.B, s.L]),
        "decay": dram("decay", [s.N, s.L]),
        "cum": dram("cum", [s.N, s.L]),
        "o": dram("o", [s.L, s.B * s.HD]),
        "ids": dram("ids", [s.B * s.L, 1], I32),
        "kept_x": dram("kept_x", [s.B * s.SEL, s.D]),
        "kept_xn": dram("kept_xn", [s.B * s.SEL, s.D]),
        "ffn": dram("ffn", [s.B * s.SEL, s.D]),
    }
    with ExitStack() as ctx:
        keep = {
            "ident": ctx.enter_context(nc.sbuf_tensor("ident", [P, P], F32)),
            "beta_steps": ctx.enter_context(nc.sbuf_tensor("beta_steps", [P, s.NC, s.N], F32)),
            "carrier_dve": ctx.enter_context(nc.semaphore("carrier_dve")),
            "carrier_pe": ctx.enter_context(nc.semaphore("carrier_pe")),
            "carrier_sp": ctx.enter_context(nc.semaphore("carrier_sp")),
            "carrier_pool": ctx.enter_context(nc.semaphore("carrier_pool")),
            "out_copied": ctx.enter_context(nc.semaphore("out_copied")),
        }
        with ExitStack() as first_stages:
            for part in ("xt_hi", "xt_lo"):
                keep[part] = first_stages.enter_context(nc.sbuf_tensor(part, [P, s.KC, s.L], F32R))
            stage_tokens(nc, s, a, scratch, keep)
            stage_recurrence(nc, s, a, scratch, keep)
        stage_kept_tokens(nc, s, a, scratch, keep, gated=False)
        stage_kept_tokens(nc, s, a, scratch, keep, gated=True)


def kernel(**inputs):
    import concourse.bacc as bacc
    from concourse.bass_utils import run_bass_kernel_spmd

    nc = bacc.Bacc("TRN2", target_bir_lowering=False, num_devices=1)
    arrays, a = {}, {}
    for name, given in ARGUMENTS.items():
        array = np.ascontiguousarray(inputs[given])
        if array.ndim == 0:
            array = array.reshape(1)
        arrays["in_" + name] = array
        a[name] = nc.dram_tensor("in_" + name, array.shape, mybir.dt.from_np(array.dtype), kind="ExternalInput").ap()
    x = inputs["L0_attn_hidden_states"]
    a["out"] = nc.dram_tensor("out", x.shape, F32, kind="ExternalOutput").ap()
    build(nc, a)
    result = run_bass_kernel_spmd(nc, [arrays], core_ids=[0])
    return result.results[0]["out"]
```

```python
from contextlib import ExitStack

import numpy as np

import concourse.bass as bass
from concourse import mybir

ALU = mybir.AluOpType
ACT = mybir.ActivationFunctionType
F32 = mybir.dt.float32
F32R = mybir.dt.float32r
I32 = mybir.dt.int32
P = 128
EPS = 1e-5
BANK = 512


class Shapes:

    def __init__(self, x, wq, wb, qn_w, w1):
        self.B, self.L, self.D = x.shape
        self.H = wb.shape[1]
        self.DK = qn_w.shape[0]
        self.HD = wq.shape[1]
        self.F = w1.shape[1]
        self.KC = self.D // P
        self.NC = self.L // P
        self.HALVES = self.L // BANK
        self.SEL = self.L // 2
        self.ST = self.SEL // P
        self.N = self.B * self.H
        self.BLK = self.F // P
        self.PAIRS_PER_SEQ = self.H // 2
        assert self.DK == P and self.HD == self.H * P and self.F == self.HD
        assert self.KC == self.ST and self.D == BANK and self.SEL == BANK and self.HALVES == 2


def after(eng, sem, n):
    if isinstance(n, int) and n <= 0:
        return
    eng.wait_ge(sem, n)


def stand(eng, carrier):
    eng.sem_inc(carrier, 1)


def peeled(eng, first, count, body):
    for n in range(first):
        body(n)
    with eng.Fori(first, count) as n:
        body(n)


def row(ap, n):
    return ap[n] if isinstance(n, int) else ap[bass.ds(n, 1)].squeeze(0)


def stage_tokens(nc, s, a, scratch, keep):
    B, L, D, H, KC, NC = s.B, s.L, s.D, s.H, s.KC, s.NC
    HALF_K = KC // 2
    ROUTER = 32
    with ExitStack() as ctx:
        def sb(name, shape, dt=F32):
            return ctx.enter_context(nc.sbuf_tensor("tk_" + name, shape, dt))

        def two(name, shape, dt=F32):
            return [sb(f"{name}{i}", shape, dt) for i in range(2)]

        def sem(name):
            return ctx.enter_context(nc.semaphore("tk_" + name))

        xt_hi, xt_lo = keep["xt_hi"], keep["xt_lo"]
        x_in = [sb(f"x_in{i}", [P, NC, D]) for i in range(3)]
        xn = sb("xn", [P, NC, D])
        stats = sb("stats", [P, NC, 6])
        mean_var = two("mean_var", [P, NC, 2])
        var_eps = two("var_eps", [P, NC])
        rstd = two("rstd", [P, NC])
        shift = two("shift", [P, NC])
        minus_half = sb("minus_half", [P, NC])
        w_raw = sb("w_raw", [P, KC, ROUTER + 1])
        w_hi = sb("w_hi", [P, KC, P], F32R)
        w_lo = sb("w_lo", [P, KC, P], F32R)
        bias = sb("bias", [ROUTER + 1, 1])
        beta = sb("beta", [H, L])
        score = sb("score", [ROUTER + 1, L])
        one_minus = sb("one_minus", [H, L])
        inside = sb("inside", [H, L])
        decay = sb("decay", [H, L])
        restart = sb("restart", [H, L])
        cum = sb("cum", [H, L])
        ps_t = ctx.enter_context(nc.psum_tensor("tk_ps_t", [P, 2, L], F32))
        ps_gate = ctx.enter_context(nc.psum_tensor("tk_ps_gate", [P, L], F32))
        ps_tok = ctx.enter_context(nc.psum_tensor("tk_ps_tok", [P, NC, H], F32))

        names = """consts_loaded consts_set w_split score_stored decay_stored cum_stored
            stats_done mean_done var_done rstd_done shift_done xn_done score_done t_done hi_done lo_done gate_mm
            beta_done tok_mm tok_done one_minus_done decay_done restart_done cum_done"""
        S = {n: sem(n) for n in names.split()}
        x_half_loaded, x_loaded = sem("x_half_loaded"), [sem(f"x_loaded{n}") for n in range(B)]
        hi_stored, lo_stored = ([sem(f"{part}_stored{i}") for i in range(2)] for part in ("hi", "lo"))
        w_recurrence, w_loaded = keep["w_raw"], keep["w_loaded"]

        x_rows = a["x"].rearrange("b (c p) d -> b p c d", p=P)
        decay_rows = scratch["decay"].rearrange("(b h) t -> b h t", h=H)
        cum_rows = scratch["cum"].rearrange("(b h) t -> b h t", h=H)
        sequences = [(n, B - 1 - n, n % 2) for n in range(B)]

        block = ctx.enter_context(nc.Block())

        @block.sync
        def _(sp):
            def load_x(n, b):
                if n == 0:
                    half = NC // 2
                    sp.dma_start(x_in[0][:, 0:half], x_rows[b][:, 0:half]).then_inc(x_half_loaded, 16)
                    sp.dma_start(x_in[0][:, half:], x_rows[b][:, half:]).then_inc(x_loaded[0], 16)
                else:
                    sp.dma_start(x_in[n % 3][:], x_rows[b]).then_inc(x_loaded[n], 16)

            def store_decays(n, b):
                sp.wait_ge(S["decay_done"], n + 1)
                sp.dma_start(decay_rows[b], decay[:]).then_inc(S["decay_stored"], 16)
                sp.wait_ge(S["cum_done"], n + 1)
                sp.dma_start(cum_rows[b], cum[:]).then_inc(S["cum_stored"], 16)

            with nc.allow_non_contiguous_dma("small constants"):
                load_x(0, B - 1)
                sp.dma_start(w_raw[:, :, 0:H], a["wb"].rearrange("(k p) h -> p k h", p=P)).then_inc(S["consts_loaded"], 16)
                sp.dma_start(w_raw[:, :, ROUTER:ROUTER + 1], a["w_r"].rearrange("(k p o) -> p k o", p=P, o=1)
                             ).then_inc(S["consts_loaded"], 16)
                sp.dma_start(bias[0:H], a["bb"].rearrange("(h o) -> h o", o=1)).then_inc(S["consts_loaded"], 16)
                sp.dma_start(bias[ROUTER:ROUTER + 1], a["b_r"].rearrange("(h o) -> h o", o=1)
                             ).then_inc(S["consts_loaded"], 16)
                load_x(1, B - 2)
                load_x(2, B - 3)
            for n, b, par in sequences:
                if n > 0 and b > 1:
                    sp.wait_ge(S["xn_done"], n)
                    load_x(n + 2, b - 2)
                elif b == 1:
                    for i in range(2):
                        for j, name in enumerate(("wq", "wk")):
                            columns = a[name].rearrange("(k p) n -> p k n", p=P)[:, :, i * P:(i + 1) * P]
                            sp.dma_start(w_recurrence[i][:, j], columns).then_inc(w_loaded[i], 16)
                    sp.dma_start(keep["wv_raw"][:], a["wv"].rearrange("(k p) n -> p k n", p=P)[:, :, 0:2 * P]
                                 ).then_inc(keep["wv_loaded"], 16)
                if b > 0:
                    for i in range(2):
                        ks = slice(i * HALF_K, (i + 1) * HALF_K)
                        sp.wait_ge(S["hi_done"], KC * n + ks.stop)
                        sp.dma_start(scratch["xt_hi"][b][:, ks], xt_hi[:, ks].bitcast(F32)).then_inc(hi_stored[i], 16)
                        sp.wait_ge(S["lo_done"], KC * n + ks.stop)
                        sp.dma_start(scratch["xt_lo"][b][:, ks], xt_lo[:, ks].bitcast(F32)).then_inc(lo_stored[i], 16)
                sp.wait_ge(S["score_done"], n + 1)
                sp.dma_start(scratch["score"][b:b + 1, :], score[ROUTER:ROUTER + 1]).then_inc(S["score_stored"], 16)
                if n:
                    store_decays(n - 1, b + 1)
            store_decays(B - 1, 0)
            for stored in ("score_stored", "decay_stored", "cum_stored"):
                sp.wait_ge(S[stored], 16 * B)
            for stored in hi_stored + lo_stored:
                sp.wait_ge(stored, 16 * (B - 1))

        @block.gpsimd
        def _(pool):
            nc.gpsimd.memset(minus_half[:], -0.5).then_inc(S["consts_set"], 1)
            nc.gpsimd.memset(w_hi[:].bitcast(F32), 0.0).then_inc(S["consts_set"], 1)
            nc.gpsimd.memset(w_lo[:].bitcast(F32), 0.0).then_inc(S["consts_set"], 1)
            nc.gpsimd.memset(keep["ident"][:], 0.0).then_inc(S["consts_set"], 1)
            nc.gpsimd.memset(inside[:], 1.0).then_inc(S["consts_set"], 1)
            pool.wait_ge(S["consts_set"], 5)
            nc.gpsimd.affine_select(out=keep["ident"][:], in_=keep["ident"][:], compare_op=ALU.not_equal,
                                    fill=1.0, base=0, pattern=[[-1, P]], channel_multiplier=1
                                    ).then_inc(S["consts_set"], 1)
            nc.gpsimd.memset(inside[:].rearrange("h (c t) -> h c t", t=P)[:, :, 0:1], 0.0).then_inc(S["consts_set"], 1)
            for n, b, par in sequences:
                pool.wait_ge(S["var_done"], n + 1)
                nc.gpsimd.tensor_tensor(rstd[par][:], var_eps[par][:], minus_half[:], ALU.pow).then_inc(S["rstd_done"], 1)
            pool.wait_ge(w_loaded[0], 16 * 2)
            nc.gpsimd.tensor_copy(keep["w_hi"][0][:], w_recurrence[0][:]).then_inc(keep["w_hi_done"], 1)
            pool.wait_ge(keep["w_hi_done"], 1)
            nc.gpsimd.tensor_tensor(keep["w_lo"][0][:], w_recurrence[0][:], keep["w_hi"][0][:].bitcast(F32),
                                    ALU.subtract).then_inc(keep["w_lo_done"], 1)
            pool.wait_ge(keep["wv_loaded"], 16)
            nc.gpsimd.tensor_copy(keep["wv_hi"][:], keep["wv_raw"][:]).then_inc(keep["wv_hi_done"], 1)
            pool.wait_ge(keep["wv_hi_done"], 1)
            nc.gpsimd.tensor_tensor(keep["wv_lo"][:], keep["wv_raw"][:], keep["wv_hi"][:].bitcast(F32),
                                    ALU.subtract).then_inc(keep["wv_lo_done"], 1)

        @block.scalar
        def _(act):
            act.wait_ge(S["consts_loaded"], 64)
            act.wait_ge(S["consts_set"], 3)
            nc.scalar.activation(w_hi[:, :, 0:H], w_raw[:, :, 0:H], ACT.Copy).then_inc(S["w_split"], 1)
            nc.scalar.activation(w_hi[:, :, ROUTER:ROUTER + 1], w_raw[:, :, ROUTER:ROUTER + 1], ACT.Copy
                                 ).then_inc(S["w_split"], 1)

            def normalise(n, par):
                act.wait_ge(S["shift_done"], n + 1)
                act.wait_ge(S["rstd_done"], n + 1)
                after(act, S["t_done"], KC * n)
                for c in range(NC):
                    last = nc.scalar.activation(xn[:, c], x_in[n % 3][:, c], ACT.Identity,
                                                bias=shift[par][:, c:c + 1], scale=rstd[par][:, c:c + 1])
                last.then_inc(S["xn_done"], 1)

            normalise(0, 0)
            for n, b, par in sequences:
                for k in range(KC):
                    act.wait_ge(S["t_done"], KC * n + k + 1)
                    after(act, hi_stored[k // HALF_K], 16 * n)
                    after(act, S["gate_mm"], n)
                    nc.scalar.activation(xt_hi[:, k], ps_t[:, k % 2], ACT.Copy).then_inc(S["hi_done"], 1)
                if n + 1 < B:
                    normalise(n + 1, 1 - par)
                act.wait_ge(S["gate_mm"], n + 1)
                after(act, S["tok_mm"], n)
                after(act, S["one_minus_done"], n)
                nc.scalar.activation(beta[:], ps_gate[0:H], ACT.Sigmoid, bias=bias[0:H]).then_inc(S["beta_done"], 1)
                after(act, S["score_stored"], 16 * n)
                nc.scalar.activation(score[ROUTER:ROUTER + 1], ps_gate[ROUTER:ROUTER + 1], ACT.Identity,
                                     bias=bias[ROUTER:ROUTER + 1]).then_inc(S["score_done"], 1)

        @block.vector
        def _(dve):
            def statistics(n, par):
                after(dve, S["mean_done"], n)
                for c in range(NC):
                    if c % (NC // 2) == 0:
                        dve.wait_ge(x_half_loaded if n == 0 and c == 0 else x_loaded[n], 16)
                    last = nc.vector.bn_stats(stats[:, c], x_in[n % 3][:, c])
                last.then_inc(S["stats_done"], 1)
                dve.wait_ge(S["stats_done"], n + 1)
                for c in range(NC):
                    last = nc.vector.bn_aggr(mean_var[par][:, c], stats[:, c])
                last.then_inc(S["mean_done"], 1)
                dve.wait_ge(S["mean_done"], n + 1)
                nc.vector.tensor_scalar(var_eps[par][:], mean_var[par][:, :, 1], EPS, None, ALU.add
                                        ).then_inc(S["var_done"], 1)

            def shifts(n, par):
                dve.wait_ge(S["rstd_done"], n + 1)
                after(dve, S["xn_done"], n - 1)
                nc.vector.scalar_tensor_tensor(out=shift[par][:], in0=mean_var[par][:, :, 0], scalar=-1.0,
                                               in1=rstd[par][:], op0=ALU.mult, op1=ALU.mult
                                               ).then_inc(S["shift_done"], 1)

            def decays(n, b):
                dve.wait_ge(S["beta_done"], n + 1)
                nc.vector.tensor_scalar(one_minus[:], beta[:], -1.0, 1.0, ALU.mult, ALU.add
                                        ).then_inc(S["one_minus_done"], 1)
                dve.wait_ge(S["one_minus_done"], n + 1)
                after(dve, S["decay_stored"], 16 * n)
                nc.vector.tensor_tensor(decay[:], one_minus[:], inside[:], ALU.mult).then_inc(S["decay_done"], 1)
                dve.wait_ge(S["decay_done"], n + 1)
                nc.vector.tensor_tensor(restart[:], one_minus[:], decay[:], ALU.subtract).then_inc(S["restart_done"], 1)
                dve.wait_ge(S["restart_done"], n + 1)
                after(dve, S["cum_stored"], 16 * n)
                nc.vector.tensor_tensor_scan(cum[:], decay[:], restart[:], 0.0, ALU.mult, ALU.add
                                             ).then_inc(S["cum_done"], 1)
                dve.wait_ge(S["tok_mm"], n + 1)
                nc.vector.tensor_copy(keep["beta_steps"][:, :, b * H:(b + 1) * H], ps_tok[:]).then_inc(S["tok_done"], 1)

            statistics(0, 0)
            shifts(0, 0)
            statistics(1, 1)
            shifts(1, 1)
            dve.wait_ge(S["w_split"], 2)
            nc.vector.tensor_tensor(w_lo[:, :, 0:H], w_raw[:, :, 0:H], w_hi[:, :, 0:H].bitcast(F32), ALU.subtract
                                    ).then_inc(S["w_split"], 1)
            nc.vector.tensor_tensor(w_lo[:, :, ROUTER:ROUTER + 1], w_raw[:, :, ROUTER:ROUTER + 1],
                                    w_hi[:, :, ROUTER:ROUTER + 1].bitcast(F32), ALU.subtract
                                    ).then_inc(S["w_split"], 1)
            dve.wait_ge(S["consts_set"], 7)
            for n, b, par in sequences:
                for k in range(KC):
                    dve.wait_ge(S["hi_done"], KC * n + k + 1)
                    after(dve, lo_stored[k // HALF_K], 16 * n)
                    nc.vector.tensor_tensor(xt_lo[:, k], ps_t[:, k % 2], xt_hi[:, k].bitcast(F32), ALU.subtract
                                            ).then_inc(S["lo_done"], 1)
                if n:
                    decays(n - 1, b + 1)
                if n + 2 < B:
                    statistics(n + 2, par)
                    shifts(n + 2, par)
            decays(B - 1, 0)

        @block.tensor
        def _(pe):
            pe.wait_ge(S["consts_set"], 6)
            for n, b, par in sequences:
                def turn(k):
                    after(pe, S["lo_done"], KC * n + k - 1)
                    for c in range(NC):
                        last = nc.tensor.transpose(ps_t[:, k % 2, c * P:(c + 1) * P],
                                                   xn[:, c, k * P:(k + 1) * P], keep["ident"][:])
                    last.then_inc(S["t_done"], 1)

                def gates(k):
                    pe.wait_ge(S["hi_done"], KC * n + k + 1)
                    pe.wait_ge(S["lo_done"], KC * n + k + 1)
                    for half in range(s.HALVES):
                        cols = slice(half * BANK, (half + 1) * BANK)
                        nc.tensor.matmul(ps_gate[:, cols], w_hi[:, k], xt_hi[:, k, cols], start=k == 0, stop=False)
                        nc.tensor.matmul(ps_gate[:, cols], w_hi[:, k], xt_lo[:, k, cols], start=False, stop=False)
                        last = nc.tensor.matmul(ps_gate[:, cols], w_lo[:, k], xt_hi[:, k, cols],
                                                start=False, stop=k == KC - 1)
                    return last

                pe.wait_ge(S["xn_done"], n + 1)
                turn(0)
                turn(1)
                pe.wait_ge(S["w_split"], 4)
                after(pe, S["beta_done"], n)
                after(pe, S["score_done"], n)
                for k in range(2, KC):
                    turn(k)
                    gates(k - 2)
                for k in range(KC - 2, KC):
                    last = gates(k)
                last.then_inc(S["gate_mm"], 1)
                pe.wait_ge(S["beta_done"], n + 1)
                after(pe, S["tok_done"], n)
                for c in range(NC):
                    last = nc.tensor.transpose(ps_tok[:, c], beta[:, c * P:(c + 1) * P], keep["ident"][0:H, 0:H])
                last.then_inc(S["tok_mm"], 1)


def weight_piece(s, a, keep, gated, n):
    up, down = (a["wg"], a["wo"]) if gated else (a["w1"], a["w2"])
    g, part = divmod(n, 4)
    first = (4 * g + 2 * (part % 2)) * P
    place = keep["staging"][:, n % 2]
    if part < 2:
        return up.rearrange("(k p) n -> p k n", p=P)[:, :, first:first + 2 * P], place
    return (down[first:first + 2 * P, :].rearrange("(m p) n -> p m n", p=P),
            place.rearrange("p k w -> p (k w)").rearrange("p (m d) -> p m d", d=s.D))


class KeptRows:

    def __init__(self, nc, s, a, ctx, keep):
        sb = lambda name, shape, dt=F32: ctx.enter_context(nc.sbuf_tensor("kept_" + name, shape, dt))
        self.nc, self.s, self.keep = nc, s, keep
        self.x = a["x"].rearrange("b l d -> (b l) d")
        self.ids = sb("ids", [P, s.B, s.ST], I32)
        self.x_rows = sb("x_rows", [P, s.ST, s.D])
        self.stats = sb("stats", [P, s.ST, 6])
        self.mean_var = sb("mean_var", [P, s.ST, 2])
        self.var_eps = sb("var_eps", [P, s.ST])
        self.rstd = sb("rstd", [P, s.ST])
        self.shift = sb("shift", [P, s.ST])
        self.minus_half = sb("minus_half", [P, s.ST])
        names = "ids_loaded minus_half_set x_loaded x_kept stats_done mean_done var_done rstd_done shift_done xn_done"
        self.S = {n: ctx.enter_context(nc.semaphore("kept_" + n)) for n in names.split()}

    def load_ids(self, sp, scratch):
        s = self.s
        rows = scratch["ids"].rearrange("(b h p t) o -> h p b (t o)", p=P, t=s.ST, h=s.L // s.SEL)[0]
        sp.dma_start(self.ids[:], rows).then_inc(self.S["ids_loaded"], 16)

    def gather(self, pool, b):
        if b == 0:
            self.nc.gpsimd.memset(self.minus_half[:], -0.5).then_inc(self.S["minus_half_set"], 1)
            pool.wait_ge(self.S["ids_loaded"], 16)
        after(pool, self.S["xn_done"], b)
        after(pool, self.S["x_kept"], 16 * b)
        for t in range(self.s.ST):
            self.nc.gpsimd.indirect_dma_start(
                out=self.x_rows[:, t], out_offset=None, in_=self.x,
                in_offset=bass.IndirectOffsetOnAxis(ap=self.ids[:, b, t:t + 1], axis=0)
            ).then_inc(self.S["x_loaded"], 16)

    def statistics(self, dve, b):
        nc, s, S = self.nc, self.s, self.S
        dve.wait_ge(S["x_loaded"], 16 * (s.ST * b + s.ST))
        after(dve, S["xn_done"], b)
        stand(dve, self.keep["carrier_dve"])
        for t in range(s.ST):
            last = nc.vector.bn_stats(self.stats[:, t], self.x_rows[:, t])
        last.then_inc(S["stats_done"], 1)
        dve.wait_ge(S["stats_done"], b + 1)
        stand(dve, self.keep["carrier_dve"])
        for t in range(s.ST):
            last = nc.vector.bn_aggr(self.mean_var[:, t], self.stats[:, t])
        last.then_inc(S["mean_done"], 1)
        dve.wait_ge(S["mean_done"], b + 1)
        after(dve, S["rstd_done"], b)
        nc.vector.tensor_scalar(self.var_eps[:], self.mean_var[:, :, 1], EPS, None, ALU.add
                                ).then_inc(S["var_done"], 1)

    def rstd_of(self, pool, b):
        pool.wait_ge(self.S["minus_half_set"], 1)
        pool.wait_ge(self.S["var_done"], b + 1)
        after(pool, self.S["xn_done"], b)
        self.nc.gpsimd.tensor_tensor(self.rstd[:], self.var_eps[:], self.minus_half[:], ALU.pow
                                     ).then_inc(self.S["rstd_done"], 1)

    def shifts(self, dve, b):
        dve.wait_ge(self.S["rstd_done"], b + 1)
        self.nc.vector.scalar_tensor_tensor(out=self.shift[:], in0=self.mean_var[:, :, 0], scalar=-1.0,
                                            in1=self.rstd[:], op0=ALU.mult, op1=ALU.mult
                                            ).then_inc(self.S["shift_done"], 1)

    def normalise(self, act, b):
        act.wait_ge(self.S["shift_done"], b + 1)
        act.wait_ge(self.S["rstd_done"], b + 1)
        for t in range(self.s.ST):
            last = self.nc.scalar.activation(self.keep["xn_rows"][:, t], self.x_rows[:, t], ACT.Identity,
                                             bias=self.shift[:, t:t + 1], scale=self.rstd[:, t:t + 1])
        last.then_inc(self.S["xn_done"], 1)


def stage_recurrence(nc, s, a, scratch, keep, kept):
    B, L, H, KC, NC, N = s.B, s.L, s.H, s.KC, s.NC, s.N
    TAPS = a["qconv_w"].shape[1]
    PAD = TAPS - 1
    LAG_B, LAG_C, LAG_D = 1, 2, 3
    PEELED_PAIRS = 2
    PAIRS = N // 2
    PPS = s.PAIRS_PER_SEQ
    with ExitStack() as ctx:
        def sb(name, shape, dt=F32):
            return ctx.enter_context(nc.sbuf_tensor("rc_" + name, shape, dt))

        def two(name, shape, dt=F32):
            return [sb(f"{name}{i}", shape, dt) for i in range(2)]

        def sem(name):
            return ctx.enter_context(nc.semaphore("rc_" + name))

        ident = keep["ident"]
        xt_hi, xt_lo = keep["xt_hi"], keep["xt_lo"]
        w_raw, w_hi, w_lo = keep["w_raw"], keep["w_hi"], keep["w_lo"]
        wv_raw, wv_hi, wv_lo = keep["wv_raw"], keep["wv_hi"], keep["wv_lo"]
        conv = two("conv", [P, 2, TAPS + 1])
        norm = sb("norm", [P, 2, 2])
        k_norm_rows = sb("k_norm_rows", [P, 2, P])
        raw = [keep["raw"][:, j * (PAD + L):(j + 1) * (PAD + L)] for j in range(2)]
        act_cm = [keep["xn_rows"][:].rearrange("p t d -> p (t d)")[:, j * L:(j + 1) * L] for j in range(2)]
        tok = [sb("tok_q", [P, NC, P]), sb("tok_k", [P, NC, P])]
        v_raw = sb("v_raw", [P, NC, 2, P])
        q_cm = two("q_cm", [P, L])
        k_cm = two("k_cm", [P, L])
        k_state = two("k_state", [P, NC, P])
        v_beta = two("v_beta", [P, NC, P])
        decay_all = two("decay_all", [P, L])
        cum_all = two("cum_all", [P, L])
        dmat = two("dmat", [P, NC, P])
        q_cum = sb("q_cum", [P, L])
        scores = sb("scores", [P, NC, P])
        states = sb("states", [P, NC - 1, P])
        o_sb = two("o_sb", [P, NC, P])
        chunk_ident = sb("chunk_ident", [P, NC, P])
        stats = sb("stats", [P, 2, NC, 6])
        small = sb("small", [P, 8, 2, NC])
        minus_half = sb("minus_half", [P, 2, NC])
        score_all = sb("score_all", [P, L])
        score_tok = sb("score_tok", [P, B * NC])
        equal = sb("equal", [P, L])
        token_row = sb("token_row", [P, L])
        token_col = sb("token_col", [P, B * NC])
        first_slot = sb("first_slot", [P, B * NC])
        greater = sb("greater", [P, 1])
        ties = sb("ties", [P, 1])
        slot = sb("slot", [P, 1], I32)
        token_id = sb("token_id", [P, 1], I32)

        ps_proj = ctx.enter_context(nc.psum_tensor("rc_ps_proj", [P, 2, L], F32))
        ps_work = ctx.enter_context(nc.psum_tensor("rc_ps_work", [P, 2, L], F32))

        names = """consts_loaded consts_set k_half
            q_projected k_projected v_projected q_raw k_raw q_tap k_tap q_conv k_conv q_silu k_silu v_copied
            q_turned k_turned q_tok k_tok stats_done small_done rstd_done shift_done q_normed k_normed
            q_back k_back k_weighted k_tokens_done q_ready k_ready k_state_done v_beta_done
            dmat_done scores_mm scores_done updates_mm states_done outputs_mm outputs_done q_cum_done
            score_loaded greater_done equal_done ties_done slot_done id_done scattered"""
        S = {n: sem(n) for n in names.split()}
        w_loaded, wv_loaded = keep["w_loaded"], keep["wv_loaded"]
        for n in ("w_hi_done", "w_lo_done", "wv_hi_done", "wv_lo_done"):
            S[n] = keep[n]
        xt_loaded = [sem(f"xt_loaded{i}") for i in range(2)]
        conv_loaded = [sem(f"conv_loaded{i}") for i in range(2)]
        decay_loaded = [sem(f"decay_loaded{i}") for i in range(2)]
        cum_loaded = [sem(f"cum_loaded{i}") for i in range(2)]
        o_stored = keep["o_stored"]

        w_views = [a[n].rearrange("(k p) n -> p k n", p=P) for n in ("wq", "wk", "wv")]
        conv_w = [a["qconv_w"], a["kconv_w"]]
        conv_b = [a["qconv_b"].rearrange("(n o) -> n o", o=1), a["kconv_b"].rearrange("(n o) -> n o", o=1)]
        o_rows = scratch["o"].rearrange("(c p) n -> p c n", p=P)
        W_PARTS, CONV_PARTS = 2, 4
        VC = NC // 2

        class At:

            def __init__(self, u, par, lag=0):
                self.i = 2 * u + par - lag
                self.par = (par - lag) % 2
                self.pair = u + (par - lag) // 2
                self.live = not isinstance(self.i, int) or 0 <= self.i < N

        def after_step(eng, name, i, per=1, part=None):
            if isinstance(i, int):
                if i < 0:
                    return
                i = min(i, N - 1)
            eng.wait_ge(S[name], per * i + (per if part is None else part))

        def after_pair(eng, semaphore, pair, per=16):
            if isinstance(pair, int) and pair < 0:
                return
            eng.wait_ge(semaphore, per * pair + per)

        def steps(eng, step, between=None):
            for u in range(PEELED_PAIRS):
                for par in range(2):
                    step(u, par)
            with eng.Fori(PEELED_PAIRS, PAIRS - 1) as u:
                for par in range(2):
                    step(u, par)
            for i in range(N - 2, N + LAG_D):
                step(i // 2, i % 2)
                if between and i == N + 1:
                    between()

        block = ctx.enter_context(nc.Block())

        @block.sync
        def _(sp):
            def load_weights(pair, head):
                for par in range(2):
                    after(sp, S["w_lo_done"], 2 * pair + par - 1)
                    for j in range(W_PARTS):
                        sp.dma_start(w_raw[par][:, j], w_views[j][:, :, bass.ds((head + par) * P, P)]
                                     ).then_inc(w_loaded[par], 16)
                after(sp, S["wv_lo_done"], pair)
                sp.dma_start(wv_raw[:], w_views[2][:, :, bass.ds(head * P, 2 * P)]).then_inc(wv_loaded, 16)

            def load_constants(pair, head, seq):
                for par in range(2):
                    after(sp, S["k_conv"], PAD * (2 * pair + par - 1))
                    stand(sp, keep["carrier_sp"])
                    for j in range(2):
                        sp.dma_start(conv[par][:, j, 0:TAPS], conv_w[j][bass.ds((head + par) * P, P), :]
                                     ).then_inc(conv_loaded[par], 16)
                        sp.dma_start(conv[par][:, j, TAPS:TAPS + 1], conv_b[j][bass.ds((head + par) * P, P), :]
                                     ).then_inc(conv_loaded[par], 16)
                after(sp, S["greater_done"], pair)
                after(sp, S["equal_done"], pair)
                sp.dma_start(score_all[:], row(scratch["score"], seq).partition_broadcast(P)
                             ).then_inc(S["score_loaded"], 16)

            with nc.allow_non_contiguous_dma("per-channel constants"):
                for half in range(s.HALVES):
                    sp.sem_inc(xt_loaded[half], 32)
                for j in range(2):
                    for n, name in enumerate((("qn_w", "qn_b"), ("kn_w", "kn_b"))[j]):
                        sp.dma_start(norm[:, j, n:n + 1], a[name].rearrange("(n o) -> n o", o=1)
                                     ).then_inc(S["consts_loaded"], 16)
                for n, name in enumerate(("kn_w", "kn_b")):
                    sp.dma_start(k_norm_rows[:, n], a[name].partition_broadcast(P)).then_inc(S["consts_loaded"], 16)
                sp.dma_start(score_tok[:], scratch["score"].rearrange("b (c p) -> p (b c)", p=P)
                             ).then_inc(S["consts_loaded"], 16)
                load_constants(0, 0, 0)
                with sp.Fori(0, B - 1) as b:
                    with sp.Fori(0, PPS - 1) as hp:
                        load_weights(b * PPS + hp + 1, hp * 2 + 2)
                        load_constants(b * PPS + hp + 1, hp * 2 + 2, b)
                    load_weights((b + 1) * PPS, 0)
                    for half in range(s.HALVES):
                        cols = slice(half * BANK, (half + 1) * BANK)
                        sp.wait_ge(S[("k_half", "v_projected")[half]], b * H + H)
                        for part, name in ((xt_hi, "xt_hi"), (xt_lo, "xt_lo")):
                            sp.dma_start(part[:, :, cols].bitcast(F32), row(scratch[name], b + 1)[:, :, cols]
                                         ).then_inc(xt_loaded[half], 16)
                    load_constants((b + 1) * PPS, 0, b + 1)
                with sp.Fori(0, PPS - 1) as hp:
                    load_weights((B - 1) * PPS + hp + 1, hp * 2 + 2)
                    load_constants((B - 1) * PPS + hp + 1, hp * 2 + 2, B - 1)
                sp.wait_ge(S["q_conv"], PAD * N)
                sp.wait_ge(S["k_conv"], PAD * N)
                for n in range(2):
                    source, staged = weight_piece(s, a, keep, False, n)
                    sp.dma_start(staged, source).then_inc(keep["piece_loaded"][False][n], 16)
                sp.wait_ge(S["scattered"], 16 * PAIRS)
                kept.load_ids(sp, scratch)

        @block.gpsimd
        def _(pool):
            nc.gpsimd.memset(minus_half[:], -0.5).then_inc(S["consts_set"], 1)
            nc.gpsimd.memset(raw[0][:, 0:PAD], 0.0).then_inc(S["consts_set"], 1)
            nc.gpsimd.memset(raw[1][:, 0:PAD], 0.0).then_inc(S["consts_set"], 1)
            for c in range(NC):
                last = nc.gpsimd.tensor_copy(chunk_ident[:, c], ident[:])
            last.then_inc(S["consts_set"], 1)
            nc.gpsimd.iota(token_row[:], pattern=[[1, L]], base=0, channel_multiplier=0,
                           allow_small_or_imprecise_dtypes=True).then_inc(S["consts_set"], 1)
            nc.gpsimd.iota(token_col[:], pattern=[[0, B], [P, NC]], base=0, channel_multiplier=1,
                           allow_small_or_imprecise_dtypes=True).then_inc(S["consts_set"], 1)
            nc.gpsimd.iota(first_slot[:], pattern=[[L, B], [0, NC]], base=0, channel_multiplier=0,
                           allow_small_or_imprecise_dtypes=True).then_inc(S["consts_set"], 1)

            def step(u, par):
                A_, B_, C_, D_, nxt = (At(u, par, lag) for lag in (0, LAG_B, LAG_C, LAG_D, -1))
                if par == 0 and A_.live and not (isinstance(u, int) and u == 0):
                    after_step(pool, "wv_hi_done", u)
                    after_step(pool, "v_projected", A_.i - 1)
                    stand(pool, keep["carrier_pool"])
                    nc.gpsimd.tensor_tensor(wv_lo[:], wv_raw[:], wv_hi[:].bitcast(F32), ALU.subtract
                                            ).then_inc(S["wv_lo_done"], 1)
                if C_.live:
                    k_tokens = k_state[C_.par]
                    after_step(pool, "k_normed", C_.i)
                    after_step(pool, "updates_mm", C_.i - 2)
                    nc.gpsimd.tensor_tensor(k_tokens[:], tok[1][:], k_norm_rows[:, 0:1].to_broadcast([P, NC, P]),
                                            ALU.mult).then_inc(S["k_weighted"], 1)
                    after_step(pool, "k_weighted", C_.i)
                    nc.gpsimd.tensor_tensor(k_tokens[:], k_tokens[:], k_norm_rows[:, 1:2].to_broadcast([P, NC, P]),
                                            ALU.add).then_inc(S["k_tokens_done"], 1)
                if D_.live:
                    after_step(pool, "q_ready", D_.i)
                    after_pair(pool, cum_loaded[D_.par], D_.pair)
                    after_step(pool, "outputs_mm", D_.i - 1)
                    nc.gpsimd.tensor_tensor(q_cum[:], q_cm[D_.par][:], cum_all[D_.par][:], ALU.mult
                                            ).then_inc(S["q_cum_done"], 1)
                if B_.live:
                    after_step(pool, "small_done", B_.i, 6)
                    nc.gpsimd.tensor_tensor(small[:, 6], small[:, 5], minus_half[:], ALU.pow
                                            ).then_inc(S["rstd_done"], 1)
                if nxt.live:
                    after_step(pool, "w_hi_done", nxt.i)
                    after_step(pool, "k_projected", nxt.i - 2)
                    stand(pool, keep["carrier_pool"])
                    nc.gpsimd.tensor_tensor(w_lo[nxt.par][:], w_raw[nxt.par][:], w_hi[nxt.par][:].bitcast(F32),
                                            ALU.subtract).then_inc(S["w_lo_done"], 1)

            pool.wait_ge(S["consts_loaded"], 16 * 7)

            def pair_steps(u):
                step(u, 0)
                step(u, 1)
                scatter(u)

            def scatter(u):
                pool.wait_ge(S["slot_done"], u + 1)
                pool.wait_ge(S["id_done"], u + 1)
                stand(pool, keep["carrier_pool"])
                nc.gpsimd.indirect_dma_start(
                    out=scratch["ids"], out_offset=bass.IndirectOffsetOnAxis(ap=slot[:, 0:1], axis=0),
                    in_=token_id[:, 0:1], in_offset=None).then_inc(S["scattered"], 16)

            for u in range(PEELED_PAIRS):
                pair_steps(u)
            with pool.Fori(PEELED_PAIRS, PAIRS - 1) as u:
                pair_steps(u)
            pair_steps(PAIRS - 1)
            step(N // 2, N % 2)
            kept.gather(pool, 0)
            step((N + 1) // 2, (N + 1) % 2)
            kept.rstd_of(pool, 0)
            step((N + 2) // 2, (N + 2) % 2)
            pool.wait_ge(S["scattered"], 16 * PAIRS)

        @block.scalar
        def _(act):
            act.wait_ge(S["consts_loaded"], 16 * 7)
            act.wait_ge(S["consts_set"], 7)

            def load_decay(par, i, pair):
                after_step(act, "dmat_done", i - 2)
                act.dma_start(decay_all[par][:], row(scratch["decay"], i).partition_broadcast(P)
                              ).then_inc(decay_loaded[par], 16)

            def load_cum(par, i, pair):
                after_step(act, "states_done", i - 2, NC - 1)
                after_step(act, "q_cum_done", i - 2)
                act.dma_start(cum_all[par][:], row(scratch["cum"], i).partition_broadcast(P)
                              ).then_inc(cum_loaded[par], 16)

            def step(u, par):
                A_, B_, C_, D_, nxt = (At(u, par, lag) for lag in (0, LAG_B, LAG_C, LAG_D, -1))
                proj_of = lambda pos: ps_proj[:, (par + pos) % 2]

                def ready(j, name_in, name_out, out):
                    after_step(act, name_in, C_.i)
                    after_step(act, "scores_mm", C_.i - 2)
                    if j == 0:
                        after_step(act, "q_cum_done", C_.i - 2)
                    nc.scalar.activation(out[:], work(par, j), ACT.Identity,
                                         bias=norm[:, j, 1:2], scale=norm[:, j, 0:1]).then_inc(S[name_out], 1)

                def own_raw(j):
                    n = "qk"[j]
                    after_step(act, n + "_projected", A_.i)
                    after_step(act, n + "_conv", A_.i - 1, PAD)
                    nc.scalar.activation(raw[j][:, PAD:], proj_of(j), ACT.Copy).then_inc(S[n + "_raw"], 1)

                def tap(j):
                    n = "qk"[j]
                    if j == 0:
                        after_pair(act, conv_loaded[par], A_.pair, 16 * CONV_PARTS)
                    after_step(act, n + "_turned", A_.i - 1)
                    nc.scalar.activation(act_cm[j], proj_of(j), ACT.Identity,
                                         bias=conv[par][:, j, TAPS:TAPS + 1],
                                         scale=conv[par][:, j, PAD:TAPS]).then_inc(S[n + "_tap"], 1)

                def tokens(j):
                    n = "qk"[j]
                    after_step(act, n + "_turned", B_.i)
                    after_step(act, n + "_back", B_.i - 1)
                    if j == 1:
                        after_step(act, "k_weighted", B_.i - 1)
                    nc.scalar.activation(tok[j][:], work(par, 2 + j), ACT.Copy).then_inc(S[n + "_tok"], 1)

                def silu(j):
                    n = "qk"[j]
                    after_step(act, n + "_conv", B_.i, PAD)
                    nc.scalar.activation(act_cm[j], act_cm[j], ACT.Silu).then_inc(S[n + "_silu"], 1)

                if C_.live:
                    ready(0, "q_back", "q_ready", q_cm[C_.par])
                if B_.live:
                    silu(0)
                    after_step(act, "v_projected", B_.i)
                    after_step(act, "v_beta_done", 2 * B_.pair - 1)
                    nc.scalar.activation(v_raw[:, B_.par * VC:(B_.par + 1) * VC].rearrange("p c h t -> p (c h t)"),
                                         ps_proj[:, B_.par], ACT.Copy).then_inc(S["v_copied"], 1)
                if par == 0 and A_.live and not (isinstance(u, int) and u == 0):
                    after_pair(act, wv_loaded, u)
                    after_step(act, "v_projected", A_.i - 1)
                    nc.scalar.activation(wv_hi[:], wv_raw[:], ACT.Copy).then_inc(S["wv_hi_done"], 1)
                if A_.live:
                    own_raw(0)
                if C_.live:
                    ready(1, "k_back", "k_ready", k_cm[C_.par])
                if B_.live:
                    silu(1)
                    tokens(0)
                if A_.live:
                    tap(0)
                if B_.live:
                    tokens(1)
                if A_.live:
                    own_raw(1)
                    tap(1)
                if B_.live:
                    load_decay(B_.par, B_.i, B_.pair)
                if C_.live:
                    load_cum(C_.par, C_.i, C_.pair)
                if nxt.live:
                    after_pair(act, w_loaded[nxt.par], nxt.pair, 16 * W_PARTS)
                    after_step(act, "k_projected", nxt.i - 2)
                    nc.scalar.activation(w_hi[nxt.par][:], w_raw[nxt.par][:], ACT.Copy).then_inc(S["w_hi_done"], 1)
                if B_.live:
                    after_step(act, "rstd_done", B_.i)
                    after_step(act, "shift_done", B_.i)
                    for c in range(NC):
                        last = nc.scalar.activation(tok[1][:, c], tok[1][:, c], ACT.Identity,
                                                    bias=small[:, 7, 1, c:c + 1], scale=small[:, 6, 1, c:c + 1])
                    last.then_inc(S["k_normed"], 1)
                if D_.live:
                    after_step(act, "outputs_mm", D_.i)
                    after_pair(act, o_stored[D_.par], D_.pair - 1)
                    nc.scalar.activation(o_sb[D_.par][:], work(par, 6), ACT.Copy).then_inc(S["outputs_done"], 1)
                    after_step(act, "outputs_done", D_.i)
                    act.dma_start(o_rows[:, :, bass.ds(D_.i * P, P)], o_sb[D_.par][:]).then_inc(o_stored[D_.par], 16)

            def work(par, pos):
                return ps_work[:, (par + pos) % 2]

            def first_kept_rows():
                act.wait_ge(S["k_turned"], N)
                kept.normalise(act, 0)

            steps(act, step, first_kept_rows)

        @block.vector
        def _(dve):
            dve.wait_ge(S["consts_loaded"], 16 * 7)
            dve.wait_ge(S["consts_set"], 7)

            def work(par, pos):
                return ps_work[:, (par + pos) % 2]

            def chunks(ap):
                return ap.rearrange("p (c t) -> p c t", t=P)

            def step(u, par):
                A_, B_, C_, D_ = (At(u, par, lag) for lag in (0, LAG_B, LAG_C, LAG_D))

                def convolve(j):
                    n = "qk"[j]
                    after_step(dve, n + "_raw", B_.i)
                    after_step(dve, n + "_tap", B_.i)
                    for t in range(PAD):
                        if t:
                            after_step(dve, n + "_conv", B_.i, PAD, t)
                        nc.vector.scalar_tensor_tensor(out=act_cm[j], in0=raw[j][:, t:t + L],
                                                       scalar=conv[B_.par][:, j, t:t + 1], in1=act_cm[j],
                                                       op0=ALU.mult, op1=ALU.add).then_inc(S[n + "_conv"], 1)

                def statistics(j):
                    n = "qk"[j]
                    after_step(dve, n + "_tok", B_.i)
                    for c in range(NC):
                        last = nc.vector.bn_stats(stats[:, j, c], tok[j][:, c])
                    last.then_inc(S["stats_done"], 1)

                def variance():
                    m_even, q_even, m_odd, q_odd = (stats[:, :, :, n] for n in (1, 2, 4, 5))
                    after_step(dve, "stats_done", B_.i, 2)
                    after_step(dve, "q_normed", B_.i - 1)
                    after_step(dve, "k_normed", B_.i - 1)
                    done = lambda part: after_step(dve, "small_done", B_.i, 6, part)
                    inc = lambda ins: ins.then_inc(S["small_done"], 1)
                    inc(nc.vector.tensor_tensor(small[:, 0], m_even, m_odd, ALU.add))
                    inc(nc.vector.tensor_tensor(small[:, 1], m_even, m_odd, ALU.subtract))
                    inc(nc.vector.tensor_tensor(small[:, 2], q_even, q_odd, ALU.add))
                    done(2)
                    inc(nc.vector.tensor_tensor(small[:, 3], small[:, 1], small[:, 1], ALU.mult))
                    done(3)
                    inc(nc.vector.tensor_scalar(small[:, 4], small[:, 2], 1.0 / P, EPS, ALU.mult, ALU.add))
                    done(5)
                    inc(nc.vector.scalar_tensor_tensor(out=small[:, 5], in0=small[:, 3], scalar=0.25,
                                                       in1=small[:, 4], op0=ALU.mult, op1=ALU.add))

                def normalise():
                    after_step(dve, "rstd_done", B_.i)
                    nc.vector.scalar_tensor_tensor(out=small[:, 7], in0=small[:, 0], scalar=-0.5, in1=small[:, 6],
                                                   op0=ALU.mult, op1=ALU.mult).then_inc(S["shift_done"], 1)
                    after_step(dve, "shift_done", B_.i)
                    for c in range(NC):
                        last = nc.vector.tensor_scalar(tok[0][:, c], tok[0][:, c], small[:, 6, 0, c:c + 1],
                                                       small[:, 7, 0, c:c + 1], ALU.mult, ALU.add)
                    last.then_inc(S["q_normed"], 1)

                def gate_values():
                    after_step(dve, "v_copied", 2 * C_.pair + 1)
                    after_step(dve, "outputs_mm", C_.i - 2)
                    after_step(dve, "updates_mm", C_.i - 2)
                    gate = keep["beta_steps"][:, :, bass.ds(C_.i, 1)].to_broadcast([P, NC, P])
                    nc.vector.tensor_tensor(v_beta[C_.par][:], v_raw[:, :, C_.par], gate, ALU.mult
                                            ).then_inc(S["v_beta_done"], 1)

                if B_.live:
                    convolve(0)
                if C_.live and par == 1:
                    gate_values()
                if B_.live:
                    convolve(1)
                if C_.live:
                    after_pair(dve, decay_loaded[C_.par], C_.pair)
                    after_step(dve, "scores_done", C_.i - 2)
                    nc.vector.tensor_tensor_scan(dmat[C_.par][:].rearrange("p c t -> p (c t)"), decay_all[C_.par][:],
                                                 chunk_ident[:].rearrange("p c t -> p (c t)"), 0.0,
                                                 ALU.mult, ALU.add).then_inc(S["dmat_done"], 1)
                if C_.live and par == 0:
                    gate_values()
                if A_.live and par == 1:
                    ranks(u)
                if B_.live:
                    statistics(0)
                    statistics(1)
                if D_.live:
                    after_step(dve, "scores_mm", D_.i)
                    after_step(dve, "outputs_mm", D_.i - 1)
                    nc.vector.tensor_tensor(scores[:], chunks(work(par, 4)), dmat[D_.par][:], ALU.mult
                                            ).then_inc(S["scores_done"], 1)
                if B_.live:
                    variance()
                if C_.live:
                    after_step(dve, "k_tokens_done", C_.i)
                    after_step(dve, "dmat_done", C_.i)
                    nc.vector.tensor_tensor(k_state[C_.par][:], k_state[C_.par][:],
                                            dmat[C_.par][:, :, P - 1:P].to_broadcast([P, NC, P]), ALU.mult
                                            ).then_inc(S["k_state_done"], 1)
                if D_.live:
                    after_step(dve, "updates_mm", D_.i)
                    after_step(dve, "outputs_mm", D_.i - 1)
                    after_pair(dve, cum_loaded[D_.par], D_.pair)
                    updates = chunks(work(par, 5))
                    nc.vector.tensor_copy(states[:, 0], updates[:, 0]).then_inc(S["states_done"], 1)
                    for c in range(1, NC - 1):
                        after_step(dve, "states_done", D_.i, NC - 1, c)
                        last_token = c * P + P - 1
                        nc.vector.scalar_tensor_tensor(out=states[:, c], in0=states[:, c - 1],
                                                       scalar=cum_all[D_.par][:, last_token:last_token + 1],
                                                       in1=updates[:, c], op0=ALU.mult, op1=ALU.add
                                                       ).then_inc(S["states_done"], 1)
                if B_.live:
                    normalise()

            def ranks(u):
                dve.wait_ge(S["score_loaded"], 16 * u + 16)
                own = score_tok[:, bass.ds(u, 1)]
                after(dve, S["slot_done"], u)
                nc.vector.tensor_scalar(equal[:], score_all[:], own, None, ALU.is_gt, ALU.add, accum_out=greater[:]
                                        ).then_inc(S["greater_done"], 1)
                dve.wait_ge(S["greater_done"], u + 1)
                after(dve, S["ties_done"], u)
                nc.vector.tensor_scalar(equal[:], score_all[:], own, None, ALU.is_equal).then_inc(S["equal_done"], 1)
                dve.wait_ge(S["equal_done"], u + 1)
                nc.vector.scalar_tensor_tensor(out=equal[:], in0=token_row[:], scalar=token_col[:, bass.ds(u, 1)],
                                               in1=equal[:], op0=ALU.is_lt, op1=ALU.mult, accum_out=ties[:]
                                               ).then_inc(S["ties_done"], 1)
                dve.wait_ge(S["ties_done"], u + 1)
                after(dve, S["scattered"], 16 * u)
                nc.vector.scalar_tensor_tensor(out=slot[:], in0=greater[:], scalar=ties[:], in1=first_slot[:, bass.ds(u, 1)],
                                               op0=ALU.add, op1=ALU.add).then_inc(S["slot_done"], 1)
                nc.vector.tensor_scalar(token_id[:], token_col[:, bass.ds(u, 1)], 1.0, first_slot[:, bass.ds(u, 1)],
                                        ALU.mult, ALU.add).then_inc(S["id_done"], 1)

            def first_kept_rows():
                kept.statistics(dve, 0)
                kept.shifts(dve, 0)

            steps(dve, step, first_kept_rows)

        @block.tensor
        def _(pe):
            def work(par, pos):
                return ps_work[:, (par + pos) % 2]

            def turn(out, source):
                for c in range(NC):
                    last = nc.tensor.transpose(out[:, c * P:(c + 1) * P], source(c), ident[:])
                return last

            def step(u, par):
                A_, B_, C_, D_ = (At(u, par, lag) for lag in (0, LAG_B, LAG_C, LAG_D))

                def project(pos, half):
                    if half == 0 and pos == 0:
                        after_step(pe, "w_hi_done", A_.i)
                        after_step(pe, "w_lo_done", A_.i)
                        after_step(pe, "k_tap", A_.i - 1)
                    elif half == 0:
                        after_step(pe, "v_copied", A_.i - 1)
                    if pos == 0:
                        pe.wait_ge(xt_loaded[half], (A_.i // H) * 32 + 32)
                    out = ps_proj[:, (par + pos) % 2, half * BANK:(half + 1) * BANK]
                    cols = slice(half * BANK, (half + 1) * BANK)
                    for k in range(KC):
                        hi, lo = w_hi[par][:, pos, k], w_lo[par][:, pos, k]
                        nc.tensor.matmul(out, hi, xt_hi[:, k, cols], start=k == 0, stop=False)
                        nc.tensor.matmul(out, hi, xt_lo[:, k, cols], start=False, stop=False)
                        last = nc.tensor.matmul(out, lo, xt_hi[:, k, cols], start=False, stop=k == KC - 1)
                    if half == s.HALVES - 1:
                        last.then_inc(S["qk"[pos] + "_projected"], 1)
                    elif pos == 1:
                        last.then_inc(S["k_half"], 1)

                def project_v(half):
                    if half == 0:
                        after_step(pe, "wv_hi_done", A_.pair)
                        after_step(pe, "wv_lo_done", A_.pair)
                        after_step(pe, "q_tap", A_.i)
                    for j in range(half * VC // 2, (half + 1) * VC // 2):
                        c = par * VC + j
                        cols = slice(c * P, (c + 1) * P)
                        out = ps_proj[:, par, j * 2 * P:(j + 1) * 2 * P]
                        for k in range(KC):
                            nc.tensor.matmul(out, xt_hi[:, k, cols], wv_hi[:, k], start=k == 0, stop=False)
                            nc.tensor.matmul(out, xt_hi[:, k, cols], wv_lo[:, k], start=False, stop=False)
                            last = nc.tensor.matmul(out, xt_lo[:, k, cols], wv_hi[:, k], start=False, stop=k == KC - 1)
                    if half == 1:
                        last.then_inc(S["v_projected"], 1)

                if A_.live:
                    project(0, 0)
                if C_.live:
                    after_step(pe, "q_normed", C_.i)
                    after_step(pe, "states_done", D_.i - 1, NC - 1)
                    turn(work(par, 0), lambda c: tok[0][:, c]).then_inc(S["q_back"], 1)
                if A_.live:
                    project(0, 1)
                if C_.live:
                    after_step(pe, "k_normed", C_.i)
                    after_step(pe, "outputs_done", D_.i - 1)
                    turn(work(par, 1), lambda c: tok[1][:, c]).then_inc(S["k_back"], 1)
                if B_.live:
                    after_step(pe, "q_silu", B_.i)
                    after_step(pe, "q_ready", C_.i)
                    turn(work(par, 2), lambda c: act_cm[0][:, c * P:(c + 1) * P]).then_inc(S["q_turned"], 1)
                if A_.live:
                    project(1, 0)
                if B_.live:
                    after_step(pe, "k_silu", B_.i)
                    after_step(pe, "k_ready", C_.i)
                    turn(work(par, 3), lambda c: act_cm[1][:, c * P:(c + 1) * P]).then_inc(S["k_turned"], 1)
                if D_.live:
                    after_step(pe, "k_ready", D_.i)
                    after_step(pe, "q_ready", D_.i)
                    after_step(pe, "q_tok", B_.i)
                    if not B_.live:
                        after_step(pe, "q_ready", C_.i)
                    if not C_.live:
                        after_step(pe, "states_done", D_.i - 1, NC - 1)
                    for c in range(NC):
                        t = slice(c * P, (c + 1) * P)
                        last = nc.tensor.matmul(work(par, 4)[:, t], k_cm[D_.par][:, t], q_cm[D_.par][:, t],
                                                start=True, stop=True)
                    last.then_inc(S["scores_mm"], 1)
                if A_.live:
                    project(1, 1)
                if D_.live:
                    after_step(pe, "k_state_done", D_.i)
                    after_step(pe, "v_beta_done", D_.i)
                    if B_.live:
                        after_step(pe, "k_tok", B_.i)
                    elif C_.live:
                        after_step(pe, "k_ready", C_.i)
                    else:
                        after_step(pe, "outputs_done", D_.i - 1)
                    for c in range(NC - 1):
                        last = nc.tensor.matmul(work(par, 5)[:, c * P:(c + 1) * P], k_state[D_.par][:, c],
                                                v_beta[D_.par][:, c], start=True, stop=True)
                    last.then_inc(S["updates_mm"], 1)
                if A_.live:
                    project_v(0)
                if A_.live:
                    project_v(1)
                if D_.live:
                    after_step(pe, "states_done", D_.i, NC - 1)
                    after_step(pe, "q_cum_done", D_.i)
                    after_step(pe, "scores_done", D_.i)
                    for c in range(NC):
                        out = work(par, 6)[:, c * P:(c + 1) * P]
                        last = nc.tensor.matmul(out, scores[:, c], v_beta[D_.par][:, c], start=True, stop=c == 0)
                        if c:
                            last = nc.tensor.matmul(out, q_cum[:, c * P:(c + 1) * P], states[:, c - 1],
                                                    start=False, stop=True)
                    last.then_inc(S["outputs_mm"], 1)

            steps(pe, step)


def stage_kept_tokens(nc, s, a, scratch, keep, kept, gated):
    B, L, H, KC, ST, SEL, BLK, D = s.B, s.L, s.H, s.KC, s.ST, s.SEL, s.BLK, s.D
    tag = "gt_" if gated else "ff_"
    GROUP = 4
    GROUPS = BLK // GROUP
    WIDE = GROUP * P
    with ExitStack() as ctx:
        def sb(name, shape, dt=F32):
            return ctx.enter_context(nc.sbuf_tensor(tag + name, shape, dt))

        def two(name, shape, dt=F32):
            return [sb(f"{name}{i}", shape, dt) for i in range(2)]

        def sem(name):
            return ctx.enter_context(nc.semaphore(tag + name))

        ident = keep["ident"]
        up_hi = sb("up_hi", [P, GROUPS, KC, WIDE], F32R)
        up_lo = sb("up_lo", [P, GROUPS, KC, WIDE], F32R)
        down_hi = sb("down_hi", [P, GROUPS, GROUP, D], F32R)
        down_lo = sb("down_lo", [P, GROUPS, GROUP, D], F32R)
        staging, xn_rows, x_rows, ids = keep["staging"], keep["xn_rows"], kept.x_rows, kept.ids
        xt_hi = sb("xt_hi", [P, KC, SEL], F32R)
        xt_lo = sb("xt_lo", [P, KC, SEL], F32R)
        wide = two("wide", [P, SEL])
        wide_hi = two("wide_hi", [P, SEL], F32R)
        wide_lo = two("wide_lo", [P, SEL], F32R)
        o_ids = keep["o_ids"]
        if gated:
            o_rows = [keep["o_rows"], sb("o_rows1", [P, ST, WIDE])]
            gate = sb("gate", [P, SEL])
            ffn = staging.rearrange("p i k w -> p (i k w)").rearrange("p (t d) -> p t d", d=D)
        else:
            b1 = sb("b1", [P, BLK])
            b2 = sb("b2", [P, D])
            result = sb("result", [P, ST, D])
            ids_f = sb("ids_f", [P, B, ST])
            seq_shift = sb("seq_shift", [P, B, ST])
            o_ids_f = sb("o_ids_f", [P, B, ST])
        ps_up = ctx.enter_context(nc.psum_tensor(tag + "ps_up", [P, 2, SEL], F32))
        ps_turn = ctx.enter_context(nc.psum_tensor(tag + "ps_turn", [P, 2, SEL], F32))
        ps_out = ctx.enter_context(nc.psum_tensor(tag + "ps_out", [P, ST, D], F32))

        names = """w_hi_done w_lo_done x_turned x_hi_done x_lo_done
            up_mm wide_done wide_hi_done wide_lo_done down_mm"""
        names += """ x_loaded o_turned gate_done ffn_loaded silu_done times_done plus_done stored""" if gated else """
            consts_loaded xn_kept result_done seq_shift_set ids_f_done o_ids_f_done o_ids_done"""
        S = {n: sem(n) for n in names.split()}
        w_loaded = keep["piece_loaded"][gated]
        o_gathered = keep["o_gathered"]

        PIECES = 4 * GROUPS
        HALF_W, HALF_G = WIDE // 2, GROUP // 2
        by_rank = lambda name: scratch[name].rearrange("(b p t) d -> b p t d", p=P, t=ST)
        ffn_rows, kept_x, kept_xn = by_rank("ffn"), by_rank("kept_x"), by_rank("kept_xn")
        ffn_stored = keep["ffn_stored"]
        STAT_M, SHIFT_M, NORM_M = 5, 7, 9
        KEEP_M = 1
        PLUS_M, SILU_M = 2, 13

        def is_last(b):
            return isinstance(b, int) and b == B - 1

        def piece(n):
            g, part = divmod(n, 4)
            half = part % 2
            staged = weight_piece(s, a, keep, gated, n)[1]
            if part < 2:
                cols = slice(half * HALF_W, (half + 1) * HALF_W)
                return staged, up_hi[:, g, :, cols], up_lo[:, g, :, cols]
            blocks = slice(half * HALF_G, (half + 1) * HALF_G)
            return staged, down_hi[:, g, blocks], down_lo[:, g, blocks]

        block = ctx.enter_context(nc.Block())

        @block.sync
        def _(sp):
            with nc.allow_non_contiguous_dma("per-channel constants"):
                if not gated:
                    sp.dma_start(b1[:], a["b1"].rearrange("(m p) -> p m", p=P)).then_inc(S["consts_loaded"], 16)
                for n in range(2, PIECES):
                    sp.wait_ge(S["w_lo_done"], n - 1)
                    source, staged = weight_piece(s, a, keep, gated, n)
                    sp.dma_start(staged, source).then_inc(w_loaded[n % 2], 16)
                    if n == 3 and not gated:
                        sp.dma_start(b2[:], a["b2"].partition_broadcast(P)).then_inc(S["consts_loaded"], 16)

                if not gated:
                    for n in range(2):
                        sp.wait_ge(S["w_lo_done"], PIECES)
                        source, staged = weight_piece(s, a, keep, True, n)
                        sp.dma_start(staged, source).then_inc(keep["piece_loaded"][True][n], 16)
                    sp.dma_start(a["out"].rearrange("b l d -> (b l) d"),
                                 a["x"].rearrange("b l d -> (b l) d")).then_inc(keep["out_copied"], 16)

                def sequence(b):
                    if not gated:
                        sp.wait_ge(S["result_done"], ST * b + ST)
                        sp.dma_start(row(ffn_rows, b), result[:]).then_inc(ffn_stored, 16)
                        return
                    if not (isinstance(b, int) and b == 0):
                        sp.wait_ge(S["x_turned"], KC * b)
                        sp.dma_start(xn_rows[:], row(kept_xn, b)).then_inc(keep["xn_loaded"], 16)
                    sp.wait_ge(S["w_lo_done"], PIECES)
                    if isinstance(b, int) and b == 0:
                        sp.wait_ge(ffn_stored, 16 * B)
                    after(sp, S["plus_done"], b)
                    sp.dma_start(ffn, row(ffn_rows, b)).then_inc(S["ffn_loaded"], 16)
                    after(sp, S["stored"], 16 * ST * b)
                    sp.dma_start(x_rows[:], row(kept_x, b)).then_inc(S["x_loaded"], 16)

                sequence(0)
                with sp.Fori(1, B - 1) as b:
                    sequence(b)
                if not gated:
                    sp.wait_ge(S["x_turned"], KC * B)
                    sp.wait_ge(S["xn_kept"], 16 * B)
                    sp.dma_start(xn_rows[:], kept_xn[0]).then_inc(keep["xn_loaded"], 16)
                sequence(B - 1)
            if not gated:
                sp.wait_ge(kept.S["x_kept"], 16 * B)

        @block.gpsimd
        def _(pool):
            def gather(out, source, index):
                return nc.gpsimd.indirect_dma_start(out=out, out_offset=None, in_=source,
                                                    in_offset=bass.IndirectOffsetOnAxis(ap=index, axis=0))

            def gather_o(b, g):
                if b or g > 1:
                    pool.wait_ge(S["o_turned"], BLK * b + GROUP * (g - 1))
                into = o_rows[g % 2] if gated else keep["o_rows"]
                for t in range(ST):
                    gather(into[:, t], scratch["o"].rearrange("l (g w) -> (l g) w", w=WIDE),
                           o_ids[:, g, b, t:t + 1]).then_inc(o_gathered[g % 2], 16)

            def scatter(b):
                if b == 0:
                    pool.wait_ge(keep["out_copied"], 16)
                for t in range(ST):
                    pool.wait_ge(S["plus_done"], b + 1 + (t if b == B - 1 else 0))
                    nc.gpsimd.indirect_dma_start(
                        out=a["out"].rearrange("b l d -> (b l) d"),
                        out_offset=bass.IndirectOffsetOnAxis(ap=ids[:, b, t:t + 1], axis=0),
                        in_=x_rows[:, t], in_offset=None).then_inc(S["stored"], 16)

            if gated:
                pool.wait_ge(ffn_stored, 16 * B)
                for b in range(B):
                    if b:
                        gather_o(b, 0)
                    gather_o(b, 1)
                    if b:
                        scatter(b - 1)
                    gather_o(b, 2)
                    gather_o(b, 3)
                scatter(B - 1)
                pool.wait_ge(S["stored"], 16 * ST * B)
            else:
                nc.gpsimd.iota(seq_shift[:], pattern=[[-(L * B - 1) * GROUPS, B], [0, ST]], base=0,
                               channel_multiplier=0, allow_small_or_imprecise_dtypes=True
                               ).then_inc(S["seq_shift_set"], 1)
                for b in range(1, B):
                    kept.gather(pool, b)
                    kept.rstd_of(pool, b)
                for stored in keep["o_stored"]:
                    pool.wait_ge(stored, 16 * (s.N // 2))
                pool.wait_ge(S["o_ids_done"], 1)
                gather_o(0, 0)

        @block.scalar
        def _(act):
            def split_piece(n):
                staged, hi, _ = piece(n)
                act.wait_ge(w_loaded[n % 2], 16 * (n // 2 + 1))
                nc.scalar.activation(hi, staged, ACT.Copy).then_inc(S["w_hi_done"], 1)

            def split_x(b):
                after(act, S["up_mm"], BLK * b)
                for k in range(KC):
                    act.wait_ge(S["x_turned"], KC * b + k + 1)
                    nc.scalar.activation(xt_hi[:, k], ps_turn[:, k % 2], ACT.Copy).then_inc(S["x_hi_done"], 1)

            def normalise(b):
                act.wait_ge(kept.S["x_loaded"], 16 * (ST * b + ST))
                act.dma_start(row(kept_x, b), x_rows[:]).then_inc(kept.S["x_kept"], 16)
                after(act, S["x_turned"], KC * b)
                after(act, S["xn_kept"], 16 * b)
                kept.normalise(act, b)
                keep_normalised(b)

            def keep_normalised(b):
                act.wait_ge(kept.S["xn_done"], b + 1)
                act.dma_start(row(kept_xn, b), xn_rows[:]).then_inc(S["xn_kept"], 16)

            def sequence(b, pieces=False):
                split_x(b)
                if pieces:
                    split_piece(2)
                    split_piece(3)
                    if not gated:
                        for stored in keep["o_stored"]:
                            act.wait_ge(stored, 16 * (s.N // 2))
                        act.wait_ge(S["consts_loaded"], 32)
                for m in range(BLK):
                    act.wait_ge(S["up_mm"], BLK * b + m + 1)
                    if gated:
                        after(act, S["wide_done"], BLK * b + m)
                        nc.scalar.activation(gate[:], ps_up[:, m % 2], ACT.Silu).then_inc(S["gate_done"], 1)
                    else:
                        after(act, S["wide_lo_done"], BLK * b + m - 1)
                        nc.scalar.activation(wide[m % 2][:], ps_up[:, m % 2], ACT.Gelu_apprx_tanh,
                                             bias=b1[:, m:m + 1]).then_inc(S["wide_done"], 1)
                    act.wait_ge(S["wide_done"], BLK * b + m + 1)
                    after(act, S["down_mm"], BLK * b + m - 1)
                    nc.scalar.activation(wide_hi[m % 2][:], wide[m % 2][:], ACT.Copy).then_inc(S["wide_hi_done"], 1)
                    if pieces and m + 4 < PIECES:
                        split_piece(m + 4)
                    if pieces and not gated and m == KEEP_M:
                        act.dma_start(kept_x[0], x_rows[:]).then_inc(kept.S["x_kept"], 16)
                        keep_normalised(0)
                    if not gated and m == NORM_M and not is_last(b):
                        normalise(b + 1)
                    if gated and m == SILU_M:
                        act.wait_ge(S["ffn_loaded"], 16 * b + 16)
                        nc.scalar.activation(ffn, ffn, ACT.Silu).then_inc(S["silu_done"], 1)

            split_piece(0)
            split_piece(1)
            sequence(0, True)
            with act.Fori(1, B - 1) as b:
                sequence(b)
            sequence(B - 1)

        @block.vector
        def _(dve):
            def split_piece(n):
                staged, hi, lo = piece(n)
                dve.wait_ge(S["w_hi_done"], n + 1)
                nc.vector.tensor_tensor(lo, staged, hi.bitcast(F32), ALU.subtract).then_inc(S["w_lo_done"], 1)

            def o_indices():
                dve.wait_ge(kept.S["ids_loaded"], 16)
                nc.vector.tensor_copy(ids_f[:], ids[:]).then_inc(S["ids_f_done"], 1)
                dve.wait_ge(S["ids_f_done"], 1)
                dve.wait_ge(S["seq_shift_set"], 1)
                nc.vector.scalar_tensor_tensor(out=o_ids_f[:], in0=ids_f[:], scalar=float(B * GROUPS),
                                               in1=seq_shift[:], op0=ALU.mult, op1=ALU.add
                                               ).then_inc(S["o_ids_f_done"], 1)
                dve.wait_ge(S["o_ids_f_done"], 1)
                for g in range(GROUPS):
                    last = nc.vector.tensor_scalar(o_ids[:, g], o_ids_f[:], float(g), None, ALU.add)
                last.then_inc(S["o_ids_done"], 1)

            def finish(b):
                dve.wait_ge(S["down_mm"], BLK * b + BLK)
                if gated:
                    dve.wait_ge(S["silu_done"], b + 1)
                    for t in range(ST):
                        nc.vector.tensor_tensor(ffn[:, t], ps_out[:, t], ffn[:, t], ALU.mult
                                                ).then_inc(S["times_done"], 1)
                else:
                    after(dve, ffn_stored, 16 * b)
                    for t in range(ST):
                        nc.vector.tensor_tensor(result[:, t], ps_out[:, t], b2[:], ALU.add
                                                ).then_inc(S["result_done"], 1)

            def plus(b):
                dve.wait_ge(S["times_done"], ST * b + ST)
                dve.wait_ge(S["x_loaded"], 16 * b + 16)
                nc.vector.tensor_tensor(x_rows[:], x_rows[:], ffn, ALU.add).then_inc(S["plus_done"], 1)

            def sequence(b, pieces=False):
                for k in range(KC):
                    dve.wait_ge(S["x_hi_done"], KC * b + k + 1)
                    nc.vector.tensor_tensor(xt_lo[:, k], ps_turn[:, k % 2], xt_hi[:, k].bitcast(F32), ALU.subtract
                                            ).then_inc(S["x_lo_done"], 1)
                if pieces:
                    split_piece(2)
                    split_piece(3)
                    if not gated:
                        dve.wait_ge(S["consts_loaded"], 32)
                else:
                    finish(b - 1)
                for m in range(BLK):
                    if gated:
                        dve.wait_ge(S["gate_done"], BLK * b + m + 1)
                        dve.wait_ge(S["o_turned"], BLK * b + m + 1)
                        after(dve, S["wide_hi_done"], BLK * b + m - 1)
                        after(dve, S["wide_lo_done"], BLK * b + m - 1)
                        nc.vector.tensor_tensor(wide[m % 2][:], ps_turn[:, m % 2], gate[:], ALU.mult
                                                ).then_inc(S["wide_done"], 1)
                    dve.wait_ge(S["wide_hi_done"], BLK * b + m + 1)
                    after(dve, S["down_mm"], BLK * b + m - 1)
                    nc.vector.tensor_tensor(wide_lo[m % 2][:], wide[m % 2][:], wide_hi[m % 2][:].bitcast(F32),
                                            ALU.subtract).then_inc(S["wide_lo_done"], 1)
                    if pieces and m + 4 < PIECES:
                        split_piece(m + 4)
                    if gated and m == PLUS_M and not pieces:
                        plus(b - 1)
                    if not gated and not is_last(b):
                        if m == STAT_M:
                            kept.statistics(dve, b + 1)
                        if m == SHIFT_M:
                            kept.shifts(dve, b + 1)

            split_piece(0)
            split_piece(1)
            sequence(0, True)
            if not gated:
                o_indices()
            with dve.Fori(1, B - 1) as b:
                sequence(b)
            sequence(B - 1)
            finish(B - 1)
            if gated:
                dve.wait_ge(S["x_loaded"], 16 * B)
                for t in range(ST):
                    dve.wait_ge(S["times_done"], ST * (B - 1) + t + 1)
                    nc.vector.tensor_tensor(x_rows[:, t], x_rows[:, t], ffn[:, t], ALU.add
                                            ).then_inc(S["plus_done"], 1)

        @block.tensor
        def _(pe):
            def turn_x(b, k):
                if gated and k < 2:
                    after(pe, S["wide_done"], BLK * b + k - 1)
                else:
                    after(pe, S["x_lo_done"], KC * b + k - 1)
                for t in range(ST):
                    last = nc.tensor.transpose(ps_turn[:, k % 2, t * P:(t + 1) * P],
                                               xn_rows[:, t, k * P:(k + 1) * P], ident[:])
                last.then_inc(S["x_turned"], 1)

            def up(b, m):
                g, j = divmod(m, GROUP)
                if isinstance(b, int) and b == 0 and j % HALF_G == 0:
                    pe.wait_ge(S["w_lo_done"], 4 * g + j // HALF_G + 1)
                after(pe, S["gate_done" if gated else "wide_done"], BLK * b + m - 1)
                for k in range(KC):
                    if m == 0:
                        pe.wait_ge(S["x_hi_done"], KC * b + k + 1)
                        pe.wait_ge(S["x_lo_done"], KC * b + k + 1)
                    hi, lo = (w[:, g, k, j * P:(j + 1) * P] for w in (up_hi, up_lo))
                    out = ps_up[:, m % 2]
                    nc.tensor.matmul(out, hi, xt_hi[:, k], start=k == 0, stop=False)
                    nc.tensor.matmul(out, hi, xt_lo[:, k], start=False, stop=False)
                    last = nc.tensor.matmul(out, lo, xt_hi[:, k], start=False, stop=k == KC - 1)
                last.then_inc(S["up_mm"], 1)
                if gated:
                    if j == 0:
                        pe.wait_ge(o_gathered[g % 2], 16 * ST * ((GROUPS // 2) * b + g // 2 + 1))
                    if m < 2:
                        pe.wait_ge(S["x_lo_done"], KC * b + KC)
                    else:
                        pe.wait_ge(S["wide_done"], BLK * b + m - 1)
                    for t in range(ST):
                        last = nc.tensor.transpose(ps_turn[:, m % 2, t * P:(t + 1) * P],
                                                   o_rows[g % 2][:, t, j * P:(j + 1) * P], ident[:])
                    last.then_inc(S["o_turned"], 1)

            def down(b, m):
                g, j = divmod(m, GROUP)
                if isinstance(b, int) and b == 0 and j % HALF_G == 0:
                    pe.wait_ge(S["w_lo_done"], 4 * g + 2 + j // HALF_G + 1)
                pe.wait_ge(S["wide_hi_done"], BLK * b + m + 1)
                pe.wait_ge(S["wide_lo_done"], BLK * b + m + 1)
                for t in range(ST):
                    if m == 0:
                        after(pe, S["times_done" if gated else "result_done"], ST * (b - 1) + t + 1)
                    cols = slice(t * P, (t + 1) * P)
                    hi, lo = wide_hi[m % 2][:, cols], wide_lo[m % 2][:, cols]
                    nc.tensor.matmul(ps_out[:, t], hi, down_hi[:, g, j], start=m == 0, stop=False)
                    nc.tensor.matmul(ps_out[:, t], hi, down_lo[:, g, j], start=False, stop=False)
                    last = nc.tensor.matmul(ps_out[:, t], lo, down_hi[:, g, j], start=False, stop=m == BLK - 1)
                last.then_inc(S["down_mm"], 1)

            def sequence(b):
                if gated:
                    pe.wait_ge(keep["xn_loaded"], 16 * b + 16)
                else:
                    pe.wait_ge(kept.S["xn_done"], b + 1)
                stand(pe, keep["carrier_pe"])
                turn_x(b, 0)
                turn_x(b, 1)
                if not (isinstance(b, int) and b == 0):
                    down(b - 1, BLK - 1)
                for k in range(2, KC):
                    turn_x(b, k)
                for m in range(BLK):
                    up(b, m)
                    if m:
                        down(b, m - 1)

            peeled(pe, 1, B, sequence)
            down(B - 1, BLK - 1)


ARGUMENTS = {
    "x": "L0_attn_hidden_states", "wq": "L0_attn_Wq", "wk": "L0_attn_Wk", "wv": "L0_attn_Wv",
    "wb": "L0_attn_Wb", "bb": "L0_attn_bb", "wg": "L0_attn_Wg", "wo": "L0_attn_Wo",
    "qconv_w": "L0_attn_qconv_w", "qconv_b": "L0_attn_qconv_b",
    "kconv_w": "L0_attn_kconv_w", "kconv_b": "L0_attn_kconv_b",
    "qn_w": "L0_attn_qn_w", "qn_b": "L0_attn_qn_b", "kn_w": "L0_attn_kn_w", "kn_b": "L0_attn_kn_b",
    "w_r": "L0_ffn_w_r", "b_r": "L0_ffn_b_r", "w1": "L0_ffn_w1", "b1": "L0_ffn_b1",
    "w2": "L0_ffn_w2", "b2": "L0_ffn_b2",
}


def build(nc, a):
    s = Shapes(a["x"], a["wq"], a["wb"], a["qn_w"], a["w1"])

    def dram(name, shape, dt=F32):
        return nc.dram_tensor("scratch_" + name, shape, dt).ap()

    scratch = {
        "xt_hi": dram("xt_hi", [s.B, P, s.KC, s.L]),
        "xt_lo": dram("xt_lo", [s.B, P, s.KC, s.L]),
        "score": dram("score", [s.B, s.L]),
        "decay": dram("decay", [s.N, s.L]),
        "cum": dram("cum", [s.N, s.L]),
        "o": dram("o", [s.L, s.B * s.HD]),
        "ids": dram("ids", [s.B * s.L, 1], I32),
        "kept_x": dram("kept_x", [s.B * s.SEL, s.D]),
        "kept_xn": dram("kept_xn", [s.B * s.SEL, s.D]),
        "ffn": dram("ffn", [s.B * s.SEL, s.D]),
    }
    with ExitStack() as ctx:
        keep = {
            "ident": ctx.enter_context(nc.sbuf_tensor("ident", [P, P], F32)),
            "carrier_dve": ctx.enter_context(nc.semaphore("carrier_dve")),
            "carrier_pe": ctx.enter_context(nc.semaphore("carrier_pe")),
            "carrier_sp": ctx.enter_context(nc.semaphore("carrier_sp")),
            "carrier_pool": ctx.enter_context(nc.semaphore("carrier_pool")),
            "w_loaded": [ctx.enter_context(nc.semaphore(f"w_loaded{i}")) for i in range(2)],
            "wv_loaded": ctx.enter_context(nc.semaphore("wv_loaded")),
            "w_hi_done": ctx.enter_context(nc.semaphore("w_hi_done")),
            "w_lo_done": ctx.enter_context(nc.semaphore("w_lo_done")),
            "wv_hi_done": ctx.enter_context(nc.semaphore("wv_hi_done")),
            "wv_lo_done": ctx.enter_context(nc.semaphore("wv_lo_done")),
            "piece_loaded": [[ctx.enter_context(nc.semaphore(f"piece_loaded{stage}_{i}")) for i in range(2)]
                             for stage in (3, 4)],
            "o_stored": [ctx.enter_context(nc.semaphore(f"o_stored{i}")) for i in range(2)],
            "ffn_stored": ctx.enter_context(nc.semaphore("ffn_stored")),
            "xn_loaded": ctx.enter_context(nc.semaphore("xn_loaded")),
            "o_gathered": [ctx.enter_context(nc.semaphore(f"o_gathered{i}")) for i in range(2)],
            "out_copied": ctx.enter_context(nc.semaphore("out_copied")),
        }
        kept = KeptRows(nc, s, a, ctx, keep)
        raw_width = s.L + a["qconv_w"].shape[1] - 1
        keep["raw"] = ctx.enter_context(nc.sbuf_tensor("raw", [P, 2 * raw_width], F32))
        keep["staging"] = keep["raw"][:, 0:2 * s.L].rearrange("p (i k w) -> p i k w", i=2, k=s.KC)
        keep["xn_rows"] = ctx.enter_context(nc.sbuf_tensor("xn_rows", [P, s.ST, s.D], F32))
        with ExitStack() as first_stages:
            for part in ("xt_hi", "xt_lo"):
                keep[part] = first_stages.enter_context(nc.sbuf_tensor(part, [P, s.KC, s.L], F32R))
            keep["beta_steps"] = first_stages.enter_context(nc.sbuf_tensor("beta_steps", [P, s.NC, s.N], F32))
            for part, dt in (("w_raw", F32), ("w_hi", F32R), ("w_lo", F32R)):
                keep[part] = [first_stages.enter_context(nc.sbuf_tensor(f"{part}{i}", [P, 2, s.KC, P], dt))
                              for i in range(2)]
                keep["wv" + part[1:]] = first_stages.enter_context(nc.sbuf_tensor("wv" + part[1:], [P, s.KC, 2 * P], dt))
            stage_tokens(nc, s, a, scratch, keep)
            stage_recurrence(nc, s, a, scratch, keep, kept)
        keep["o_rows"] = ctx.enter_context(nc.sbuf_tensor("o_rows", [P, s.ST, s.D], F32))
        keep["o_ids"] = ctx.enter_context(nc.sbuf_tensor("o_ids", [P, s.HD // s.D, s.B, s.ST], I32))
        stage_kept_tokens(nc, s, a, scratch, keep, kept, gated=False)
        stage_kept_tokens(nc, s, a, scratch, keep, kept, gated=True)


def kernel(**inputs):
    import concourse.bacc as bacc
    from concourse.bass_utils import run_bass_kernel_spmd

    nc = bacc.Bacc("TRN2", target_bir_lowering=False, num_devices=1)
    arrays, a = {}, {}
    for name, given in ARGUMENTS.items():
        array = np.ascontiguousarray(inputs[given])
        if array.ndim == 0:
            array = array.reshape(1)
        arrays["in_" + name] = array
        a[name] = nc.dram_tensor("in_" + name, array.shape, mybir.dt.from_np(array.dtype), kind="ExternalInput").ap()
    x = inputs["L0_attn_hidden_states"]
    a["out"] = nc.dram_tensor("out", x.shape, F32, kind="ExternalOutput").ap()
    build(nc, a)
    result = run_bass_kernel_spmd(nc, [arrays], core_ids=[0])
    return result.results[0]["out"]
```
